# Optimizing a Trainium2 kernel written in Bass

```python
import numpy as np
import jax
import jax.numpy as jnp

def _softmax(x, axis=-1):
    return jax.nn.softmax(x, axis=axis)

def _gelu(x):
    return jax.nn.gelu(x, approximate=True)

def _silu(x):
    return jax.nn.silu(x)

def _sigmoid(x):
    return jax.nn.sigmoid(x)

def _layernorm(x, axis=-1, eps=1e-05):
    m = jnp.mean(x, axis=axis, keepdims=True)
    v = jnp.var(x, axis=axis, keepdims=True)
    return (x - m) / jnp.sqrt(v + eps)

def _scatter_add(tgt, idx, src, axis=0):
    return tgt.at[idx].add(src)

def _segment_sum(src, seg, n):
    return jax.ops.segment_sum(src, seg, n)
kernel_name = 'mk_lm_tower_d2_tok_ids512_r4_0d5804'

def setup_inputs(seed: int=0):
    np.random.seed(seed)
    _w = jnp.asarray

    def _rec_inputs():
        import jax
        import jax.numpy as jnp
        _rk = jax.random.key(seed)
        x = jax.random.randint(jax.random.fold_in(_rk, 1), (32, 256), 0, 2500, jnp.int32)
        return x
    x = _rec_inputs()

    def _L0_tok_setup():
        import jax, jax.numpy as jnp
        import numpy as np
        EMBED_DIM = 128
        MAX_POSITION = 2500
        BASE = 10000.0
        BATCH, SEQ = (8, 2048)

        def _build_cache():
            freqs = 1.0 / BASE ** (jnp.arange(0, EMBED_DIM, 2, dtype=jnp.float32) / EMBED_DIM)
            positions = jnp.arange(MAX_POSITION, dtype=jnp.float32)
            angles = jnp.outer(positions, freqs)
            return jnp.stack([jnp.sin(angles), jnp.cos(angles)], axis=-1)
        key = jax.random.key(seed)
        positions = jax.random.randint(key, (BATCH, SEQ), 0, MAX_POSITION, dtype=jnp.int64)
        sin_cos_cache = _build_cache()
        return {'positions': positions, 'sin_cos_cache': sin_cos_cache}
    _L0_tok_all = _L0_tok_setup()
    _L0_tok_in = {k: v for k, v in _L0_tok_all.items() if k in ('sin_cos_cache',)}
    del _L0_tok_all

    def _L0_attn_setup():
        import jax, jax.numpy as jnp
        import numpy as np
        B, N, D = (2, 2048, 128)
        L, H, DH, M = (2, 8, 64, 64)
        EPS_K = 0.0001

        def _layernorm(x, s, b):
            m = x.mean(-1, keepdims=True)
            v = x.var(-1, keepdims=True)
            return (x - m) / jnp.sqrt(v + 1e-05) * s + b

        def _softmax_kernel(x, proj, is_query):
            dh = x.shape[-1]
            data_norm = dh ** (-0.25)
            ratio = proj.shape[0] ** (-0.5)
            dd = jnp.einsum('bhnd,md->bhnm', x * data_norm, proj)
            diag = 0.5 * jnp.sum(x * x, axis=-1) * data_norm ** 2
            if is_query:
                stab = jnp.max(dd, axis=-1, keepdims=True)
            else:
                stab = jnp.max(dd, axis=(-1, -2), keepdims=True)
            return ratio * (jnp.exp(dd - diag[..., None] - stab) + EPS_K)

        def _linear_attention(qp, kp, v):
            k_sum = kp.sum(axis=2)
            d_inv = 1.0 / jnp.einsum('bhnm,bhm->bhn', qp, k_sum)
            ctx = jnp.einsum('bhnm,bhnd->bhmd', kp, v)
            return jnp.einsum('bhnm,bhmd,bhn->bhnd', qp, ctx, d_inv)

        def _performer_forward(x, ln1_s, ln1_b, Wq, bq, Wk, bk, Wv, bv, Wo, bo, proj, ln2_s, ln2_b, W1, b1, W2, b2):
            depth = Wq.shape[0]
            for l in range(depth):
                h = _layernorm(x, ln1_s[l], ln1_b[l])
                b, n, d = h.shape

                def heads(t):
                    return t.reshape(b, n, H, DH).transpose(0, 2, 1, 3)
                q = heads(h @ Wq[l] + bq[l])
                k = heads(h @ Wk[l] + bk[l])
                v = heads(h @ Wv[l] + bv[l])
                qp = _softmax_kernel(q, proj[l], True)
                kp = _softmax_kernel(k, proj[l], False)
                attn = _linear_attention(qp, kp, v)
                attn = attn.transpose(0, 2, 1, 3).reshape(b, n, H * DH)
                x = x + (attn @ Wo[l] + bo[l])
                h2 = _layernorm(x, ln2_s[l], ln2_b[l])
                ff = jax.nn.gelu(h2 @ W1[l] + b1[l]) @ W2[l] + b2[l]
                x = x + ff
            return x
        key = jax.random.key(seed)
        ks = jax.random.split(key, 16)
        s = 0.02
        inp = {'x': jax.random.normal(ks[0], (B, N, D), jnp.float32), 'ln1_s': jnp.ones((L, D), jnp.float32), 'ln1_b': jnp.zeros((L, D), jnp.float32), 'Wq': s * jax.random.normal(ks[1], (L, D, H * DH), jnp.float32), 'bq': jnp.zeros((L, H * DH), jnp.float32), 'Wk': s * jax.random.normal(ks[2], (L, D, H * DH), jnp.float32), 'bk': jnp.zeros((L, H * DH), jnp.float32), 'Wv': s * jax.random.normal(ks[3], (L, D, H * DH), jnp.float32), 'bv': jnp.zeros((L, H * DH), jnp.float32), 'Wo': s * jax.random.normal(ks[4], (L, H * DH, D), jnp.float32), 'bo': jnp.zeros((L, D), jnp.float32), 'proj': jax.random.normal(ks[5], (L, M, DH), jnp.float32), 'ln2_s': jnp.ones((L, D), jnp.float32), 'ln2_b': jnp.zeros((L, D), jnp.float32), 'W1': s * jax.random.normal(ks[6], (L, D, 4 * D), jnp.float32), 'b1': jnp.zeros((L, 4 * D), jnp.float32), 'W2': s * jax.random.normal(ks[7], (L, 4 * D, D), jnp.float32), 'b2': jnp.zeros((L, D), jnp.float32)}
        return inp
    _L0_attn_all = _L0_attn_setup()
    _L0_attn_in = {k: v for k, v in _L0_attn_all.items() if k in ('ln1_s', 'ln1_b', 'Wq', 'bq', 'Wk', 'bk', 'Wv', 'bv', 'Wo', 'bo', 'proj', 'ln2_s', 'ln2_b', 'W1', 'b1', 'W2', 'b2')}
    del _L0_attn_all

    def _L0_ffn_setup():
        import jax, jax.numpy as jnp
        import numpy as np
        B, S, D, F, E = (4, 512, 128, 512, 8)
        key = jax.random.key(seed)
        k = jax.random.split(key, 5)
        x = jax.random.normal(k[0], (B, S, D), dtype=jnp.float32)
        Ws = jax.random.normal(k[1], (D, E), dtype=jnp.float32) * 0.02
        bs = jnp.zeros((E,), dtype=jnp.float32)
        W1 = jax.random.normal(k[2], (E, D, F), dtype=jnp.float32) * 0.02
        b1 = jnp.zeros((E, F), dtype=jnp.float32)
        W2 = jax.random.normal(k[3], (E, F, D), dtype=jnp.float32) * 0.02
        b2 = jnp.zeros((E, D), dtype=jnp.float32)
        return {'x': x, 'Ws': Ws, 'bs': bs, 'W1': W1, 'b1': b1, 'W2': W2, 'b2': b2}
    _L0_ffn_all = _L0_ffn_setup()
    _L0_ffn_in = {k: v for k, v in _L0_ffn_all.items() if k in ('Ws', 'bs', 'W1', 'b1', 'W2', 'b2')}
    del _L0_ffn_all

    def _L1_attn_setup():
        import jax, jax.numpy as jnp
        import numpy as np
        D_MODEL = 128
        D_STATE = 64
        D_CONV = 4
        HEADDIM = 64
        D_INNER = 2 * D_MODEL
        NHEADS = D_INNER // HEADDIM
        CONV_DIM = D_INNER + 2 * D_STATE
        D_IN_PROJ = 2 * D_INNER + 2 * D_STATE + NHEADS
        BATCH, SEQ = (4, 256)
        EPS = 1e-05

        def rmsnorm(x, w):
            return x * jax.lax.rsqrt(jnp.mean(x * x, axis=-1, keepdims=True) + EPS) * w

        def mamba2(u, in_w, conv_w, conv_b, dt_bias, A_log, D, gnorm_w, out_w):
            b, l, _ = u.shape
            zxbcdt = u @ in_w.T
            z = zxbcdt[..., :D_INNER]
            xBC = zxbcdt[..., D_INNER:D_INNER + CONV_DIM]
            dt = jax.nn.softplus(zxbcdt[..., -NHEADS:] + dt_bias)
            pad = jnp.pad(xBC, ((0, 0), (D_CONV - 1, 0), (0, 0)))
            acc = conv_b
            for k in range(D_CONV):
                acc = acc + pad[:, k:k + l, :] * conv_w[:, k]
            xBC = jax.nn.silu(acc)
            x = xBC[..., :D_INNER].reshape(b, l, NHEADS, HEADDIM)
            Bm = xBC[..., D_INNER:D_INNER + D_STATE]
            Cm = xBC[..., D_INNER + D_STATE:]
            A = -jnp.exp(A_log)
            decay = jnp.exp(dt * A)
            dtx = dt[..., None] * x

            def step(h, inp):
                dec, dx, Bt, Ct = inp
                h = h * dec[:, :, None, None] + dx[..., None] * Bt[:, None, None, :]
                y = jnp.einsum('bhpn,bn->bhp', h, Ct)
                return (h, y)
            h0 = jnp.zeros((b, NHEADS, HEADDIM, D_STATE), u.dtype)
            _, ys = jax.lax.scan(step, h0, (decay.transpose(1, 0, 2), dtx.transpose(1, 0, 2, 3), Bm.transpose(1, 0, 2), Cm.transpose(1, 0, 2)))
            y = ys.transpose(1, 0, 2, 3) + x * D[None, None, :, None]
            y = y.reshape(b, l, D_INNER)
            y = rmsnorm(y * jax.nn.silu(z), gnorm_w)
            return y @ out_w.T
        key = jax.random.key(seed)
        ks = iter(jax.random.split(key, 32))

        def rn(shape, scale=0.02):
            return jax.random.normal(next(ks), shape, dtype=jnp.float32) * scale
        inp = {'x': jax.random.normal(next(ks), (BATCH, SEQ, D_MODEL), dtype=jnp.float32), 'norm_w': jnp.ones((D_MODEL,), jnp.float32)}
        for p in ('f', 'b'):
            inp[p + '_in_w'] = rn((D_IN_PROJ, D_MODEL))
            inp[p + '_conv_w'] = rn((CONV_DIM, D_CONV), 0.1)
            inp[p + '_conv_b'] = jnp.zeros((CONV_DIM,), jnp.float32)
            inp[p + '_dt_bias'] = rn((NHEADS,), 0.5)
            inp[p + '_A_log'] = jnp.log(jnp.arange(1, NHEADS + 1, dtype=jnp.float32))
            inp[p + '_D'] = jnp.ones((NHEADS,), jnp.float32)
            inp[p + '_gnorm_w'] = jnp.ones((D_INNER,), jnp.float32)
            inp[p + '_out_w'] = rn((D_MODEL, D_INNER))
        inp['proj_w'] = rn((D_MODEL, 2 * D_MODEL))
        return inp
    _L1_attn_all = _L1_attn_setup()
    _L1_attn_in = {k: v for k, v in _L1_attn_all.items() if k in ('norm_w', 'f_in_w', 'f_conv_w', 'f_conv_b', 'f_dt_bias', 'f_A_log', 'f_D', 'f_gnorm_w', 'f_out_w', 'b_in_w', 'b_conv_w', 'b_conv_b', 'b_dt_bias', 'b_A_log', 'b_D', 'b_gnorm_w', 'b_out_w', 'proj_w')}
    del _L1_attn_all

    def _L1_ffn_setup():
        import jax, jax.numpy as jnp
        import numpy as np
        B, S, D, H, E = (4, 512, 128, 8, 8)
        FF = 4 * D
        HD = D // H
        EPS = 1e-05

        def _layernorm(x, g, b):
            mu = jnp.mean(x, axis=-1, keepdims=True)
            var = jnp.mean((x - mu) ** 2, axis=-1, keepdims=True)
            return (x - mu) * jax.lax.rsqrt(var + EPS) * g + b
        key = jax.random.key(seed)
        ks = jax.random.split(key, 16)
        s = 0.02
        return {'x': jax.random.normal(ks[0], (B, S, D), dtype=jnp.float32), 'ln1_g': jnp.ones((D,), jnp.float32), 'ln1_b': jnp.zeros((D,), jnp.float32), 'Wq': jax.random.normal(ks[1], (D, D), jnp.float32) * s, 'bq': jnp.zeros((D,), jnp.float32), 'Wk': jax.random.normal(ks[2], (D, D), jnp.float32) * s, 'bk': jnp.zeros((D,), jnp.float32), 'Wv': jax.random.normal(ks[3], (D, D), jnp.float32) * s, 'bv': jnp.zeros((D,), jnp.float32), 'Wo': jax.random.normal(ks[4], (D, D), jnp.float32) * s, 'bo': jnp.zeros((D,), jnp.float32), 'gate_W': jax.random.normal(ks[5], (D, E), jnp.float32) * s, 'gate_b': jnp.zeros((E,), jnp.float32), 'W1': jax.random.normal(ks[6], (E, D, FF), jnp.float32) * s, 'b1': jnp.zeros((E, FF), jnp.float32), 'W2': jax.random.normal(ks[7], (E, FF, D), jnp.float32) * s, 'b2': jnp.zeros((E, D), jnp.float32)}
    _L1_ffn_all = _L1_ffn_setup()
    _L1_ffn_in = {k: v for k, v in _L1_ffn_all.items() if k in ('ln1_g', 'ln1_b', 'Wq', 'bq', 'Wk', 'bk', 'Wv', 'bv', 'Wo', 'bo', 'gate_W', 'gate_b', 'W1', 'b1', 'W2', 'b2')}
    del _L1_ffn_all
    return {'x': x, 'L0_tok_sin_cos_cache': _L0_tok_in['sin_cos_cache'], 'L0_attn_ln1_s': _L0_attn_in['ln1_s'], 'L0_attn_ln1_b': _L0_attn_in['ln1_b'], 'L0_attn_Wq': _L0_attn_in['Wq'], 'L0_attn_bq': _L0_attn_in['bq'], 'L0_attn_Wk': _L0_attn_in['Wk'], 'L0_attn_bk': _L0_attn_in['bk'], 'L0_attn_Wv': _L0_attn_in['Wv'], 'L0_attn_bv': _L0_attn_in['bv'], 'L0_attn_Wo': _L0_attn_in['Wo'], 'L0_attn_bo': _L0_attn_in['bo'], 'L0_attn_proj': _L0_attn_in['proj'], 'L0_attn_ln2_s': _L0_attn_in['ln2_s'], 'L0_attn_ln2_b': _L0_attn_in['ln2_b'], 'L0_attn_W1': _L0_attn_in['W1'], 'L0_attn_b1': _L0_attn_in['b1'], 'L0_attn_W2': _L0_attn_in['W2'], 'L0_attn_b2': _L0_attn_in['b2'], 'L0_ffn_Ws': _L0_ffn_in['Ws'], 'L0_ffn_bs': _L0_ffn_in['bs'], 'L0_ffn_W1': _L0_ffn_in['W1'], 'L0_ffn_b1': _L0_ffn_in['b1'], 'L0_ffn_W2': _L0_ffn_in['W2'], 'L0_ffn_b2': _L0_ffn_in['b2'], 'L1_attn_norm_w': _L1_attn_in['norm_w'], 'L1_attn_f_in_w': _L1_attn_in['f_in_w'], 'L1_attn_f_conv_w': _L1_attn_in['f_conv_w'], 'L1_attn_f_conv_b': _L1_attn_in['f_conv_b'], 'L1_attn_f_dt_bias': _L1_attn_in['f_dt_bias'], 'L1_attn_f_A_log': _L1_attn_in['f_A_log'], 'L1_attn_f_D': _L1_attn_in['f_D'], 'L1_attn_f_gnorm_w': _L1_attn_in['f_gnorm_w'], 'L1_attn_f_out_w': _L1_attn_in['f_out_w'], 'L1_attn_b_in_w': _L1_attn_in['b_in_w'], 'L1_attn_b_conv_w': _L1_attn_in['b_conv_w'], 'L1_attn_b_conv_b': _L1_attn_in['b_conv_b'], 'L1_attn_b_dt_bias': _L1_attn_in['b_dt_bias'], 'L1_attn_b_A_log': _L1_attn_in['b_A_log'], 'L1_attn_b_D': _L1_attn_in['b_D'], 'L1_attn_b_gnorm_w': _L1_attn_in['b_gnorm_w'], 'L1_attn_b_out_w': _L1_attn_in['b_out_w'], 'L1_attn_proj_w': _L1_attn_in['proj_w'], 'L1_ffn_ln1_g': _L1_ffn_in['ln1_g'], 'L1_ffn_ln1_b': _L1_ffn_in['ln1_b'], 'L1_ffn_Wq': _L1_ffn_in['Wq'], 'L1_ffn_bq': _L1_ffn_in['bq'], 'L1_ffn_Wk': _L1_ffn_in['Wk'], 'L1_ffn_bk': _L1_ffn_in['bk'], 'L1_ffn_Wv': _L1_ffn_in['Wv'], 'L1_ffn_bv': _L1_ffn_in['bv'], 'L1_ffn_Wo': _L1_ffn_in['Wo'], 'L1_ffn_bo': _L1_ffn_in['bo'], 'L1_ffn_gate_W': _L1_ffn_in['gate_W'], 'L1_ffn_gate_b': _L1_ffn_in['gate_b'], 'L1_ffn_W1': _L1_ffn_in['W1'], 'L1_ffn_b1': _L1_ffn_in['b1'], 'L1_ffn_W2': _L1_ffn_in['W2'], 'L1_ffn_b2': _L1_ffn_in['b2']}

def reference(x, L0_tok_sin_cos_cache, L0_attn_ln1_s, L0_attn_ln1_b, L0_attn_Wq, L0_attn_bq, L0_attn_Wk, L0_attn_bk, L0_attn_Wv, L0_attn_bv, L0_attn_Wo, L0_attn_bo, L0_attn_proj, L0_attn_ln2_s, L0_attn_ln2_b, L0_attn_W1, L0_attn_b1, L0_attn_W2, L0_attn_b2, L0_ffn_Ws, L0_ffn_bs, L0_ffn_W1, L0_ffn_b1, L0_ffn_W2, L0_ffn_b2, L1_attn_norm_w, L1_attn_f_in_w, L1_attn_f_conv_w, L1_attn_f_conv_b, L1_attn_f_dt_bias, L1_attn_f_A_log, L1_attn_f_D, L1_attn_f_gnorm_w, L1_attn_f_out_w, L1_attn_b_in_w, L1_attn_b_conv_w, L1_attn_b_conv_b, L1_attn_b_dt_bias, L1_attn_b_A_log, L1_attn_b_D, L1_attn_b_gnorm_w, L1_attn_b_out_w, L1_attn_proj_w, L1_ffn_ln1_g, L1_ffn_ln1_b, L1_ffn_Wq, L1_ffn_bq, L1_ffn_Wk, L1_ffn_bk, L1_ffn_Wv, L1_ffn_bv, L1_ffn_Wo, L1_ffn_bo, L1_ffn_gate_W, L1_ffn_gate_b, L1_ffn_W1, L1_ffn_b1, L1_ffn_W2, L1_ffn_b2):
    import jax
    import jax.numpy as jnp

    def _L0_tok_ref(positions, sin_cos_cache):
        import jax, jax.numpy as jnp
        import numpy as np
        EMBED_DIM = 128
        MAX_POSITION = 2500
        BASE = 10000.0
        BATCH, SEQ = (8, 2048)

        def _build_cache():
            freqs = 1.0 / BASE ** (jnp.arange(0, EMBED_DIM, 2, dtype=jnp.float32) / EMBED_DIM)
            positions = jnp.arange(MAX_POSITION, dtype=jnp.float32)
            angles = jnp.outer(positions, freqs)
            return jnp.stack([jnp.sin(angles), jnp.cos(angles)], axis=-1)
        sc = sin_cos_cache[positions]
        interleaved = jnp.stack([sc[..., 1], sc[..., 0]], axis=-1)
        return interleaved.reshape(*positions.shape, EMBED_DIM)

    def _L0_attn_ref(x, ln1_s, ln1_b, Wq, bq, Wk, bk, Wv, bv, Wo, bo, proj, ln2_s, ln2_b, W1, b1, W2, b2):
        import jax, jax.numpy as jnp
        import numpy as np
        B, N, D = (2, 2048, 128)
        L, H, DH, M = (2, 8, 64, 64)
        EPS_K = 0.0001

        def _layernorm(x, s, b):
            m = x.mean(-1, keepdims=True)
            v = x.var(-1, keepdims=True)
            return (x - m) / jnp.sqrt(v + 1e-05) * s + b

        def _softmax_kernel(x, proj, is_query):
            dh = x.shape[-1]
            data_norm = dh ** (-0.25)
            ratio = proj.shape[0] ** (-0.5)
            dd = jnp.einsum('bhnd,md->bhnm', x * data_norm, proj)
            diag = 0.5 * jnp.sum(x * x, axis=-1) * data_norm ** 2
            if is_query:
                stab = jnp.max(dd, axis=-1, keepdims=True)
            else:
                stab = jnp.max(dd, axis=(-1, -2), keepdims=True)
            return ratio * (jnp.exp(dd - diag[..., None] - stab) + EPS_K)

        def _linear_attention(qp, kp, v):
            k_sum = kp.sum(axis=2)
            d_inv = 1.0 / jnp.einsum('bhnm,bhm->bhn', qp, k_sum)
            ctx = jnp.einsum('bhnm,bhnd->bhmd', kp, v)
            return jnp.einsum('bhnm,bhmd,bhn->bhnd', qp, ctx, d_inv)

        def _performer_forward(x, ln1_s, ln1_b, Wq, bq, Wk, bk, Wv, bv, Wo, bo, proj, ln2_s, ln2_b, W1, b1, W2, b2):
            depth = Wq.shape[0]
            for l in range(depth):
                h = _layernorm(x, ln1_s[l], ln1_b[l])
                b, n, d = h.shape

                def heads(t):
                    return t.reshape(b, n, H, DH).transpose(0, 2, 1, 3)
                q = heads(h @ Wq[l] + bq[l])
                k = heads(h @ Wk[l] + bk[l])
                v = heads(h @ Wv[l] + bv[l])
                qp = _softmax_kernel(q, proj[l], True)
                kp = _softmax_kernel(k, proj[l], False)
                attn = _linear_attention(qp, kp, v)
                attn = attn.transpose(0, 2, 1, 3).reshape(b, n, H * DH)
                x = x + (attn @ Wo[l] + bo[l])
                h2 = _layernorm(x, ln2_s[l], ln2_b[l])
                ff = jax.nn.gelu(h2 @ W1[l] + b1[l]) @ W2[l] + b2[l]
                x = x + ff
            return x
        return _performer_forward(x, ln1_s, ln1_b, Wq, bq, Wk, bk, Wv, bv, Wo, bo, proj, ln2_s, ln2_b, W1, b1, W2, b2)

    def _L0_ffn_ref(x, Ws, bs, W1, b1, W2, b2):
        import jax, jax.numpy as jnp
        import numpy as np
        B, S, D, F, E = (4, 512, 128, 512, 8)
        Bb, Ss, Dd = x.shape
        xt = x.reshape(-1, Dd)
        logits = xt @ Ws + bs
        probs = jax.nn.softmax(logits, axis=-1)
        prob_max = jnp.max(probs, axis=-1)
        routes = jnp.argmax(probs, axis=-1)
        onehot = jax.nn.one_hot(routes, W1.shape[0], dtype=xt.dtype)

        def expert_ffn(w1, bb1, w2, bb2):
            h = jax.nn.gelu(xt @ w1 + bb1, approximate=False)
            return h @ w2 + bb2
        y = jax.vmap(expert_ffn)(W1, b1, W2, b2)
        out = jnp.einsum('te,etd->td', onehot, y)
        out = out * prob_max[:, None]
        return out.reshape(Bb, Ss, Dd)

    def _L1_attn_ref(x, norm_w, f_in_w, f_conv_w, f_conv_b, f_dt_bias, f_A_log, f_D, f_gnorm_w, f_out_w, b_in_w, b_conv_w, b_conv_b, b_dt_bias, b_A_log, b_D, b_gnorm_w, b_out_w, proj_w):
        import jax, jax.numpy as jnp
        import numpy as np
        D_MODEL = 128
        D_STATE = 64
        D_CONV = 4
        HEADDIM = 64
        D_INNER = 2 * D_MODEL
        NHEADS = D_INNER // HEADDIM
        CONV_DIM = D_INNER + 2 * D_STATE
        D_IN_PROJ = 2 * D_INNER + 2 * D_STATE + NHEADS
        BATCH, SEQ = (4, 256)
        EPS = 1e-05

        def rmsnorm(x, w):
            return x * jax.lax.rsqrt(jnp.mean(x * x, axis=-1, keepdims=True) + EPS) * w

        def mamba2(u, in_w, conv_w, conv_b, dt_bias, A_log, D, gnorm_w, out_w):
            b, l, _ = u.shape
            zxbcdt = u @ in_w.T
            z = zxbcdt[..., :D_INNER]
            xBC = zxbcdt[..., D_INNER:D_INNER + CONV_DIM]
            dt = jax.nn.softplus(zxbcdt[..., -NHEADS:] + dt_bias)
            pad = jnp.pad(xBC, ((0, 0), (D_CONV - 1, 0), (0, 0)))
            acc = conv_b
            for k in range(D_CONV):
                acc = acc + pad[:, k:k + l, :] * conv_w[:, k]
            xBC = jax.nn.silu(acc)
            x = xBC[..., :D_INNER].reshape(b, l, NHEADS, HEADDIM)
            Bm = xBC[..., D_INNER:D_INNER + D_STATE]
            Cm = xBC[..., D_INNER + D_STATE:]
            A = -jnp.exp(A_log)
            decay = jnp.exp(dt * A)
            dtx = dt[..., None] * x

            def step(h, inp):
                dec, dx, Bt, Ct = inp
                h = h * dec[:, :, None, None] + dx[..., None] * Bt[:, None, None, :]
                y = jnp.einsum('bhpn,bn->bhp', h, Ct)
                return (h, y)
            h0 = jnp.zeros((b, NHEADS, HEADDIM, D_STATE), u.dtype)
            _, ys = jax.lax.scan(step, h0, (decay.transpose(1, 0, 2), dtx.transpose(1, 0, 2, 3), Bm.transpose(1, 0, 2), Cm.transpose(1, 0, 2)))
            y = ys.transpose(1, 0, 2, 3) + x * D[None, None, :, None]
            y = y.reshape(b, l, D_INNER)
            y = rmsnorm(y * jax.nn.silu(z), gnorm_w)
            return y @ out_w.T
        h = rmsnorm(x, norm_w)
        fo = mamba2(h, f_in_w, f_conv_w, f_conv_b, f_dt_bias, f_A_log, f_D, f_gnorm_w, f_out_w)
        bo = jnp.flip(mamba2(jnp.flip(h, 1), b_in_w, b_conv_w, b_conv_b, b_dt_bias, b_A_log, b_D, b_gnorm_w, b_out_w), 1)
        return x + jnp.concatenate([fo, bo], axis=-1) @ proj_w.T

    def _L1_ffn_ref(x, ln1_g, ln1_b, Wq, bq, Wk, bk, Wv, bv, Wo, bo, gate_W, gate_b, W1, b1, W2, b2):
        import jax, jax.numpy as jnp
        import numpy as np
        B, S, D, H, E = (4, 512, 128, 8, 8)
        FF = 4 * D
        HD = D // H
        EPS = 1e-05

        def _layernorm(x, g, b):
            mu = jnp.mean(x, axis=-1, keepdims=True)
            var = jnp.mean((x - mu) ** 2, axis=-1, keepdims=True)
            return (x - mu) * jax.lax.rsqrt(var + EPS) * g + b
        b, s, d = x.shape
        q = (x @ Wq + bq).reshape(b, s, H, HD)
        k = (x @ Wk + bk).reshape(b, s, H, HD)
        v = (x @ Wv + bv).reshape(b, s, H, HD)
        scores = jnp.einsum('bqhd,bkhd->bhqk', q, k) / jnp.sqrt(jnp.float32(HD))
        attn = jax.nn.softmax(scores, axis=-1)
        o = jnp.einsum('bhqk,bkhd->bqhd', attn, v).reshape(b, s, d) @ Wo + bo
        h = _layernorm(x + o, ln1_g, ln1_b)
        t = h.reshape(b * s, d)
        probs = jax.nn.softmax(t @ gate_W + gate_b, axis=-1)
        idx = jnp.argmax(probs, axis=-1)
        gw = jnp.max(probs, axis=-1)
        hid = jax.nn.gelu(jnp.einsum('nd,edf->enf', t, W1) + b1[:, None, :])
        out_all = jnp.einsum('enf,efd->end', hid, W2) + b2[:, None, :]
        onehot = jax.nn.one_hot(idx, E, dtype=t.dtype)
        out = jnp.einsum('ne,end->nd', onehot, out_all)
        out = out * gw[:, None]
        return out.reshape(b, s, d)
    h = _L0_tok_ref(x, L0_tok_sin_cos_cache)
    h = h + _L0_attn_ref(_layernorm(h, axis=-1), L0_attn_ln1_s, L0_attn_ln1_b, L0_attn_Wq, L0_attn_bq, L0_attn_Wk, L0_attn_bk, L0_attn_Wv, L0_attn_bv, L0_attn_Wo, L0_attn_bo, L0_attn_proj, L0_attn_ln2_s, L0_attn_ln2_b, L0_attn_W1, L0_attn_b1, L0_attn_W2, L0_attn_b2)
    h = h + _L0_ffn_ref(_layernorm(h, axis=-1), L0_ffn_Ws, L0_ffn_bs, L0_ffn_W1, L0_ffn_b1, L0_ffn_W2, L0_ffn_b2)
    h = h + _L1_attn_ref(_layernorm(h, axis=-1), L1_attn_norm_w, L1_attn_f_in_w, L1_attn_f_conv_w, L1_attn_f_conv_b, L1_attn_f_dt_bias, L1_attn_f_A_log, L1_attn_f_D, L1_attn_f_gnorm_w, L1_attn_f_out_w, L1_attn_b_in_w, L1_attn_b_conv_w, L1_attn_b_conv_b, L1_attn_b_dt_bias, L1_attn_b_A_log, L1_attn_b_D, L1_attn_b_gnorm_w, L1_attn_b_out_w, L1_attn_proj_w)
    h = h + _L1_ffn_ref(_layernorm(h, axis=-1), L1_ffn_ln1_g, L1_ffn_ln1_b, L1_ffn_Wq, L1_ffn_bq, L1_ffn_Wk, L1_ffn_bk, L1_ffn_Wv, L1_ffn_bv, L1_ffn_Wo, L1_ffn_bo, L1_ffn_gate_W, L1_ffn_gate_b, L1_ffn_W1, L1_ffn_b1, L1_ffn_W2, L1_ffn_b2)
    return h

_drawn_inputs = setup_inputs


def setup_inputs(seed=0):
    import zlib

    import numpy as np

    out = dict(_drawn_inputs(seed))
    spreads = {'L0_attn_ln1_s': (1.0, 0.6),
     'L0_attn_ln1_b': (0.0, 0.8),
     'L0_attn_bq': (0.0, 2.0),
     'L0_attn_bk': (0.0, 0.8),
     'L0_attn_bv': (0.0, 0.1),
     'L0_attn_bo': (0.0, 0.1),
     'L0_attn_ln2_s': (1.0, 0.6),
     'L0_attn_ln2_b': (0.0, 0.8),
     'L0_attn_b1': (0.0, 0.397),
     'L0_attn_b2': (0.0, 0.1),
     'L0_ffn_bs': (0.0, 0.8),
     'L0_ffn_b1': (0.0, 0.8),
     'L0_ffn_b2': (0.0, 0.8),
     'L1_attn_norm_w': (1.0, 0.6),
     'L1_attn_f_conv_b': (0.0, 0.345),
     'L1_attn_f_D': (1.0, 0.6),
     'L1_attn_f_gnorm_w': (1.0, 0.6),
     'L1_attn_b_conv_b': (0.0, 0.334),
     'L1_attn_b_D': (1.0, 0.6),
     'L1_attn_b_gnorm_w': (1.0, 0.6),
     'L1_ffn_ln1_g': (1.0, 0.6),
     'L1_ffn_ln1_b': (0.0, 0.8),
     'L1_ffn_bq': (0.0, 0.8),
     'L1_ffn_bk': (0.0, 2.0),
     'L1_ffn_bv': (0.0, 0.8),
     'L1_ffn_bo': (0.0, 0.8),
     'L1_ffn_gate_b': (0.0, 0.8),
     'L1_ffn_b1': (0.0, 0.8),
     'L1_ffn_b2': (0.0, 0.8)}
    factors = {'L0_attn_Wq': 64.0,
     'L0_attn_Wk': 8.0,
     'L0_attn_proj': 64.0,
     'L0_ffn_Ws': 5.119,
     'L0_ffn_W1': 8.0,
     'L0_ffn_W2': 8.0,
     'L1_attn_f_conv_w': 5.649,
     'L1_attn_f_dt_bias': 8.0,
     'L1_attn_f_A_log': 8.0,
     'L1_attn_b_conv_w': 5.059,
     'L1_attn_b_dt_bias': 8.0,
     'L1_attn_b_A_log': 23.825,
     'L1_ffn_Wq': 8.0,
     'L1_ffn_Wk': 8.0,
     'L1_ffn_Wv': 8.0,
     'L1_ffn_Wo': 8.0,
     'L1_ffn_gate_W': 7.569,
     'L1_ffn_W1': 8.0,
     'L1_ffn_W2': 8.0}
    for name, (base, spread) in spreads.items():
        noise = np.random.default_rng([zlib.crc32(name.encode()), seed]).standard_normal(out[name].shape)
        drawn = base * np.exp(spread * noise) if base else spread * noise
        out[name] = jnp.asarray(drawn.astype(out[name].dtype))
    for name, factor in factors.items():
        out[name] = (out[name] * factor).astype(out[name].dtype)
    return out
```

```python
from contextlib import ExitStack

import concourse.bass as bass
from concourse import mybir

F32 = mybir.dt.float32
I32 = mybir.dt.int32
U32 = mybir.dt.uint32
ALU = mybir.AluOpType
ACT = mybir.ActivationFunctionType
AX = mybir.AxisListType.X

P = 128
SEQS, SEQ_TILES = 32, 2
TILES = SEQS * SEQ_TILES
LANES = 4
HEADS, HEAD = 8, 64
WIDE = HEADS * HEAD
BLOCKS = WIDE // P
EXPERTS = 8
SORTED = TILES + EXPERTS
EPS = 1e-5
KERNEL_EPS = 1e-4
DATA_NORM = HEAD ** -0.25
DIAG = 0.5 * HEAD ** -0.5


def both(i, s):
    return i + (s + 1)


def signals(nc, ctx):
    taken = []

    def take(name):
        taken.append(nc.alloc_semaphore(name))
        return taken[-1]

    def clear():
        nc.clear_and_free_semaphores(taken)
        nc.all_engine_barrier()

    ctx.callback(clear)
    return take


def in_turn(*parts):
    waiting = [[next(part, None), n, part] for n, part in enumerate(parts)]
    while True:
        ready = [w for w in waiting if w[0] is not None]
        if not ready:
            return
        least = min(ready, key=lambda w: (w[0], w[1]))
        least[0] = next(least[2], None)


def skewed(engine, first, second):
    in_turn(first(0, 0))
    with engine.Fori(0, SEQS - 3, 2) as i:
        in_turn(first(i, 1), second(i, 0))
        in_turn(first(i + 2, 0), second(i, 1))
    in_turn(first(SEQS - 2, 1), second(SEQS - 2, 0))
    in_turn(second(SEQS - 2, 1))


class Chip:
    pass


def broadcast_rows(vector_ap, width):
    return bass.AP(vector_ap.tensor, vector_ap.offset, [[0, P], [1, width]])


def fold_norm(nc, c, ctx, name, items, landed, landed_count, folds=()):
    take = signals(nc, ctx)
    raw_product = take(f"{name}_raw_product")
    scaled = take(f"{name}_scaled")
    row_product = take(f"{name}_row_product")
    folded = take(f"{name}_folded")
    turned = take(f"{name}_turned")
    turned_kept = take(f"{name}_turned_kept")
    joined = take(f"{name}_joined")
    joined_kept = take(f"{name}_joined_kept")
    row_sum = ctx.enter_context(nc.sbuf_tensor(f"{name}_row_sum", [P, WIDE], F32))
    turned_sb = ctx.enter_context(nc.sbuf_tensor(f"{name}_turned_sb", [P, WIDE], F32))

    with nc.Block() as block:
        @block.tensor
        def _(pe):
            pe.wait_ge(landed, landed_count)
            for m, (w, scale, norm_bias, bias) in enumerate(items):
                n = w.shape[1]
                rows = c.PS[:, m % 4, 0:n]
                if m >= 4:
                    pe.wait_ge(folded, m - 3)
                if norm_bias is not None:
                    nc.tensor.matmul(rows, norm_bias, w, start=True, stop=False).then_inc(raw_product, 1)
                if scale is not None:
                    pe.wait_ge(scaled, m + 1)
                nc.tensor.matmul(rows, c.minus_ones[:, :], w, start=norm_bias is None, stop=True).then_inc(row_product, 1)
            for m, (w, matrix, _) in enumerate(folds):
                pe.wait_ge(folded, len(items))
                if m:
                    pe.wait_ge(joined_kept, m)
                for b in range(BLOCKS):
                    last = nc.tensor.transpose(c.PS[:, 4, bass.ts(b, P)], w[:, bass.ts(b, P)], c.ident[:, :])
                last.then_inc(turned, 1)
                pe.wait_ge(turned_kept, m + 1)
                for b in range(BLOCKS):
                    last = nc.tensor.matmul(c.PS[:, 5, bass.ts(b, P)], turned_sb[:, bass.ts(b, P)], matrix,
                                            start=True, stop=True)
                last.then_inc(joined, 1)

        @block.vector
        def _(dve):
            dve.wait_ge(landed, landed_count)
            for m, (w, scale, norm_bias, bias) in enumerate(items):
                n = w.shape[1]
                rows = c.PS[:, m % 4, 0:n]
                if scale is not None:
                    dve.wait_ge(raw_product, m + 1)
                    nc.vector.tensor_scalar(w, w, scale, None, ALU.mult).then_inc(scaled, 1)
                dve.wait_ge(row_product, m + 1)
                if bias is not None:
                    nc.vector.tensor_tensor(row_sum[:, 0:n], rows, bias, ALU.add)
                else:
                    nc.vector.tensor_copy(row_sum[:, 0:n], rows)
                dve.drain()
                nc.vector.scalar_tensor_tensor(w, row_sum[:, 0:n], 1.0 / P, w, ALU.mult, ALU.add).then_inc(folded, 1)
                dve.drain()
            for m, (_, _, product) in enumerate(folds):
                dve.wait_ge(turned, m + 1)
                nc.vector.tensor_copy(turned_sb[:, :], c.PS[:, 4, :]).then_inc(turned_kept, 1)
                dve.wait_ge(joined, m + 1)
                nc.vector.tensor_copy(product, c.PS[:, 5, :]).then_inc(joined_kept, 1)


def load_constants(nc, c, ins, ctx):
    sb = lambda n, shape, dt=F32: ctx.enter_context(nc.sbuf_tensor(n, shape, dt))
    c.H = sb("H", [P, TILES, P])
    c.X = sb("X", [P, SORTED, P])
    c.ident = sb("ident", [P, P])
    c.minus_ones = sb("minus_ones", [P, P])
    c.minus_half = sb("minus_half", [P, 4])
    c.eps = sb("eps", [P, 4])
    c.kernel_eps = sb("kernel_eps", [P, 1])
    c.ids = sb("ids", [P, TILES], I32)
    c.before = sb("before", [P, P])
    c.experts = sb("experts", [P, EXPERTS])
    c.tile_start = sb("tile_start", [1, SORTED])
    c.logits = sb("logits", [P, TILES, EXPERTS])
    c.weight = sb("weight", [P, TILES])
    c.row_of = sb("row_of", [P, TILES], I32)
    c.tile_expert = sb("tile_expert", [1, SORTED], I32)
    c.sorted_in = nc.dram_tensor("sorted_in", [(SORTED + LANES) * P, P], F32).ap()
    c.sorted_out = nc.dram_tensor("sorted_out", [SORTED * P, P], F32).ap()
    c.PS = ctx.enter_context(nc.psum_tensor("PS", [P, 8, 512], F32))
    landed = ctx.enter_context(nc.semaphore("constants_landed"))
    zeroed = ctx.enter_context(nc.semaphore("zeroed"))
    c.weights_landed = [ctx.enter_context(nc.semaphore(f"expert_weights_landed_{n}")) for n in range(2)]
    with nc.Block() as block:
        @block.sync
        def _(sp):
            sp.dma_start(c.ident[:, :], ins["ident"]).then_inc(landed, 16)
            sp.dma_start(c.ids[:, :], ins["ids"]).then_inc(landed, 16)
            sp.dma_start(c.before[:, :], ins["before"]).then_inc(landed, 16)
            sp.dma_start(c.experts[:, :], ins["experts"]).then_inc(landed, 16)
            sp.dma_start(c.tile_start[:, :], ins["tile_start"]).then_inc(landed, 16)
            sp.wait_ge(zeroed, 1)
            rows = c.sorted_in.rearrange("(p r) d -> p (r d)", p=P)
            sp.dma_start(rows[:, 0:SORTED * P], c.X[:, :, :].rearrange("p r d -> p (r d)")).then_inc(landed, 16)
            sp.dma_start(rows[:, SORTED * P:], c.X[:, 0:LANES, :].rearrange("p r d -> p (r d)")).then_inc(landed, 16)
            sp.wait_ge(landed, 7 * 16)

        @block.vector
        def _(dve):
            nc.vector.memset(c.X[:, :, :], 0.0).then_inc(zeroed, 1)
            nc.vector.memset(c.minus_ones[:, :], -1.0)
            nc.vector.memset(c.minus_half[:, :], -0.5)
            nc.vector.memset(c.eps[:, :], EPS)
            dve.drain()


def embed(nc, c, ins):
    with ExitStack() as ctx:
        sb = lambda n, shape, dt=F32: ctx.enter_context(nc.sbuf_tensor(n, shape, dt))
        sem = signals(nc, ctx)
        ids = [[sb(f"id_{s}_{t}", [P, 1], I32) for t in range(2)] for s in range(2)]
        rows = [sb(f"rows_{s}", [P, SEQ_TILES, P]) for s in range(2)]
        norm = [NormBuffers(nc, ctx, f"embed_{s}") for s in range(2)]
        ids_ready = [sem(f"ids_ready_{s}") for s in range(2)]
        gathered = [sem(f"gathered_{s}") for s in range(2)]
        stats = sem("embed_stats")
        rstd = sem("embed_rstd")
        normed = sem("embed_normed")
        block = ctx.enter_context(nc.Block())

        @block.gpsimd
        def _(pool):
            with pool.Fori(0, SEQS - 1, 2) as i:
                for s in range(2):
                    for t in range(2):
                        nc.gpsimd.tensor_copy(ids[s][t][:, :], c.ids[:, bass.ds((i + s) * 2 + t, 1)])
                pool.drain()
                for s in range(2):
                    for t in range(2):
                        pool.indirect_dma_start(out=rows[s][:, t, :], out_offset=None, in_=ins["cache"],
                                                in_offset=bass.IndirectOffsetOnAxis(ap=ids[s][t][:, :], axis=0)
                                                ).then_inc(gathered[s], 16)
                for s in range(2):
                    pool.wait_ge(stats, both(i, s))
                    norm_rstd(nc, pool, c, norm[s])
                    norm[s].last.then_inc(rstd, 1)
                for s in range(2):
                    pool.wait_ge(normed, both(i, s))

        @block.vector
        def _(dve):
            with dve.Fori(0, SEQS - 1, 2) as i:
                for s in range(2):
                    dve.wait_ge(gathered[s], (i + 2) * 16)
                    norm_stats(nc, dve, norm[s], rows[s])
                    norm[s].last.then_inc(stats, 1)
                for s in range(2):
                    dve.wait_ge(rstd, both(i, s))
                    nc.vector.tensor_copy(c.H[:, bass.ds((i + s) * 2, 2), :], rows[s][:, :, :])
                    norm_apply(nc, norm[s], rows[s], lambda t: c.X[:, bass.ds((i + s) * 2 + t, 1), :])
                    norm[s].last.then_inc(normed, 1)
                dve.drain()


class NormBuffers:

    def __init__(self, nc, ctx, name):
        sb = lambda n, shape: ctx.enter_context(nc.sbuf_tensor(f"{name}_{n}", shape, F32))
        self.sums = sb("sums", [P, SEQ_TILES, 6])
        self.stat = sb("stat", [P, SEQ_TILES, 2])
        self.rstd = sb("rstd", [P, SEQ_TILES])
        self.last = None


def norm_stats(nc, dve, norm, rows):
    for t in range(SEQ_TILES):
        nc.vector.bn_stats(norm.sums[:, t, :], rows[:, t, :])
    dve.drain()
    for t in range(SEQ_TILES):
        norm.last = nc.vector.bn_aggr(norm.stat[:, t, :], norm.sums[:, t, :])


def norm_rstd(nc, pool, c, norm):
    nc.gpsimd.tensor_tensor(norm.rstd[:, :], norm.stat[:, :, 1], c.eps[:, 0:SEQ_TILES], ALU.add)
    pool.drain()
    norm.last = nc.gpsimd.tensor_tensor(norm.rstd[:, :], norm.rstd[:, :], c.minus_half[:, 0:SEQ_TILES], ALU.pow)


def norm_apply(nc, norm, rows, out):
    for t in range(SEQ_TILES):
        norm.last = nc.vector.tensor_scalar(out(t), rows[:, t, :], norm.stat[:, t, 0:1], norm.rstd[:, t:t + 1],
                                            ALU.subtract, ALU.mult)


def performer_weights(nc, c, ctx):
    sb = lambda n, shape: ctx.enter_context(nc.sbuf_tensor(f"performer_{n}", shape, F32))
    w = Chip()
    w.q, w.k, w.v, w.qd, w.kd, w.w1 = (sb(n, [P, WIDE]) for n in ("q", "k", "v", "qd", "kd", "w1"))
    w.wo, w.w2 = (sb(n, [P, BLOCKS, P]) for n in ("wo", "w2"))
    w.bo, w.b2 = (sb(n, [P, P]) for n in ("bo", "b2"))
    return w


def prepare_performer(nc, c, w, ins, layer):
    with ExitStack() as ctx:
        sb = lambda n, shape: ctx.enter_context(nc.sbuf_tensor(f"prepare_{layer}_{n}", shape, F32))
        take = signals(nc, ctx)
        sem = lambda n: take(f"prepare_{layer}_{n}")
        loaded = sem("loaded")
        ready = sem("ready")
        columns = sb("columns", [P, 4])
        wide_bias = {n: sb(n, [P, WIDE]) for n in ("bq", "bk", "bv", "b1")}
        norm_bias = [sb("ln1_bias_wide", [P, P]), sb("ln2_bias_wide", [P, P])]
        proj = sb("proj", [P, P])
        row = lambda n: ins[n][layer]
        with nc.Block() as block:
            @block.sync
            def _(sp):
                n = 0
                for at, name in ((w.q, "Wq"), (w.k, "Wk"), (w.v, "Wv"), (w.w1, "W1")):
                    sp.dma_start(at[:, :], row(f"L0_attn_{name}")).then_inc(loaded, 16)
                for at, name in ((w.wo, "Wo"), (w.w2, "W2")):
                    sp.dma_start(at[:, :, :], row(f"L0_attn_{name}").rearrange("(b p) d -> p b d", p=P)).then_inc(loaded, 16)
                for at, name in ((w.bo, "bo"), (w.b2, "b2")):
                    sp.dma_start(at[:, :], broadcast_rows(row(f"L0_attn_{name}"), P)).then_inc(loaded, 16)
                for name, at in wide_bias.items():
                    sp.dma_start(at[:, :], broadcast_rows(row(f"L0_attn_{name}"), WIDE)).then_inc(loaded, 16)
                for k, name in enumerate(("ln1_s", "ln1_b", "ln2_s", "ln2_b")):
                    sp.dma_start(columns[:, k:k + 1], row(f"L0_attn_{name}").rearrange("(p o) -> p o", o=1)).then_inc(loaded, 16)
                sp.wait_ge(ready, 1)
                for h in range(2):
                    sp.dma_start(proj[bass.ts(h, HEAD), bass.ts(h, HEAD)], ins["projT"][layer]).then_inc(loaded, 16)
                sp.wait_ge(loaded, 18 * 16)

            @block.vector
            def _(dve):
                nc.vector.memset(proj[:, :], 0.0).then_inc(ready, 1)
                dve.wait_ge(loaded, 18 * 16)
                for k in range(2):
                    nc.vector.tensor_copy(norm_bias[k][:, :], columns[:, 2 * k + 1:2 * k + 2].to_broadcast([P, P]))
                nc.vector.tensor_scalar(proj[:, :], proj[:, :], DATA_NORM, None, ALU.mult)
                dve.drain()
        scale1, scale2 = columns[:, 0:1], columns[:, 2:3]
        fold_norm(nc, c, ctx, f"performer_{layer}",
                  [(w.q[:, :], scale1, norm_bias[0][:, :], wide_bias["bq"][:, :]),
                   (w.k[:, :], scale1, norm_bias[0][:, :], wide_bias["bk"][:, :]),
                   (w.v[:, :], scale1, norm_bias[0][:, :], wide_bias["bv"][:, :]),
                   (w.w1[:, :], scale2, norm_bias[1][:, :], wide_bias["b1"][:, :])],
                  loaded, 18 * 16,
                  [(w.q[:, :], proj[:, :], w.qd[:, :]), (w.k[:, :], proj[:, :], w.kd[:, :])])


def performer(nc, c, w, layer):
    with ExitStack() as ctx:
        sb = lambda n, shape: [ctx.enter_context(nc.sbuf_tensor(f"p{layer}_{n}_{s}", shape, F32)) for s in range(2)]
        take = signals(nc, ctx)
        sem = lambda n: take(f"p{layer}_{n}")
        xn = sb("xn", [P, SEQ_TILES, P])
        xb = sb("xb", [P, SEQ_TILES, P])
        x2 = sb("x2", [P, SEQ_TILES, P])
        hT = sb("hT", [P, SEQ_TILES * P])
        square = sb("square", [P, SEQ_TILES * WIDE])
        feat = sb("feat", [P, SEQ_TILES * WIDE])
        featT = sb("featT", [P, BLOCKS, SEQ_TILES * P])
        attn = sb("attn", [P, SEQ_TILES * WIDE])
        v = sb("v", [P, SEQ_TILES, HEADS, HEAD + 1])
        ctx_sb = sb("ctx", [P, BLOCKS, 2, HEAD + 1])
        top = sb("top", [P, 2 * HEADS])
        top8 = sb("top8", [P, HEADS])
        top1 = sb("top1", [HEADS, 1])
        power = sb("power", [P, 2 * HEADS])
        shift = sb("shift", [P, 2 * HEADS])
        share = sb("share", [P, 2 * HEADS])
        norm = [NormBuffers(nc, ctx, f"p{layer}_norm_{s}") for s in range(2)]
        bank = lambda s, b: c.PS[:, 4 * s + b, :]
        banks = lambda s, b, n: c.PS[:, 4 * s + b:4 * s + b + n, :]
        m = Chip()
        m.stats, m.rstd, m.xb_ready, m.xn_ready, m.xnT, m.hT_ready, m.k_made = map(sem, (
            "stats", "rstd", "xb_ready", "xn_ready", "xnT", "hT_ready", "k_made"))
        m.k_squared, m.k_top, m.k_topT, m.k_top1, m.k_topped, m.k_arg, m.k_exp = map(sem, (
            "k_squared", "k_top", "k_topT", "k_top1", "k_topped", "k_arg", "k_exp"))
        m.k_feat, m.v_made, m.v_kept, m.ctx_made, m.ctx_kept, m.q_made, m.q_squared = map(sem, (
            "k_feat", "v_made", "v_kept", "ctx_made", "ctx_kept", "q_made", "q_squared"))
        m.qd_made, m.q_arg, m.q_exp, m.q_featT, m.q_featT_kept, m.weighed, m.attn_kept = map(sem, (
            "qd_made", "q_arg", "q_exp", "q_featT", "q_featT_kept", "weighed", "attn_kept"))
        m.attnT, m.attnT_kept, m.o_made, m.x2_stats, m.x2_rstd, m.x2b_ready, m.x2n_ready = map(sem, (
            "attnT", "attnT_kept", "o_made", "x2_stats", "x2_rstd", "x2b_ready", "x2n_ready"))
        m.x2nT, m.h2T_ready, m.f_made, m.f_kept, m.y_made, m.done, m.constant = map(sem, (
            "x2nT", "h2T_ready", "f_made", "f_kept", "y_made", "done", "constant"))
        N = SEQS

        block = ctx.enter_context(nc.Block())

        @block.tensor
        def _(pe):
            def first(i, s):
                yield 2.36
                pe.wait_ge(m.xn_ready, both(i, s))
                for t in range(2):
                    last = nc.tensor.transpose(bank(s, 0)[:, bass.ts(t, P)], xn[s][:, t, :], c.ident[:, :])
                last.then_inc(m.xnT, 1)
                yield 3.66
                pe.wait_ge(m.hT_ready, both(i, s))
                for t in range(2):
                    nc.tensor.matmul(bank(s, t), hT[s][:, bass.ts(t, P)], w.k[:, :], start=True, stop=True)
                for t in range(2):
                    last = nc.tensor.matmul(bank(s, 2 + t), hT[s][:, bass.ts(t, P)], w.kd[:, :], start=True, stop=True)
                last.then_inc(m.k_made, 1)
                yield 8.96
                pe.wait_ge(m.k_top, both(i, s))
                pe.wait_ge(m.k_squared, both(i, s))
                nc.tensor.transpose(bank(s, 0)[0:HEADS, 0:P], top8[s][:, :], c.ident[:, :]).then_inc(m.k_topT, 1)
                yield 10.33
                pe.wait_ge(m.k_top1, both(i, s))
                nc.tensor.matmul(bank(s, 0)[:, 256:256 + HEADS], top1[s][:, 0:1].to_broadcast([HEADS, P]),
                                 c.ident[0:HEADS, 0:HEADS], start=True, stop=True).then_inc(m.k_topped, 1)
                yield 12.83
                pe.wait_ge(m.k_arg, both(i, s))
                for t in range(2):
                    last = nc.tensor.matmul(bank(s, t), hT[s][:, bass.ts(t, P)], w.v[:, :], start=True, stop=True)
                last.then_inc(m.v_made, 1)
                yield 14.69
                pe.wait_ge(m.v_kept, both(i, s))
                for t in range(2):
                    last = nc.tensor.matmul(bank(s, t), hT[s][:, bass.ts(t, P)], w.q[:, :], start=True, stop=True)
                last.then_inc(m.q_made, 1)
                yield 17.83
                pe.wait_ge(m.k_feat, both(i, s))
                for b in range(BLOCKS):
                    out = bank(s, 2 + b // 2)[:, (b % 2) * 130:(b % 2) * 130 + 130]
                    for t in range(2):
                        last = nc.tensor.matmul(out, feat[s][:, t * WIDE + b * P:t * WIDE + (b + 1) * P],
                                                v[s][:, t, 2 * b:2 * b + 2, :].rearrange("p h d -> p (h d)"),
                                                start=t == 0, stop=t == 1)
                last.then_inc(m.ctx_made, 1)
                yield 20.18
                pe.wait_ge(m.ctx_kept, both(i, s))
                for t in range(2):
                    last = nc.tensor.matmul(bank(s, 2 + t), hT[s][:, bass.ts(t, P)], w.qd[:, :], start=True, stop=True)
                last.then_inc(m.qd_made, 1)

            def second(i, s):
                yield 2.74
                pe.wait_ge(m.q_squared, both(i, s))
                pe.wait_ge(m.q_exp, both(i, s))
                for b in range(BLOCKS):
                    for t in range(2):
                        out = bank(s, b // 2)[:, (b % 2) * 256 + t * P:(b % 2) * 256 + (t + 1) * P]
                        last = nc.tensor.transpose(out, feat[s][:, t * WIDE + b * P:t * WIDE + (b + 1) * P], c.ident[:, :])
                last.then_inc(m.q_featT, 1)
                yield 6.4
                pe.wait_ge(m.q_featT_kept, both(i, s))
                for t in range(2):
                    for b in range(BLOCKS):
                        out = bank(s, 2 * t + b // 2)[:, (b % 2) * 130:(b % 2) * 130 + 130]
                        last = nc.tensor.matmul(out, featT[s][:, b, bass.ts(t, P)],
                                                ctx_sb[s][:, b, :, :].rearrange("p h d -> p (h d)"), start=True, stop=True)
                last.then_inc(m.weighed, 1)
                yield 9
                pe.wait_ge(m.attn_kept, both(i, s))
                for b in range(BLOCKS):
                    for t in range(2):
                        out = bank(s, b // 2)[:, (b % 2) * 256 + t * P:(b % 2) * 256 + (t + 1) * P]
                        last = nc.tensor.transpose(out, attn[s][:, t * WIDE + b * P:t * WIDE + (b + 1) * P], c.ident[:, :])
                last.then_inc(m.attnT, 1)
                yield 11.85
                pe.wait_ge(m.attnT_kept, both(i, s))
                for t in range(2):
                    for b in range(BLOCKS):
                        last = nc.tensor.matmul(bank(s, 2)[:, bass.ts(t, P)], featT[s][:, b, bass.ts(t, P)], w.wo[:, b, :],
                                                start=b == 0, stop=b == BLOCKS - 1)
                last.then_inc(m.o_made, 1)
                yield 19.53
                pe.wait_ge(m.x2n_ready, both(i, s))
                for t in range(2):
                    last = nc.tensor.transpose(bank(s, 3)[:, bass.ts(t, P)], xn[s][:, t, :], c.ident[:, :])
                last.then_inc(m.x2nT, 1)
                yield 20.32
                pe.wait_ge(m.h2T_ready, both(i, s))
                for b in range(BLOCKS):
                    last = nc.tensor.matmul(bank(s, b // 2)[:, (b % 2) * 256:(b % 2) * 256 + 256], w.w1[:, bass.ts(b, P)],
                                            hT[s][:, :], start=True, stop=True)
                last.then_inc(m.f_made, 1)
                yield 23.57
                pe.wait_ge(m.f_kept, both(i, s))
                for t in range(2):
                    for b in range(BLOCKS):
                        last = nc.tensor.matmul(bank(s, 2)[:, bass.ts(t, P)], featT[s][:, b, bass.ts(t, P)], w.w2[:, b, :],
                                                start=b == 0, stop=b == BLOCKS - 1)
                last.then_inc(m.y_made, 1)

            skewed(pe, first, second)

        @block.scalar
        def _(act):
            def first(i, s):
                yield 7.43
                act.wait_ge(m.k_made, both(i, s))
                nc.scalar.activation(square[s][:, :], banks(s, 0, 2), ACT.Square).then_inc(m.k_squared, 1)
                yield 12.55
                act.wait_ge(m.k_arg, both(i, s))
                nc.scalar.activation(feat[s][:, :], feat[s][:, :], ACT.Exp).then_inc(m.k_exp, 1)
                yield 13.8
                act.wait_ge(m.v_made, both(i, s))
                nc.scalar.activation(v[s][:, :, :, 0:HEAD].rearrange("p t h d -> p (t h) d"),
                                     banks(s, 0, 2).rearrange("p t (h d) -> p (t h) d", d=HEAD), ACT.Copy).then_inc(m.v_kept, 1)
                yield 17.93
                act.wait_ge(m.q_made, both(i, s))
                nc.scalar.activation(square[s][:, :], banks(s, 0, 2), ACT.Square).then_inc(m.q_squared, 1)

            def second(i, s):
                yield 0.96
                act.wait_ge(m.q_arg, both(i, s))
                nc.scalar.activation(feat[s][:, :], feat[s][:, :], ACT.Exp).then_inc(m.q_exp, 1)
                yield 11.28
                act.wait_ge(m.attnT, both(i, s))
                nc.scalar.activation(featT[s][:, :, :], banks(s, 0, 2).rearrange("p b (c n) -> p (b c) n", n=256), ACT.Copy).then_inc(m.attnT_kept, 1)
                yield 21.77
                act.wait_ge(m.f_made, both(i, s))
                nc.scalar.activation(featT[s][:, :, :], banks(s, 0, 2).rearrange("p b (c n) -> p (b c) n", n=256), ACT.Gelu_apprx_tanh).then_inc(m.f_kept, 1)

            skewed(act, first, second)

        @block.gpsimd
        def _(pool):
            def first(i, s):
                yield 1.45
                pool.wait_ge(m.stats, both(i, s))
                norm_rstd(nc, pool, c, norm[s])
                norm[s].last.then_inc(m.rstd, 1)
                for t in range(2):
                    last = nc.gpsimd.tensor_tensor(xb[s][:, t, :], c.X[:, bass.ds((i + s) * 2 + t, 1), :].rearrange("p o d -> p (o d)"), w.bo[:, :], ALU.add)
                last.then_inc(m.xb_ready, 1)
                yield 14.44
                pool.wait_ge(m.k_exp, both(i, s))
                nc.gpsimd.tensor_tensor(feat[s][:, :], feat[s][:, :], c.kernel_eps[:, 0:1].to_broadcast([P, SEQ_TILES * WIDE]), ALU.add).then_inc(m.k_feat, 1)

            def second(i, s):
                yield 15.58
                pool.wait_ge(m.x2_stats, both(i, s))
                norm_rstd(nc, pool, c, norm[s])
                norm[s].last.then_inc(m.x2_rstd, 1)
                for t in range(2):
                    last = nc.gpsimd.tensor_tensor(xb[s][:, t, :], x2[s][:, t, :], w.b2[:, :], ALU.add)
                last.then_inc(m.x2b_ready, 1)

            skewed(pool, first, second)

        @block.vector
        def _(dve):
            for s in range(2):
                nc.vector.memset(v[s][:, :, :, HEAD:HEAD + 1], 1.0)
                nc.vector.memset(ctx_sb[s][:, :, :, :], 0.0)
            if layer == 0:
                nc.vector.memset(c.kernel_eps[:, :], KERNEL_EPS)
            dve.drain()
            halves = lambda a: a.rearrange("p (t h) -> p t h", t=2)
            heads = lambda a: a.rearrange("p (g d) -> p g d", d=HEAD)

            def exponent(s, shift_of):
                nc.vector.tensor_reduce(power[s][:, :], heads(square[s][:, :]), AX, ALU.add)
                dve.drain()
                shift_of()
                dve.drain()
                return nc.vector.tensor_tensor(heads(feat[s][:, :]), banks(s, 2, 2).rearrange("p t (h d) -> p (t h) d", d=HEAD),
                                               shift[s][:, :].unsqueeze(2).to_broadcast([P, 2 * HEADS, HEAD]), ALU.subtract)

            def first(i, s):
                yield 0.66
                rows = c.X[:, bass.ds((i + s) * 2, 2), :]
                for t in range(SEQ_TILES):
                    nc.vector.bn_stats(norm[s].sums[:, t, :], c.X[:, bass.ds((i + s) * 2 + t, 1), :].rearrange("p o d -> p (o d)"))
                dve.drain()
                for t in range(SEQ_TILES):
                    last = nc.vector.bn_aggr(norm[s].stat[:, t, :], norm[s].sums[:, t, :])
                last.then_inc(m.stats, 1)
                yield 2.35
                dve.wait_ge(m.rstd, both(i, s))
                for t in range(SEQ_TILES):
                    last = nc.vector.tensor_scalar(xn[s][:, t, :], c.X[:, bass.ds((i + s) * 2 + t, 1), :].rearrange("p o d -> p (o d)"),
                                                   norm[s].stat[:, t, 0:1], norm[s].rstd[:, t:t + 1], ALU.subtract, ALU.mult)
                last.then_inc(m.xn_ready, 1)
                yield 2.37
                dve.wait_ge(m.xnT, both(i, s))
                nc.vector.tensor_scalar(hT[s][:, :], bank(s, 0)[:, 0:256], 1.0, None, ALU.add).then_inc(m.hT_ready, 1)
                yield 7.84
                dve.wait_ge(m.k_made, both(i, s))
                nc.vector.tensor_reduce(top[s][:, :], banks(s, 2, 2).rearrange("p t (h d) -> p (t h) d", d=HEAD), AX, ALU.max)
                dve.drain()
                nc.vector.tensor_tensor(top8[s][:, :], top[s][:, 0:HEADS], top[s][:, HEADS:], ALU.max).then_inc(m.k_top, 1)
                yield 10.32
                dve.wait_ge(m.k_topT, both(i, s))
                nc.vector.tensor_reduce(top1[s][:, :], bank(s, 0)[0:HEADS, 0:P], AX, ALU.max).then_inc(m.k_top1, 1)
                yield 10.34
                dve.wait_ge(m.k_topped, both(i, s))
                dve.wait_ge(m.k_squared, both(i, s))
                exponent(s, lambda: nc.vector.scalar_tensor_tensor(
                    halves(shift[s][:, :]), halves(power[s][:, :]), DIAG,
                    bank(s, 0)[:, 256:256 + HEADS].unsqueeze(1).to_broadcast([P, 2, HEADS]), ALU.mult, ALU.add)).then_inc(m.k_arg, 1)
                yield 19.54
                dve.wait_ge(m.ctx_made, both(i, s))
                for half in range(2):
                    r = bass.ts(half, HEAD)
                    made = c.PS[r, 4 * s + 2:4 * s + 4, 0:260].rearrange("p b (c h d) -> p b c h d", c=2, h=2)[:, :, :, half, :]
                    last = nc.vector.tensor_copy(ctx_sb[s][r, :, half, :].rearrange("p (b c) d -> p b c d", c=2), made)
                last.then_inc(m.ctx_kept, 1)
                yield 21.06
                dve.wait_ge(m.qd_made, both(i, s))
                nc.vector.tensor_reduce(top[s][:, :], banks(s, 2, 2).rearrange("p t (h d) -> p (t h) d", d=HEAD), AX, ALU.max)
                dve.wait_ge(m.q_squared, both(i, s))
                exponent(s, lambda: nc.vector.scalar_tensor_tensor(
                    shift[s][:, :], power[s][:, :], DIAG, top[s][:, :], ALU.mult, ALU.add)).then_inc(m.q_arg, 1)

            def second(i, s):
                yield 6.39
                dve.wait_ge(m.q_featT, both(i, s))
                nc.vector.tensor_scalar(featT[s][:, :, :], banks(s, 0, 2).rearrange("p b (c n) -> p (b c) n", n=256),
                                        KERNEL_EPS, None, ALU.add).then_inc(m.q_featT_kept, 1)
                yield 8.99
                dve.wait_ge(m.weighed, both(i, s))
                made = banks(s, 0, 4)[:, :, 0:260].rearrange("p b (h d) -> p b h d", h=4)
                nc.vector.reciprocal(share[s][:, :].rearrange("p (b h) -> p b h", h=4), made[:, :, :, HEAD])
                dve.drain()
                nc.vector.tensor_tensor(attn[s][:, :].rearrange("p (b h d) -> p b h d", b=4, h=4), made[:, :, :, 0:HEAD],
                                        share[s][:, :].rearrange("p (b h) -> p b h", h=4).unsqueeze(3).to_broadcast([P, 4, 4, HEAD]),
                                        ALU.mult).then_inc(m.attn_kept, 1)
                yield 14.22
                dve.wait_ge(m.o_made, both(i, s))
                dve.wait_ge(m.xb_ready, both(i, s))
                nc.vector.tensor_tensor(x2[s][:, :, :], bank(s, 2)[:, 0:256].rearrange("p (t d) -> p t d", t=2), xb[s][:, :, :], ALU.add)
                dve.drain()
                norm_stats(nc, dve, norm[s], x2[s])
                norm[s].last.then_inc(m.x2_stats, 1)
                yield 19.52
                dve.wait_ge(m.x2_rstd, both(i, s))
                norm_apply(nc, norm[s], x2[s], lambda t: xn[s][:, t, :])
                norm[s].last.then_inc(m.x2n_ready, 1)
                yield 19.54
                dve.wait_ge(m.x2nT, both(i, s))
                nc.vector.tensor_scalar(hT[s][:, :], bank(s, 3)[:, 0:256], 1.0, None, ALU.add).then_inc(m.h2T_ready, 1)
                yield 26.37
                dve.wait_ge(m.y_made, both(i, s))
                dve.wait_ge(m.x2b_ready, both(i, s))
                nc.vector.tensor_tensor(c.X[:, bass.ds((i + s) * 2, 2), :], bank(s, 2)[:, 0:256].rearrange("p (t d) -> p t d", t=2),
                                        xb[s][:, :, :], ALU.add).then_inc(m.done, 1)

            skewed(dve, first, second)


def expert_buffers(nc, c, ctx, which):
    sb = lambda n, shape, dt=F32: ctx.enter_context(nc.sbuf_tensor(f"{n}_{which}", shape, dt))
    c.w1 = sb("expert_w1", [P, EXPERTS, WIDE])
    c.w2 = sb("expert_w2", [P, EXPERTS, BLOCKS, P])
    c.b2 = sb("expert_b2", [P, EXPERTS, P])
    c.gate = sb("gate", [P, EXPERTS])


def load_experts(nc, c, sp, ins, which, prefix):
    landed = c.weights_landed[which]
    sp.dma_start(c.w1[:, :, :], ins[f"{prefix}_W1"].rearrange("e p f -> p e f")).then_inc(landed, 16)
    for e in range(EXPERTS):
        sp.dma_start(c.w2[:, e, :, :], ins[f"{prefix}_W2"][e].rearrange("(b p) d -> p b d", p=P)).then_inc(landed, 16)
    sp.dma_start(c.b2[:, :, :].rearrange("p e d -> p (e d)"), broadcast_rows(ins[f"{prefix}_b2"], EXPERTS * P)).then_inc(landed, 16)


EXPERT_LOADS = 16 * (EXPERTS + 2)


def prepare_experts(nc, c, ins, which, prefix, gate_w, gate_b, norm=None):
    with ExitStack() as ctx:
        sb = lambda n, shape: ctx.enter_context(nc.sbuf_tensor(f"prepare_{prefix}_{n}", shape, F32))
        loaded = signals(nc, ctx)(f"prepare_{prefix}_loaded")
        b1 = sb("b1", [P, EXPERTS * WIDE])
        gate_bias = sb("gate_bias", [P, EXPERTS])
        columns = sb("columns", [P, 2])
        norm_bias = sb("norm_bias", [P, P])
        count = 16 * (3 + (2 if norm else 0))
        with nc.Block() as block:
            @block.sync
            def _(sp):
                load_experts(nc, c, sp, ins, which, prefix)
                sp.dma_start(b1[:, :], broadcast_rows(ins[f"{prefix}_b1"], EXPERTS * WIDE)).then_inc(loaded, 16)
                sp.dma_start(c.gate[:, :], ins[gate_w]).then_inc(loaded, 16)
                sp.dma_start(gate_bias[:, :], broadcast_rows(ins[gate_b], EXPERTS)).then_inc(loaded, 16)
                if norm:
                    for k, name in enumerate(norm):
                        sp.dma_start(columns[:, k:k + 1], ins[name].rearrange("(p o) -> p o", o=1)).then_inc(loaded, 16)
                sp.wait_ge(loaded, count)
                sp.wait_ge(c.weights_landed[which], EXPERT_LOADS)

            if norm:
                @block.vector
                def _(dve):
                    dve.wait_ge(loaded, count)
                    nc.vector.tensor_copy(norm_bias[:, :], columns[:, 1:2].to_broadcast([P, P]))
                    dve.drain()
        scale = columns[:, 0:1] if norm else None
        bias = norm_bias[:, :] if norm else None
        fold_norm(nc, c, ctx, prefix,
                  [(c.gate[:, :], scale, bias, gate_bias[:, :])]
                  + [(c.w1[:, e, :], scale, bias, b1[:, bass.ts(e, WIDE)]) for e in range(EXPERTS)],
                  loaded, count)


def gate(nc, c, name, add):
    with ExitStack() as ctx:
        sb = lambda n, shape: [ctx.enter_context(nc.sbuf_tensor(f"{name}_{n}_{s}", shape, F32)) for s in range(2)]
        take = signals(nc, ctx)
        sem = lambda n: take(f"{name}_{n}")
        rows = sb("rows", [P, SEQ_TILES, P])
        xn = sb("xn", [P, SEQ_TILES, P])
        hT = sb("hT", [P, SEQ_TILES * P])
        norm = [NormBuffers(nc, ctx, f"{name}_norm_{s}") for s in range(2)]
        stats, rstd, ready, turned, turned_kept, made, kept, copied = (
            sem(n) for n in ("stats", "rstd", "ready", "turned", "turned_kept", "made", "kept", "copied"))
        block = ctx.enter_context(nc.Block())

        @block.vector
        def _(dve):
            with dve.Fori(0, SEQS - 1, 2) as i:
                for s in range(2):
                    here = bass.ds((i + s) * 2, 2)
                    if add:
                        nc.vector.tensor_tensor(rows[s][:, :, :], c.H[:, here, :], c.X[:, here, :], ALU.add)
                        dve.drain()
                        nc.vector.tensor_copy(c.H[:, here, :], rows[s][:, :, :])
                    else:
                        nc.vector.tensor_copy(rows[s][:, :, :], c.X[:, here, :])
                        dve.drain()
                    norm_stats(nc, dve, norm[s], rows[s])
                    norm[s].last.then_inc(stats, 1)
                for s in range(2):
                    dve.wait_ge(rstd, both(i, s))
                    norm_apply(nc, norm[s], rows[s], lambda t: xn[s][:, t, :])
                    norm[s].last.then_inc(ready, 1)
                for s in range(2):
                    dve.wait_ge(turned, both(i, s))
                    nc.vector.tensor_scalar(hT[s][:, :], c.PS[:, s, 0:256], 1.0, None, ALU.add).then_inc(turned_kept, 1)
                for s in range(2):
                    dve.wait_ge(made, both(i, s))
                    nc.vector.tensor_copy(c.logits[:, bass.ds((i + s) * 2, 2), :],
                                          c.PS[:, 2 + s, 0:16].rearrange("p (t e) -> p t e", t=2)).then_inc(kept, 1)
                dve.drain()
                for s in range(2):
                    dve.wait_ge(copied, both(i, s))

        @block.gpsimd
        def _(pool):
            with pool.Fori(0, SEQS - 1, 2) as i:
                for s in range(2):
                    pool.wait_ge(stats, both(i, s))
                    norm_rstd(nc, pool, c, norm[s])
                    norm[s].last.then_inc(rstd, 1)

        @block.scalar
        def _(act):
            with act.Fori(0, SEQS - 1, 2) as i:
                for s in range(2):
                    act.wait_ge(ready, both(i, s))
                    nc.scalar.activation(c.X[:, bass.ds((i + s) * 2, 2), :], xn[s][:, :, :], ACT.Copy).then_inc(copied, 1)

        @block.tensor
        def _(pe):
            with pe.Fori(0, SEQS - 1, 2) as i:
                for s in range(2):
                    pe.wait_ge(ready, both(i, s))
                    for t in range(2):
                        last = nc.tensor.transpose(c.PS[:, s, bass.ts(t, P)], xn[s][:, t, :], c.ident[:, :])
                    last.then_inc(turned, 1)
                for s in range(2):
                    pe.wait_ge(turned_kept, both(i, s))
                    for t in range(2):
                        last = nc.tensor.matmul(c.PS[:, 2 + s, bass.ts(t, EXPERTS)], hT[s][:, bass.ts(t, P)], c.gate[:, :],
                                                start=True, stop=True)
                    last.then_inc(made, 1)


def route(nc, c, name):
    T = TILES
    with ExitStack() as ctx:
        sb = lambda n, shape, dt=F32: ctx.enter_context(nc.sbuf_tensor(f"{name}_{n}", shape, dt))
        take = signals(nc, ctx)
        sem = lambda n: take(f"{name}_{n}")
        largest = sb("largest", [P, T])
        first = sb("first", [P, T])
        total = sb("total", [P, T])
        chosen = sb("chosen", [P, T, EXPERTS])
        work = sb("work", [P, T, EXPERTS])
        exps = sb("exps", [P, T, EXPERTS])
        before = [sb(f"before_{n}", [P, T, EXPERTS]) for n in range(2)]
        count = sb("count", [P, EXPERTS])
        count_int = sb("count_int", [P, EXPERTS], I32)
        start = sb("start", [P, EXPERTS + 1])
        passed = sb("passed", [1, SORTED, EXPERTS])
        number = sb("number", [1, SORTED])
        shifted, expd, one_hot, counted, routed, sent = (sem(n) for n in ("shifted", "expd", "one_hot", "counted", "routed", "sent"))
        wide = lambda a: a.unsqueeze(2).to_broadcast([P, T, EXPERTS])
        block = ctx.enter_context(nc.Block())

        @block.scalar
        def _(act):
            act.wait_ge(shifted, 1)
            nc.scalar.activation(exps[:, :, :], exps[:, :, :], ACT.Exp).then_inc(expd, 1)

        @block.tensor
        def _(pe):
            pe.wait_ge(one_hot, 1)
            flat = chosen[:, :, :].rearrange("p t e -> p (t e)")
            n = T * EXPERTS
            nc.tensor.matmul(c.PS[:, 0, 0:n], c.before[:, :], flat, start=True, stop=True)
            nc.tensor.matmul(c.PS[:, 1, 0:n], c.minus_ones[:, :], flat, start=True, stop=True).then_inc(counted, 1)

        @block.vector
        def _(dve):
            v = nc.vector
            v.tensor_reduce(largest[:, :], c.logits[:, 0:T, :], AX, ALU.max)
            dve.drain()
            v.tensor_tensor(exps[:, :, :], c.logits[:, 0:T, :], wide(largest[:, :]), ALU.subtract).then_inc(shifted, 1)
            v.tensor_tensor(chosen[:, :, :], c.logits[:, 0:T, :], wide(largest[:, :]), ALU.is_equal)
            dve.drain()
            v.tensor_tensor(work[:, :, :], chosen[:, :, :], c.experts[:, :].unsqueeze(1).to_broadcast([P, T, EXPERTS]), ALU.mult)
            dve.drain()
            v.tensor_reduce(first[:, :], work[:, :, :], AX, ALU.min)
            dve.drain()
            v.tensor_tensor(chosen[:, :, :], wide(first[:, :]), c.experts[:, :].unsqueeze(1).to_broadcast([P, T, EXPERTS]),
                            ALU.is_equal).then_inc(one_hot, 1)
            dve.wait_ge(expd, 1)
            v.tensor_reduce(total[:, :], exps[:, :, :], AX, ALU.add)
            dve.drain()
            v.reciprocal(c.weight[:, 0:T], total[:, :])
            dve.wait_ge(counted, 1)
            v.tensor_scalar(before[0][:, :, :], c.PS[:, 1, 0:T * EXPERTS].rearrange("p (t e) -> p t e", e=EXPERTS), -1.0, None, ALU.mult)
            dve.drain()
            k, src = 1, 0
            while k < T:
                a, b = before[src], before[1 - src]
                v.tensor_tensor(b[:, k:, :], a[:, k:, :], a[:, 0:T - k, :], ALU.add)
                v.tensor_copy(b[:, 0:k, :], a[:, 0:k, :])
                dve.drain()
                k, src = 2 * k, 1 - src
            upto = before[src]
            v.tensor_scalar(count[:, :], upto[:, T - 1, :], float(P - 1), None, ALU.add)
            dve.drain()
            v.tensor_copy(count_int[:, :], count[:, :])
            dve.drain()
            v.tensor_scalar(count_int[:, :], count_int[:, :], 7, 7, ALU.arith_shift_right, ALU.arith_shift_left)
            dve.drain()
            v.tensor_copy(count[:, :], count_int[:, :])
            v.memset(start[:, :], 0.0)
            dve.drain()
            for e in range(EXPERTS):
                v.tensor_tensor(start[:, e + 1:e + 2], start[:, e:e + 1], count[:, e:e + 1], ALU.add)
                dve.drain()
            other = before[1 - src]
            v.tensor_tensor(other[:, :, :], upto[:, :, :], c.PS[:, 0, 0:T * EXPERTS].rearrange("p (t e) -> p t e", e=EXPERTS), ALU.add)
            dve.drain()
            v.tensor_tensor(other[:, :, :], other[:, :, :], start[:, 0:EXPERTS].unsqueeze(1).to_broadcast([P, T, EXPERTS]), ALU.add)
            v.tensor_copy(work[:, :, :], c.PS[:, 1, 0:T * EXPERTS].rearrange("p (t e) -> p t e", e=EXPERTS))
            dve.drain()
            v.tensor_tensor(other[:, :, :], other[:, :, :], work[:, :, :], ALU.add)
            dve.drain()
            v.tensor_tensor(other[:, :, :], other[:, :, :], chosen[:, :, :], ALU.mult)
            dve.drain()
            v.tensor_reduce(total[:, :], other[:, :, :], AX, ALU.add)
            dve.drain()
            v.tensor_copy(c.row_of[:, 0:T], total[:, :]).then_inc(routed, 1)
            v.tensor_tensor(passed[:, :, :], start[0:1, 1:EXPERTS + 1].unsqueeze(1).to_broadcast([1, SORTED, EXPERTS]),
                            c.tile_start[:, :].unsqueeze(2).to_broadcast([1, SORTED, EXPERTS]), ALU.is_le)
            dve.drain()
            v.tensor_reduce(number[:, :], passed[:, :, :], AX, ALU.add)
            dve.drain()
            v.tensor_scalar(number[:, :], number[:, :], float(EXPERTS - 1), None, ALU.min)
            dve.drain()
            v.tensor_copy(c.tile_expert[:, :], number[:, :])
            dve.drain()

        @block.gpsimd
        def _(pool):
            pool.wait_ge(routed, 1)
            for t in range(T):
                pool.indirect_dma_start(out=c.sorted_in, out_offset=bass.IndirectOffsetOnAxis(ap=c.row_of[:, t:t + 1], axis=0),
                                        in_=c.X[:, t, :], in_offset=None).then_inc(sent, 16)
            pool.wait_ge(sent, 16 * T)


def experts(nc, c, name, gelu):
    with ExitStack() as ctx:
        sb = lambda n, shape: [ctx.enter_context(nc.sbuf_tensor(f"{name}_{n}_{s}", shape, F32)) for s in range(LANES)]
        take = signals(nc, ctx)
        sem = lambda n: take(f"{name}_{n}")
        xs = sb("xs", [P, P])
        xsT = sb("xsT", [P, P])
        hid = sb("hid", [P, WIDE])
        hidT = sb("hidT", [P, WIDE])
        landed = [sem(f"landed_{s}") for s in range(LANES)]
        turned, turned_kept, made, kept, hidden_turned, hidden_kept, out_made, out_kept, stored = (
            sem(n) for n in ("turned", "turned_kept", "made", "kept", "hidden_turned", "hidden_kept", "out_made", "out_kept", "stored"))
        bank = lambda s, b: c.PS[:, 2 * s + b, :]
        w1 = c.w1[:, :, :].rearrange("p e f -> p (e f)")
        w2 = c.w2[:, :, :, :].rearrange("p e b d -> p (e b d)")
        b2 = c.b2[:, :, :].rearrange("p e d -> p (e d)")
        block = ctx.enter_context(nc.Block())

        @block.sync
        def _(sp):
            for s in range(LANES):
                sp.dma_start(xs[s][:, :], c.sorted_in[s * P:(s + 1) * P, :]).then_inc(landed[s], 16)
            with sp.Fori(0, SORTED - LANES + 1, LANES) as i:
                for s in range(LANES):
                    sp.wait_ge(turned, both(i, s))
                    sp.dma_start(xs[s][:, :], c.sorted_in[bass.ds((i + s + LANES) * P, P), :]).then_inc(landed[s], 16)
                for s in range(LANES):
                    sp.wait_ge(out_kept, both(i, s))
                    sp.dma_start(c.sorted_out[bass.ds((i + s) * P, P), :],
                                 c.X[:, bass.ds(i + s, 1), :].rearrange("p o d -> p (o d)")).then_inc(stored, 16)
            sp.wait_ge(stored, SORTED * 16)
            for s in range(LANES):
                sp.wait_ge(landed[s], (SORTED // LANES + 1) * 16)

        @block.tensor
        def _(pe):
            with pe.Fori(0, SORTED - LANES + 1, LANES) as i:
                for s in range(LANES):
                    pe.wait_ge(landed[s], (i + LANES) * (16 // LANES))
                    nc.tensor.transpose(bank(s, 0)[:, 0:P], xs[s][:, :], c.ident[:, :]).then_inc(turned, 1)
                which = []
                for s in range(LANES):
                    which.append(pe.value_load(c.tile_expert[0:1, bass.ds(i + s, 1)], min_val=0, max_val=EXPERTS - 1))
                    pe.wait_ge(turned_kept, both(i, s))
                    nc.tensor.matmul(bank(s, 1), xsT[s][:, :], w1[:, bass.ds(which[s] * WIDE, WIDE)], start=True, stop=True).then_inc(made, 1)
                for s in range(LANES):
                    pe.wait_ge(kept, both(i, s))
                    for b in range(BLOCKS):
                        last = nc.tensor.transpose(bank(s, 0)[:, bass.ts(b, P)], hid[s][:, bass.ts(b, P)], c.ident[:, :])
                    last.then_inc(hidden_turned, 1)
                for s in range(LANES):
                    pe.wait_ge(hidden_kept, both(i, s))
                    for b in range(BLOCKS):
                        last = nc.tensor.matmul(bank(s, 1)[:, 0:P], hidT[s][:, bass.ts(b, P)],
                                                w2[:, bass.ds(which[s] * WIDE + b * P, P)], start=b == 0, stop=b == BLOCKS - 1)
                    last.then_inc(out_made, 1)

        @block.scalar
        def _(act):
            with act.Fori(0, SORTED - LANES + 1, LANES) as i:
                for s in range(LANES):
                    act.wait_ge(made, both(i, s))
                    nc.scalar.activation(hid[s][:, :], bank(s, 1), gelu).then_inc(kept, 1)

        @block.vector
        def _(dve):
            with dve.Fori(0, SORTED - LANES + 1, LANES) as i:
                for s in range(LANES):
                    dve.wait_ge(turned, both(i, s))
                    nc.vector.tensor_scalar(xsT[s][:, :], bank(s, 0)[:, 0:P], 1.0, None, ALU.add).then_inc(turned_kept, 1)
                which = [dve.value_load(c.tile_expert[0:1, bass.ds(i + s, 1)], min_val=0, max_val=EXPERTS - 1) for s in range(LANES)]
                for s in range(LANES):
                    dve.wait_ge(hidden_turned, both(i, s))
                    nc.vector.tensor_copy(hidT[s][:, :], bank(s, 0)).then_inc(hidden_kept, 1)
                for s in range(LANES):
                    dve.wait_ge(out_made, both(i, s))
                    nc.vector.tensor_tensor(c.X[:, bass.ds(i + s, 1), :].rearrange("p o d -> p (o d)"), bank(s, 1)[:, 0:P],
                                            b2[:, bass.ds(which[s] * P, P)], ALU.add).then_inc(out_kept, 1)


def combine(nc, c, name, out=None):
    with ExitStack() as ctx:
        sb = lambda n, shape, dt=F32: ctx.enter_context(nc.sbuf_tensor(f"{name}_{n}", shape, dt))
        take = signals(nc, ctx)
        sem = lambda n: take(f"{name}_{n}")
        gathered, added, stored = (sem(n) for n in ("gathered", "added", "stored"))
        block = ctx.enter_context(nc.Block())
        T = 2 * SEQS

        @block.gpsimd
        def _(pool):
            for t in range(T):
                pool.indirect_dma_start(out=c.X[:, t, :], out_offset=None, in_=c.sorted_out,
                                        in_offset=bass.IndirectOffsetOnAxis(ap=c.row_of[:, t:t + 1], axis=0)).then_inc(gathered, 16)
            pool.wait_ge(gathered, T * 16)

        @block.vector
        def _(dve):
            dve.wait_ge(gathered, T * 16)
            with dve.Fori(0, T) as t:
                row = lambda a: a[:, bass.ds(t, 1), :].rearrange("p o d -> p (o d)")
                nc.vector.scalar_tensor_tensor(row(c.H), row(c.X), c.weight[:, bass.ds(t, 1)], row(c.H), ALU.mult, ALU.add).then_inc(added, 1)

        @block.sync
        def _(sp):
            if out is not None:
                rows = out.rearrange("b (t p) d -> p (b t) d", p=P)
                with sp.Fori(0, T - 7, 8) as t:
                    sp.wait_ge(added, t + 8)
                    sp.dma_start(rows[:, bass.ds(t, 8), :], c.H[:, bass.ds(t, 8), :]).then_inc(stored, 16)
                sp.wait_ge(stored, T // 8 * 16)


INNER = 256
STATE = 64
DIRS = 2
MHEADS = INNER // HEAD
CONV = 4
MIX = 6
ATANH = [1.0 / (2 * k + 1) for k in range(8, 0, -1)]


def mamba(nc, c, ins):
    with ExitStack() as ctx:
        one = lambda n, shape: ctx.enter_context(nc.sbuf_tensor(f"mamba_{n}", shape, F32))
        sb = lambda n, shape: [one(f"{n}_{s}", shape) for s in range(2)]
        take = signals(nc, ctx)
        sem = lambda n: take(f"mamba_{n}")
        m = Chip()
        m.loaded, m.negated, m.joined, m.stats, m.rstd, m.normed, m.uT = map(sem, (
            "loaded", "negated", "joined", "stats", "rstd", "normed", "uT"))
        m.uT_kept, m.mixed, m.started, m.convolved, m.mixed_kept, m.gated, m.gated_kept = map(sem, (
            "uT_kept", "mixed", "started", "convolved", "mixed_kept", "gated", "gated_kept"))
        m.g_made, m.g_kept, m.dt_raw, m.dt_exp, m.dt_ready, m.steps, m.xT = map(sem, (
            "g_made", "g_kept", "dt_raw", "dt_exp", "dt_ready", "steps", "xT"))
        m.xT_kept, m.bT_kept, m.reach, m.reach_kept, m.ends_kept, m.state, m.state_kept = map(sem, (
            "xT_kept", "bT_kept", "reach", "reach_kept", "ends_kept", "state", "state_kept"))
        m.carried, m.carried_kept, m.span0, m.span0_exp, m.span1, m.span1_exp, m.weights0 = map(sem, (
            "carried", "carried_kept", "span0", "span0_exp", "span1", "span1_exp", "weights0"))
        m.weights1, m.weights0b, m.weights1b, m.y0, m.y1, m.yz, m.sums = map(sem, (
            "weights1", "weights0b", "weights1b", "y0", "y1", "yz", "sums"))
        m.y_rstd, m.yzT, m.yzT_kept, m.projected, m.done = map(sem, (
            "y_rstd", "yzT", "yzT_kept", "projected", "done"))
        w_in = one("w_in", [P, MIX * P + 2 * INNER + 2 * MHEADS])
        w_mix = w_in[:, 0:MIX * P]
        w_z = w_in[:, MIX * P:MIX * P + 2 * INNER]
        w_dt = w_in[:, MIX * P + 2 * INNER:]
        taps = one("taps", [P, MIX, CONV])
        tap_bias = one("tap_bias", [P, MIX])
        columns = one("columns", [P, 9])
        dt_bias = one("dt_bias", [P, 2 * MHEADS])
        decay = one("decay", [P, 2 * MHEADS])
        skip = one("skip", [P, 4, P])
        out_w = one("out_w", [P, 4 * P])
        projT = one("projT", [P, 2 * P])
        w_out = one("w_out", [P, 4, P])
        inv = one("inv", [P, 2])
        masks = one("masks", [P, 4, P])
        before, after, upto, since = (masks[:, k, :] for k in range(4))
        x1 = sb("x1", [P, SEQ_TILES, P])
        u = sb("u", [P, SEQ_TILES, P])
        uT = sb("uT", [P, SEQ_TILES * P])
        mix = sb("mix", [P, MIX, SEQ_TILES * P])
        z = sb("z", [P, SEQ_TILES, DIRS * INNER])
        g = sb("g", [P, SEQ_TILES, DIRS, P])
        dtx = sb("dtx", [P, SEQ_TILES, DIRS * INNER])
        dtxe = sb("dtxe", [P, DIRS, INNER])
        bT = sb("bT", [P, DIRS, P])
        steps = sb("steps", [P, SEQ_TILES, DIRS, MHEADS * P])
        weights = sb("weights", [P, DIRS, MHEADS * P])
        reach = sb("reach", [P, 4, MHEADS])
        state = sb("state", [P, INNER])
        carried = sb("carried", [P, DIRS, INNER])
        yz = sb("yz", [P, SEQ_TILES, DIRS * INNER])
        yzT = sb("yzT", [P, SEQ_TILES, 4, P])
        junk = sb("junk", [P, INNER])
        sums = sb("sums", [P, SEQ_TILES * DIRS])
        rnorm = sb("rnorm", [P, SEQ_TILES])
        norm = [NormBuffers(nc, ctx, f"mamba_norm_{s}") for s in range(2)]
        n_dt = 2 * SEQ_TILES * 2 * MHEADS
        dt_raw, dt_neg, dt_exp, dt_rec, dt_z, dt_z2, dt_p, dt, step_log = (one(n, [P, n_dt]) for n in (
            "dt_raw", "dt_neg", "dt_exp", "dt_rec", "dt_z", "dt_z2", "dt_p", "dt", "step_log"))
        dt_of = lambda a, s: a[:, s * 16:(s + 1) * 16].rearrange("p (t d h) -> p t d h", t=2, d=2)
        part = lambda s: bass.ts(s, 16)
        bank = lambda s, b: c.PS[:, 4 * s + b, :]
        banks = lambda s, b, n: c.PS[:, 4 * s + b:4 * s + b + n, :]
        EYE = c.ident

        with nc.Block() as block:
            loads = [(w_in[:, :], "m_w_in"), (taps[:, :, :], "m_taps"), (tap_bias[:, :], "m_tap_bias"), (columns[:, :], "m_columns"),
                     (out_w[:, :], "m_out_w"), (projT[:, :], "m_projT"), (masks[:, :, :], "m_masks")]

            @block.sync
            def _(sp):
                for at, name in loads:
                    sp.dma_start(at, ins[name]).then_inc(m.loaded, 16)
                sp.dma_start(dt_bias[:, :], broadcast_rows(ins["m_dt_bias"], 8)).then_inc(m.loaded, 16)
                sp.dma_start(decay[:, :], broadcast_rows(ins["m_A_log"], 8)).then_inc(m.loaded, 16)
                sp.wait_ge(m.loaded, 9 * 16)

            @block.scalar
            def _(act):
                act.wait_ge(m.loaded, 9 * 16)
                nc.scalar.activation(decay[:, :], decay[:, :], ACT.Exp).then_inc(m.negated, 1)

            @block.tensor
            def _(pe):
                pe.wait_ge(m.loaded, 9 * 16)
                for b in range(4):
                    last = nc.tensor.matmul(c.PS[:, 0, bass.ts(b, P)], out_w[:, bass.ts(b, P)], projT[:, bass.ts(b // 2, P)], start=True, stop=True)
                last.then_inc(m.joined, 1)

            @block.vector
            def _(dve):
                dve.wait_ge(m.loaded, 9 * 16)
                nc.vector.tensor_scalar(w_in[:, :], w_in[:, :], columns[:, 0:1], None, ALU.mult)
                for b in range(4):
                    nc.vector.tensor_scalar(skip[:, b, :], EYE[:, :], columns[:, 1 + b:2 + b], None, ALU.mult)
                nc.vector.memset(inv[:, :], 1.0 / INNER)
                dve.wait_ge(m.negated, 1)
                nc.vector.tensor_scalar(decay[:, :], decay[:, :], -1.0, None, ALU.mult)
                dve.wait_ge(m.joined, 1)
                for b in range(4):
                    nc.vector.tensor_scalar(w_out[:, b, :], c.PS[:, 0, bass.ts(b, P)], columns[:, 5 + b:6 + b], None, ALU.mult)
                dve.drain()

        block = ctx.enter_context(nc.Block())

        @block.tensor
        def _(pe):
            mm = nc.tensor.matmul

            def spans(s, t):
                for d in range(2):
                    last = mm(bank(s, 3 * d), (after, before)[d], steps[s][:, t, d, :], start=True, stop=True)
                return last

            def outputs(s, t):
                for b in range(4):
                    out = bank(s, 1 + t)[:, bass.ts(b, P)]
                    mm(out, mix[s][:, b, bass.ts(t, P)], skip[:, b, :], start=True, stop=False)
                    for h in range(2):
                        last = mm(out[:, bass.ts(h, HEAD)], weights[s][:, b // 2, bass.ts(2 * (b % 2) + h, P)],
                                  dtx[s][:, t, b * P + h * HEAD:b * P + (h + 1) * HEAD], start=False, stop=h == 1)
                return last

            with pe.Fori(0, SEQS - 1, 2) as i:
                for s in range(2):
                    pe.wait_ge(m.normed, both(i, s))
                    for t in range(2):
                        last = nc.tensor.transpose(bank(s, 0)[:, bass.ts(t, P)], u[s][:, t, :], EYE[:, :])
                    last.then_inc(m.uT, 1)
                for s in range(2):
                    pe.wait_ge(m.uT_kept, both(i, s))
                    for t in range(2):
                        mm(bank(s, 0)[:, 256 + 8 * t:264 + 8 * t], uT[s][:, bass.ts(t, P)], w_dt, start=True, stop=True)
                    for b in range(MIX):
                        last = mm(bank(s, 1 + b // 2)[:, (b % 2) * 256:(b % 2) * 256 + 256], w_mix[:, bass.ts(b, P)], uT[s][:, :], start=True, stop=True)
                    last.then_inc(m.mixed, 1)
                for s in range(2):
                    pe.wait_ge(m.convolved, both(i, s))
                    for t in range(2):
                        last = mm(bank(s, 1 + t), uT[s][:, bass.ts(t, P)], w_z, start=True, stop=True)
                    last.then_inc(m.gated, 1)
                for s in range(2):
                    pe.wait_ge(m.mixed_kept, both(i, s))
                    pe.wait_ge(m.dt_raw, both(i, s))
                    for t in range(2):
                        for d in range(2):
                            r = bass.ts(d, STATE)
                            last = mm(bank(s, 3 - 3 * d)[:, bass.ts(t, P)], mix[s][r, 4, bass.ts(t, P)], mix[s][r, 5, bass.ts(t, P)], start=True, stop=True)
                    last.then_inc(m.g_made, 1)
                for s in range(2):
                    pe.wait_ge(m.gated_kept, both(i, s))
                    pe.wait_ge(m.g_kept, both(i, s))
                    for t in range(2):
                        nc.tensor.transpose(bank(s, 3)[:, bass.ts(t, P)], mix[s][:, 4, bass.ts(t, P)], EYE[:, :])
                    for t in range(2):
                        for b in range(4):
                            last = nc.tensor.transpose(bank(s, 1 + t)[:, bass.ts(b, P)], mix[s][:, b, bass.ts(t, P)], EYE[:, :])
                    last.then_inc(m.xT, 1)
                for s in range(2):
                    pe.wait_ge(m.dt_ready, both(i, s))
                    a = dt_of(step_log, s)
                    for k, (mask, t, d) in enumerate(((upto, 1, 0), (since, 0, 1), (after, 0, 0), (before, 1, 1))):
                        last = mm(bank(s, 0)[:, bass.ts(k, MHEADS)], mask, a[:, t, d, :], start=True, stop=True)
                    last.then_inc(m.reach, 1)
                for s in range(2):
                    pe.wait_ge(m.ends_kept, both(i, s))
                    pe.wait_ge(m.bT_kept, both(i, s))
                    for d in range(2):
                        last = mm(c.PS[bass.ts(d, STATE), 4 * s + 3, 0:INNER], bT[s][:, d, bass.ts(d, STATE)], dtxe[s][:, d, :], start=True, stop=True)
                    last.then_inc(m.state, 1)
                for s in range(2):
                    pe.wait_ge(m.state_kept, both(i, s))
                    for d in range(2):
                        r = bass.ts(d, STATE)
                        last = mm(bank(s, 3 * d)[:, 0:INNER], mix[s][r, 5, bass.ts(1 - d, P)], state[s][r, :], start=True, stop=True)
                    last.then_inc(m.carried, 1)
                for s in range(2):
                    pe.wait_ge(m.steps, both(i, s))
                    pe.wait_ge(m.carried_kept, both(i, s))
                    pe.wait_ge(m.reach_kept, both(i, s))
                    spans(s, 0).then_inc(m.span0, 1)
                for s in range(2):
                    pe.wait_ge(m.weights0, both(i, s))
                    pe.wait_ge(m.weights0b, both(i, s))
                    pe.wait_ge(m.xT_kept, both(i, s))
                    outputs(s, 0).then_inc(m.y0, 1)
                for s in range(2):
                    pe.wait_ge(m.span0_exp, both(i, s))
                    spans(s, 1).then_inc(m.span1, 1)
                for s in range(2):
                    pe.wait_ge(m.weights1, both(i, s))
                    pe.wait_ge(m.weights1b, both(i, s))
                    outputs(s, 1).then_inc(m.y1, 1)
                for s in range(2):
                    pe.wait_ge(m.yz, both(i, s))
                    for t in range(2):
                        for b in range(4):
                            last = nc.tensor.transpose(bank(s, 1 + t)[:, bass.ts(b, P)], yz[s][:, t, bass.ts(b, P)], EYE[:, :])
                    last.then_inc(m.yzT, 1)
                for s in range(2):
                    pe.wait_ge(m.yzT_kept, both(i, s))
                    for t in range(2):
                        for d in range(2):
                            for b in range(2):
                                last = mm(bank(s, 3)[:, bass.ts(2 * t + d, P)], yzT[s][:, t, 2 * d + b, :], w_out[:, 2 * d + b, :], start=b == 0, stop=b == 1)
                    last.then_inc(m.projected, 1)

        @block.scalar
        def _(act):
            a = nc.scalar.activation
            with act.Fori(0, SEQS - 1, 2) as i:
                for s in range(2):
                    act.wait_ge(m.mixed, both(i, s))
                    for b in range(MIX):
                        last = a(mix[s][:, b, :], bank(s, 1 + b // 2)[:, (b % 2) * 256:(b % 2) * 256 + 256], ACT.Identity,
                                 bias=tap_bias[:, b:b + 1], scale=taps[:, b, CONV - 1:CONV])
                    last.then_inc(m.started, 1)
                for s in range(2):
                    act.wait_ge(m.convolved, both(i, s))
                    a(mix[s][:, :, :], mix[s][:, :, :], ACT.Silu).then_inc(m.mixed_kept, 1)
                for s in range(2):
                    act.wait_ge(m.gated, both(i, s))
                    a(z[s][:, :, :], banks(s, 1, 2), ACT.Silu).then_inc(m.gated_kept, 1)
                for s in range(2):
                    act.wait_ge(m.dt_raw, both(i, s))
                    a(dt_exp[:, part(s)], dt_neg[:, part(s)], ACT.Exp).then_inc(m.dt_exp, 1)
                for s in range(2):
                    act.wait_ge(m.reach, both(i, s))
                    a(reach[s][:, :, :], bank(s, 0)[:, 0:16].rearrange("p (k h) -> p k h", h=MHEADS), ACT.Exp).then_inc(m.reach_kept, 1)
                for s in range(2):
                    act.wait_ge(m.state, both(i, s))
                    a(state[s][:, :], bank(s, 3)[:, 0:INNER], ACT.Copy).then_inc(m.state_kept, 1)
                for s in range(2):
                    act.wait_ge(m.span0, both(i, s))
                    for d in range(2):
                        last = a(weights[s][:, d, :], bank(s, 3 * d), ACT.Exp)
                    last.then_inc(m.span0_exp, 1)
                for s in range(2):
                    act.wait_ge(m.span1, both(i, s))
                    act.wait_ge(m.y0, both(i, s))
                    for d in range(2):
                        last = a(weights[s][:, d, :], bank(s, 3 * d), ACT.Exp)
                    last.then_inc(m.span1_exp, 1)
                for s in range(2):
                    act.wait_ge(m.yz, both(i, s))
                    for t in range(2):
                        for d in range(2):
                            k = 2 * t + d
                            a(junk[s][:, :], yz[s][:, t, bass.ts(d, INNER)], ACT.Square, accum_out=sums[s][:, k:k + 1])
                            act.drain()
                    a(sums[s][:, :], sums[s][:, :], ACT.Copy).then_inc(m.sums, 1)
                for s in range(2):
                    act.wait_ge(m.yzT, both(i, s))
                    a(yzT[s][:, :, :, :].rearrange("p t b n -> p t (b n)"), banks(s, 1, 2), ACT.Copy).then_inc(m.yzT_kept, 1)

        @block.gpsimd
        def _(pool):
            tt = nc.gpsimd.tensor_tensor
            with pool.Fori(0, SEQS - 1, 2) as i:
                for s in range(2):
                    pool.wait_ge(m.stats, both(i, s))
                    norm_rstd(nc, pool, c, norm[s])
                    pool.drain()
                    r, q = norm[s].rstd[:, :], rnorm[s][:, :]
                    tt(q, norm[s].stat[:, :, 1], r, ALU.mult)
                    pool.drain()
                    tt(q, q, r, ALU.mult)
                    pool.drain()
                    tt(q, q, c.eps[:, 0:2], ALU.add)
                    pool.drain()
                    tt(q, q, c.minus_half[:, 0:2], ALU.pow)
                    pool.drain()
                    tt(q, q, r, ALU.mult).then_inc(m.rstd, 1)
                for s in range(2):
                    pool.wait_ge(m.dt_ready, both(i, s))
                    for t in range(2):
                        for d in range(2):
                            last = tt(steps[s][:, t, d, :].rearrange("p (h n) -> p h n", h=MHEADS),
                                      (upto, since)[d].unsqueeze(1).to_broadcast([P, MHEADS, P]),
                                      dt_of(step_log, s)[:, t, d, :].unsqueeze(2).to_broadcast([P, MHEADS, P]), ALU.mult)
                    last.then_inc(m.steps, 1)
                for s in range(2):
                    pool.wait_ge(m.span0_exp, both(i, s))
                    w = weights[s][:, 1, :].rearrange("p (h n) -> p h n", h=MHEADS)
                    tt(w, w, g[s][:, 0, 1, :].unsqueeze(1).to_broadcast([P, MHEADS, P]), ALU.mult).then_inc(m.weights0b, 1)
                for s in range(2):
                    pool.wait_ge(m.span1_exp, both(i, s))
                    w = weights[s][:, 1, :].rearrange("p (h n) -> p h n", h=MHEADS)
                    tt(w, w, g[s][:, 1, 1, :].unsqueeze(1).to_broadcast([P, MHEADS, P]), ALU.mult).then_inc(m.weights1b, 1)
                for s in range(2):
                    pool.wait_ge(m.sums, both(i, s))
                    q = sums[s][:, :]
                    tt(q, q, inv[:, 0:1].to_broadcast([P, 4]), ALU.mult)
                    pool.drain()
                    tt(q, q, c.eps[:, :], ALU.add)
                    pool.drain()
                    tt(q, q, c.minus_half[:, :], ALU.pow).then_inc(m.y_rstd, 1)

        @block.vector
        def _(dve):
            v = nc.vector
            row = lambda a, t: a[:, bass.ds(t, 1), :].rearrange("p o d -> p (o d)")
            with dve.Fori(0, SEQS - 1, 2) as i:
                for s in range(2):
                    for t in range(2):
                        v.bn_stats(norm[s].sums[:, t, :], row(c.H, (i + s) * 2 + t))
                    dve.drain()
                    for t in range(2):
                        last = v.bn_aggr(norm[s].stat[:, t, :], norm[s].sums[:, t, :])
                    last.then_inc(m.stats, 1)
                for s in range(2):
                    dve.wait_ge(m.rstd, both(i, s))
                    for t in range(2):
                        mean = norm[s].stat[:, t, 0:1]
                        v.tensor_scalar(x1[s][:, t, :], row(c.H, (i + s) * 2 + t), mean, norm[s].rstd[:, t:t + 1], ALU.subtract, ALU.mult)
                        last = v.tensor_scalar(u[s][:, t, :], row(c.H, (i + s) * 2 + t), mean, rnorm[s][:, t:t + 1], ALU.subtract, ALU.mult)
                    last.then_inc(m.normed, 1)
                for s in range(2):
                    dve.wait_ge(m.uT, both(i, s))
                    v.tensor_copy(uT[s][:, :], bank(s, 0)[:, 0:256]).then_inc(m.uT_kept, 1)
                for s in range(2):
                    dve.wait_ge(m.mixed, both(i, s))
                    v.tensor_tensor(dt_raw[:, part(s)].rearrange("p (t n) -> p t n", t=2), bank(s, 0)[:, 256:272].rearrange("p (t n) -> p t n", t=2),
                                    dt_bias[:, :].unsqueeze(1).to_broadcast([P, 2, 8]), ALU.add)
                    dve.drain()
                    v.scalar_tensor_tensor(dt_neg[:, part(s)], dt_raw[:, part(s)], -1.0, dt_raw[:, part(s)], ALU.mult, ALU.min).then_inc(m.dt_raw, 1)
                for s in range(2):
                    dve.wait_ge(m.started, both(i, s))
                    for k in range(1, CONV):
                        for b in range(MIX):
                            src = bank(s, 1 + b // 2)[:, (b % 2) * 256:(b % 2) * 256 + 256]
                            for d, r in (((0, slice(0, P)),) if b < 2 else ((1, slice(0, P)),) if b < 4 else ((0, slice(0, 64)), (1, slice(64, P)))):
                                n = SEQ_TILES * P
                                to, of = (slice(k, n), slice(0, n - k)) if d == 0 else (slice(0, n - k), slice(k, n))
                                last = v.scalar_tensor_tensor(mix[s][r, b, to], src[r, of], taps[r, b, CONV - 1 - k:CONV - k], mix[s][r, b, to], ALU.mult, ALU.add)
                        if k < CONV - 1:
                            dve.drain()
                    last.then_inc(m.convolved, 1)
                for s in range(2):
                    dve.wait_ge(m.dt_exp, both(i, s))
                    v.tensor_scalar(dt_rec[:, part(s)], dt_exp[:, part(s)], 2.0, None, ALU.add)
                    dve.drain()
                    v.reciprocal(dt_rec[:, part(s)], dt_rec[:, part(s)])
                    dve.drain()
                    v.tensor_tensor(dt_z[:, part(s)], dt_exp[:, part(s)], dt_rec[:, part(s)], ALU.mult)
                    dve.drain()
                    v.tensor_tensor(dt_z2[:, part(s)], dt_z[:, part(s)], dt_z[:, part(s)], ALU.mult)
                    dve.drain()
                    v.tensor_scalar(dt_p[:, part(s)], dt_z2[:, part(s)], ATANH[0], None, ALU.mult)
                    for k in ATANH[1:]:
                        dve.drain()
                        v.scalar_tensor_tensor(dt_p[:, part(s)], dt_p[:, part(s)], k, dt_z2[:, part(s)], ALU.add, ALU.mult)
                    dve.drain()
                    v.scalar_tensor_tensor(dt_p[:, part(s)], dt_p[:, part(s)], 1.0, dt_z[:, part(s)], ALU.add, ALU.mult)
                    v.tensor_scalar(dt_raw[:, part(s)], dt_raw[:, part(s)], 0.0, None, ALU.max)
                    dve.drain()
                    v.scalar_tensor_tensor(dt[:, part(s)], dt_p[:, part(s)], 2.0, dt_raw[:, part(s)], ALU.mult, ALU.add)
                    dve.drain()
                    v.tensor_tensor(step_log[:, part(s)].rearrange("p (t n) -> p t n", n=8), dt[:, part(s)].rearrange("p (t n) -> p t n", n=8),
                                    decay[:, :].unsqueeze(1).to_broadcast([P, 2, 8]), ALU.mult).then_inc(m.dt_ready, 1)
                for s in range(2):
                    dve.wait_ge(m.g_made, both(i, s))
                    for d in range(2):
                        last = v.tensor_tensor(g[s][:, :, d, :], bank(s, 3 - 3 * d)[:, 0:256].rearrange("p (t n) -> p t n", t=2),
                                               (upto, since)[d].unsqueeze(1).to_broadcast([P, 2, P]), ALU.mult)
                    last.then_inc(m.g_kept, 1)
                for s in range(2):
                    dve.wait_ge(m.xT, both(i, s))
                    v.tensor_copy(bT[s][:, :, :], bank(s, 3)[:, 0:256].rearrange("p (t n) -> p t n", t=2)).then_inc(m.bT_kept, 1)
                    v.tensor_tensor(dtx[s][:, :, :].rearrange("p t (h d) -> p (t h) d", d=HEAD), banks(s, 1, 2).rearrange("p t (h d) -> p (t h) d", d=HEAD),
                                    dt[:, part(s)].unsqueeze(2).to_broadcast([P, 16, HEAD]), ALU.mult).then_inc(m.xT_kept, 1)
                for s in range(2):
                    dve.drain()
                    dve.wait_ge(m.reach_kept, both(i, s))
                    for d in range(2):
                        last = v.tensor_tensor(dtxe[s][:, d, :].rearrange("p (h d) -> p h d", d=HEAD), dtx[s][:, d, bass.ts(d, INNER)].rearrange("p (h d) -> p h d", d=HEAD),
                                               reach[s][:, 2 + d, :].unsqueeze(2).to_broadcast([P, MHEADS, HEAD]), ALU.mult)
                    last.then_inc(m.ends_kept, 1)
                for s in range(2):
                    dve.wait_ge(m.carried, both(i, s))
                    for d in range(2):
                        last = v.tensor_tensor(carried[s][:, d, :].rearrange("p (h d) -> p h d", d=HEAD), bank(s, 3 * d)[:, 0:INNER].rearrange("p (h d) -> p h d", d=HEAD),
                                               reach[s][:, d, :].unsqueeze(2).to_broadcast([P, MHEADS, HEAD]), ALU.mult)
                    last.then_inc(m.carried_kept, 1)
                for s in range(2):
                    dve.wait_ge(m.span0_exp, both(i, s))
                    w = weights[s][:, 0, :].rearrange("p (h n) -> p h n", h=MHEADS)
                    v.tensor_tensor(w, w, g[s][:, 0, 0, :].unsqueeze(1).to_broadcast([P, MHEADS, P]), ALU.mult).then_inc(m.weights0, 1)
                for s in range(2):
                    dve.wait_ge(m.span1_exp, both(i, s))
                    w = weights[s][:, 0, :].rearrange("p (h n) -> p h n", h=MHEADS)
                    v.tensor_tensor(w, w, g[s][:, 1, 0, :].unsqueeze(1).to_broadcast([P, MHEADS, P]), ALU.mult).then_inc(m.weights1, 1)
                for s in range(2):
                    dve.wait_ge(m.y0, both(i, s))
                    dve.wait_ge(m.y1, both(i, s))
                    for t in range(2):
                        at = bass.ts(1 - t, INNER)
                        v.tensor_tensor(yz[s][:, t, at], bank(s, 1 + t)[:, at], carried[s][:, 1 - t, :], ALU.add)
                        other = bass.ts(t, INNER)
                        v.tensor_tensor(yz[s][:, t, other], bank(s, 1 + t)[:, other], z[s][:, t, other], ALU.mult)
                    dve.drain()
                    for t in range(2):
                        at = bass.ts(1 - t, INNER)
                        last = v.tensor_tensor(yz[s][:, t, at], yz[s][:, t, at], z[s][:, t, at], ALU.mult)
                    last.then_inc(m.yz, 1)
                for s in range(2):
                    dve.wait_ge(m.projected, both(i, s))
                    dve.wait_ge(m.y_rstd, both(i, s))
                    for d in range(2):
                        for t in range(2):
                            k = 2 * t + d
                            v.scalar_tensor_tensor(x1[s][:, t, :], bank(s, 3)[:, bass.ts(k, P)], sums[s][:, k:k + 1], x1[s][:, t, :], ALU.mult, ALU.add)
                        dve.drain()
                    here = bass.ds((i + s) * 2, 2)
                    v.tensor_tensor(c.H[:, here, :], c.H[:, here, :], x1[s][:, :, :], ALU.add).then_inc(m.done, 1)
                dve.drain()


AHEADS, AHEAD = 8, 16
GROUPS = 2
LANE = 32


def attention(nc, c, ins):
    with ExitStack() as ctx:
        one = lambda n, shape: ctx.enter_context(nc.sbuf_tensor(f"attention_{n}", shape, F32))
        sb = lambda n, shape: [one(f"{n}_{s}", shape) for s in range(2)]
        take = signals(nc, ctx)
        sem = lambda n: take(f"attention_{n}")
        m = Chip()
        m.loaded, m.cleared, m.stats, m.rstd, m.normed, m.xT, m.xT_kept = map(sem, (
            "loaded", "cleared", "stats", "rstd", "normed", "xT", "xT_kept"))
        m.qk_made, m.qk_kept, m.k_kept, m.v_made, m.v_kept, m.top_kept0, m.top_kept1 = map(sem, (
            "qk_made", "qk_kept", "k_kept", "v_made", "v_kept", "top_kept0", "top_kept1"))
        m.scored0, m.scored1, m.topT, m.q_shifted, m.summed, m.summed_kept, m.oT = map(sem, (
            "scored0", "scored1", "topT", "q_shifted", "summed", "summed_kept", "oT"))
        m.oT_kept, m.projected, m.xb_ready, m.done = map(sem, (
            "oT_kept", "projected", "xb_ready", "done"))
        spread = [sem(f"spread_{h}") for h in range(AHEADS)]
        exps = [sem(f"exps_{h}") for h in range(AHEADS)]
        w_q = one("w_q", [P, GROUPS * P])
        w_k = one("w_k", [P, GROUPS * P])
        w_v = one("w_v", [P, P])
        w_o = one("w_o", [P, P])
        b_q = one("b_q", [P, GROUPS * P])
        b_k = one("b_k", [P, GROUPS * P])
        b_v = one("b_v", [P, P])
        b_o = one("b_o", [P, P])
        x3 = sb("x3", [P, SEQ_TILES, P])
        xb = sb("xb", [P, SEQ_TILES, P])
        xT = sb("xT", [P, SEQ_TILES * P])
        q = sb("q", [P, GROUPS, SEQ_TILES * P])
        k = sb("k", [P, GROUPS, SEQ_TILES * P])
        v = sb("v", [P, SEQ_TILES, AHEADS, AHEAD + 1])
        top = sb("top", [P, SEQ_TILES, GROUPS, 4, LANE])
        probs = sb("probs", [P, AHEADS, SEQ_TILES, SEQ_TILES * P])
        share = sb("share", [P, SEQ_TILES * AHEADS])
        o = sb("o", [P, SEQ_TILES, P])
        oT = sb("oT", [P, SEQ_TILES * P])
        norm = [NormBuffers(nc, ctx, f"attention_norm_{s}") for s in range(2)]
        bank = lambda s, b: c.PS[:, 4 * s + b, :]
        banks = lambda s, b, n: c.PS[:, 4 * s + b:4 * s + b + n, :]
        EYE = c.ident
        SCALE = AHEAD ** -0.5
        LAG = 2

        with nc.Block() as block:
            lanes = lambda a: a.rearrange("p (h n) -> p h n", n=LANE)[:, :, 0:AHEAD]

            @block.sync
            def _(sp):
                sp.wait_ge(m.cleared, 1)
                for at, name in ((w_q, "Wq"), (w_k, "Wk")):
                    sp.dma_start(lanes(at[:, :]), ins[f"L1_ffn_{name}"].rearrange("p (h n) -> p h n", n=AHEAD)).then_inc(m.loaded, 16)
                for at, name in ((w_v, "Wv"), (w_o, "Wo")):
                    sp.dma_start(at[:, :], ins[f"L1_ffn_{name}"]).then_inc(m.loaded, 16)
                for at, name in ((b_q, "bq"), (b_k, "bk")):
                    a = ins[f"L1_ffn_{name}"]
                    sp.dma_start(lanes(at[:, :]), bass.AP(a.tensor, a.offset, [[0, P], [AHEAD, AHEADS], [1, AHEAD]])).then_inc(m.loaded, 16)
                for at, name in ((b_v, "bv"), (b_o, "bo")):
                    sp.dma_start(at[:, :], broadcast_rows(ins[f"L1_ffn_{name}"], P)).then_inc(m.loaded, 16)
                sp.wait_ge(m.loaded, 8 * 16)

            @block.vector
            def _(dve):
                for a in (w_q, w_k, b_q, b_k):
                    nc.vector.memset(a[:, :], 0.0)
                dve.drain()
                nc.vector.memset(b_k[:, :].rearrange("p (h n) -> p h n", n=LANE)[:, :, AHEAD:AHEAD + 1], 1.0).then_inc(m.cleared, 1)
        with ExitStack() as inner:
            fold_norm(nc, c, inner, "attention",
                      [(w_q[:, :], None, None, b_q[:, :]), (w_k[:, :], None, None, b_k[:, :]), (w_v[:, :], None, None, b_v[:, :])],
                      m.loaded, 8 * 16)

        block = ctx.enter_context(nc.Block())
        lane = lambda j: slice(LANE * j, LANE * j + AHEAD + 1)

        @block.tensor
        def _(pe):
            mm = nc.tensor.matmul
            with pe.Fori(0, SEQS - 1, 2) as i:
                for s in range(2):
                    pe.wait_ge(m.normed, both(i, s))
                    for t in range(2):
                        last = nc.tensor.transpose(bank(s, 0)[:, bass.ts(t, P)], x3[s][:, t, :], EYE[:, :])
                    last.then_inc(m.xT, 1)
                for s in range(2):
                    pe.wait_ge(m.xT_kept, both(i, s))
                    for g in range(GROUPS):
                        mm(bank(s, 1)[:, g * 256:(g + 1) * 256], w_q[:, bass.ts(g, P)], xT[s][:, :], start=True, stop=True)
                        last = mm(bank(s, 2)[:, g * 256:(g + 1) * 256], w_k[:, bass.ts(g, P)], xT[s][:, :], start=True, stop=True)
                    last.then_inc(m.qk_made, 1)
                    for t in range(2):
                        last = mm(bank(s, 3)[:, bass.ts(t, P)], xT[s][:, bass.ts(t, P)], w_v[:, :], start=True, stop=True)
                    last.then_inc(m.v_made, 1)
                for g in range(GROUPS):
                    for s in range(2):
                        if g == 0:
                            pe.wait_ge(m.qk_kept, both(i, s))
                            pe.wait_ge(m.k_kept, both(i, s))
                            pe.wait_ge(m.v_kept, both(i, s))
                        else:
                            pe.wait_ge(m.top_kept0, both(i, s))
                        for t in range(2):
                            for j in range(4):
                                last = mm(bank(s, j)[:, t * 256:(t + 1) * 256], q[s][lane(j), g, bass.ts(t, P)], k[s][lane(j), g, :], start=True, stop=True)
                        last.then_inc((m.scored0, m.scored1)[g], 1)
                for s in range(2):
                    pe.wait_ge(m.top_kept1, both(i, s))
                    for g in range(GROUPS):
                        for t in range(2):
                            last = nc.tensor.transpose(bank(s, 0)[:, (2 * g + t) * P:(2 * g + t + 1) * P],
                                                       top[s][:, t, g, :, :].rearrange("p j n -> p (j n)"), EYE[:, :])
                    last.then_inc(m.topT, 1)
                for h in range(AHEADS + LAG):
                    if h < AHEADS:
                        g, j = divmod(h, 4)
                        for s in range(2):
                            if h == 0:
                                pe.wait_ge(m.q_shifted, both(i, s))
                            if h >= 3:
                                pe.wait_ge(exps[h - 3], both(i, s))
                            for t in range(2):
                                last = mm(bank(s, h % 3)[:, t * 256:(t + 1) * 256], k[s][lane(j), g, bass.ts(t, P)], q[s][lane(j), g, :], start=True, stop=True)
                            last.then_inc(spread[h], 1)
                    if h >= LAG:
                        for s in range(2):
                            pe.wait_ge(exps[h - LAG], both(i, s))
                            for t in range(2):
                                at = (t * AHEADS + h - LAG) * (AHEAD + 1)
                                for n in range(2):
                                    last = mm(bank(s, 3)[:, at:at + AHEAD + 1], probs[s][:, h - LAG, n, bass.ts(t, P)], v[s][:, n, h - LAG, :], start=n == 0, stop=n == 1)
                            if h == AHEADS + LAG - 1:
                                last.then_inc(m.summed, 1)
                for s in range(2):
                    pe.wait_ge(m.summed_kept, both(i, s))
                    for t in range(2):
                        last = nc.tensor.transpose(bank(s, 0)[:, bass.ts(t, P)], o[s][:, t, :], EYE[:, :])
                    last.then_inc(m.oT, 1)
                for s in range(2):
                    pe.wait_ge(m.oT_kept, both(i, s))
                    for t in range(2):
                        last = mm(bank(s, 1)[:, bass.ts(t, P)], oT[s][:, bass.ts(t, P)], w_o[:, :], start=True, stop=True)
                    last.then_inc(m.projected, 1)

        @block.scalar
        def _(act):
            a = nc.scalar.activation
            with act.Fori(0, SEQS - 1, 2) as i:
                for s in range(2):
                    act.wait_ge(m.qk_made, both(i, s))
                    a(k[s][:, :, :], bank(s, 2).rearrange("p (g n) -> p g n", g=2), ACT.Copy).then_inc(m.k_kept, 1)
                for h in range(AHEADS):
                    for s in range(2):
                        act.wait_ge(spread[h], both(i, s))
                        a(probs[s][:, h, :, :], bank(s, h % 3).rearrange("p (t n) -> p t n", t=2), ACT.Exp, scale=SCALE).then_inc(exps[h], 1)

        @block.gpsimd
        def _(pool):
            with pool.Fori(0, SEQS - 1, 2) as i:
                for s in range(2):
                    pool.wait_ge(m.stats, both(i, s))
                    norm_rstd(nc, pool, c, norm[s])
                    norm[s].last.then_inc(m.rstd, 1)
                for s in range(2):
                    pool.wait_ge(m.normed, both(i, s))
                    nc.gpsimd.tensor_tensor(xb[s][:, :, :], x3[s][:, :, :], b_o[:, :].unsqueeze(1).to_broadcast([P, 2, P]), ALU.add).then_inc(m.xb_ready, 1)

        @block.vector
        def _(dve):
            vv = nc.vector
            for s in range(2):
                vv.memset(v[s][:, :, :, AHEAD:AHEAD + 1], 1.0)
                vv.memset(top[s][:, :, :, :, :], 0.0)
            dve.drain()
            row = lambda a, t: a[:, bass.ds(t, 1), :].rearrange("p o d -> p (o d)")
            with dve.Fori(0, SEQS - 1, 2) as i:
                for s in range(2):
                    for t in range(2):
                        vv.bn_stats(norm[s].sums[:, t, :], row(c.H, (i + s) * 2 + t))
                    dve.drain()
                    for t in range(2):
                        last = vv.bn_aggr(norm[s].stat[:, t, :], norm[s].sums[:, t, :])
                    last.then_inc(m.stats, 1)
                for s in range(2):
                    dve.wait_ge(m.rstd, both(i, s))
                    for t in range(2):
                        last = vv.tensor_scalar(x3[s][:, t, :], row(c.H, (i + s) * 2 + t), norm[s].stat[:, t, 0:1], norm[s].rstd[:, t:t + 1],
                                                ALU.subtract, ALU.mult)
                    last.then_inc(m.normed, 1)
                for s in range(2):
                    dve.wait_ge(m.xT, both(i, s))
                    vv.tensor_scalar(xT[s][:, :], bank(s, 0)[:, 0:256], 1.0, None, ALU.add).then_inc(m.xT_kept, 1)
                for s in range(2):
                    dve.wait_ge(m.qk_made, both(i, s))
                    vv.tensor_copy(q[s][:, :, :], bank(s, 1).rearrange("p (g n) -> p g n", g=2)).then_inc(m.qk_kept, 1)
                    dve.wait_ge(m.v_made, both(i, s))
                    vv.tensor_copy(v[s][:, :, :, 0:AHEAD].rearrange("p t h d -> p (t h) d"),
                                   bank(s, 3)[:, 0:256].rearrange("p (g d) -> p g d", d=AHEAD)).then_inc(m.v_kept, 1)
                for g in range(GROUPS):
                    for s in range(2):
                        dve.wait_ge((m.scored0, m.scored1)[g], both(i, s))
                        vv.tensor_reduce(top[s][:, :, g, :, AHEAD].rearrange("p t j -> p j t"), banks(s, 0, 4).rearrange("p j (t n) -> p j t n", t=2),
                                         AX, ALU.max, negate=True).then_inc((m.top_kept0, m.top_kept1)[g], 1)
                for s in range(2):
                    dve.wait_ge(m.topT, both(i, s))
                    vv.tensor_tensor(q[s][:, :, :], bank(s, 0).rearrange("p (g n) -> p g n", g=2), q[s][:, :, :], ALU.add).then_inc(m.q_shifted, 1)
                for s in range(2):
                    dve.wait_ge(m.summed, both(i, s))
                    made = bank(s, 3)[:, 0:2 * AHEADS * (AHEAD + 1)].rearrange("p (g d) -> p g d", d=AHEAD + 1)
                    vv.reciprocal(share[s][:, :], made[:, :, AHEAD])
                    dve.drain()
                    vv.tensor_tensor(o[s][:, :, :].rearrange("p t (h d) -> p (t h) d", d=AHEAD), made[:, :, 0:AHEAD],
                                     share[s][:, :].unsqueeze(2).to_broadcast([P, 16, AHEAD]), ALU.mult).then_inc(m.summed_kept, 1)
                for s in range(2):
                    dve.wait_ge(m.oT, both(i, s))
                    vv.tensor_copy(oT[s][:, :], bank(s, 0)[:, 0:256]).then_inc(m.oT_kept, 1)
                for s in range(2):
                    dve.wait_ge(m.projected, both(i, s))
                    dve.wait_ge(m.xb_ready, both(i, s))
                    vv.tensor_tensor(c.X[:, bass.ds((i + s) * 2, 2), :], bank(s, 1)[:, 0:256].rearrange("p (t d) -> p t d", t=2), xb[s][:, :, :],
                                     ALU.add).then_inc(m.done, 1)
                dve.drain()


def tower(nc, ins, out):
    c = Chip()
    with ExitStack() as ctx:
        load_constants(nc, c, ins, ctx)
        embed(nc, c, ins)
        with ExitStack() as layers:
            w = performer_weights(nc, c, layers)
            for layer in range(2):
                prepare_performer(nc, c, w, ins, layer)
                performer(nc, c, w, layer)
        with ExitStack() as mixture:
            expert_buffers(nc, c, mixture, 0)
            prepare_experts(nc, c, ins, 0, "L0_ffn", "L0_ffn_Ws", "L0_ffn_bs")
            gate(nc, c, "gate0", add=True)
            route(nc, c, "route0")
            experts(nc, c, "experts0", ACT.Gelu)
            combine(nc, c, "combine0")
        mamba(nc, c, ins)
        attention(nc, c, ins)
        with ExitStack() as mixture:
            expert_buffers(nc, c, mixture, 1)
            prepare_experts(nc, c, ins, 1, "L1_ffn", "L1_ffn_gate_W", "L1_ffn_gate_b", norm=("L1_ffn_ln1_g", "L1_ffn_ln1_b"))
            gate(nc, c, "gate1", add=False)
            route(nc, c, "route1")
            experts(nc, c, "experts1", ACT.Gelu_apprx_tanh)
            combine(nc, c, "combine1", out)


def laid_out(inputs):
    import numpy as np

    z = {name: np.asarray(a) for name, a in inputs.items()}
    keep = [n for n in z if n.startswith(("L0_attn_", "L0_ffn_", "L1_ffn_")) and n != "L0_attn_proj"]
    a = {n: z[n] for n in keep}
    a["ids"] = z["x"].reshape(TILES, P).T
    a["cache"] = z["L0_tok_sin_cos_cache"][..., ::-1].reshape(-1, P)
    a["projT"] = z["L0_attn_proj"].transpose(0, 2, 1)
    f, b = ({n: z[f"L1_attn_{d}_{n}"] for n in ("in_w", "conv_w", "conv_b", "dt_bias", "A_log", "D", "gnorm_w", "out_w")} for d in "fb")
    fw, bw = f["in_w"], b["in_w"]
    x, bs, cs, dts = (slice(lo, hi) for lo, hi in ((256, 512), (512, 576), (576, 640), (640, 644)))
    a["m_w_in"] = np.concatenate([fw[x], bw[x], fw[bs], bw[bs], fw[cs], bw[cs], fw[0:256], bw[0:256], fw[dts], bw[dts]]).T

    def channels(n):
        g, h = f[n], b[n]
        joined = np.concatenate([g[0:256], h[0:256], g[256:320], h[256:320], g[320:384], h[320:384]])
        return np.moveaxis(joined.reshape((MIX, P) + joined.shape[1:]), 0, 1)

    a["m_taps"] = channels("conv_w")
    a["m_tap_bias"] = channels("conv_b")
    join = lambda n: np.concatenate([f[n], b[n]])
    a["m_columns"] = np.concatenate([z["L1_attn_norm_w"][None], np.repeat(join("D"), HEAD).reshape(4, P), join("gnorm_w").reshape(4, P)]).T
    a["m_dt_bias"] = join("dt_bias")
    a["m_A_log"] = join("A_log")
    a["m_out_w"] = np.concatenate([f["out_w"], b["out_w"]], 1)
    a["m_projT"] = np.concatenate([z["L1_attn_proj_w"][:, :P].T, z["L1_attn_proj_w"][:, P:].T], 1)
    r, t = np.arange(P)[:, None], np.arange(P)[None]
    a["m_masks"] = np.stack([r < t, r > t, r <= t, r >= t], 1).astype(np.float32)
    a["before"] = (r < t).astype(np.float32)
    a["ident"] = (r == t).astype(np.float32)
    a["experts"] = np.broadcast_to(np.arange(EXPERTS, dtype=np.float32) - EXPERTS, (P, EXPERTS))
    a["tile_start"] = (np.arange(SORTED, dtype=np.float32) * P)[None]
    return {n: np.ascontiguousarray(v) for n, v in a.items()}


def kernel(**inputs):
    import concourse.bacc as bacc
    from concourse.bass_utils import run_bass_kernel_spmd

    nc = bacc.Bacc("TRN2", target_bir_lowering=False, num_devices=1)
    arrays = laid_out(inputs)
    ins = {n: nc.dram_tensor(f"in_{n}", v.shape, mybir.dt.from_np(v.dtype), kind="ExternalInput").ap() for n, v in arrays.items()}
    out = nc.dram_tensor("out_0", (SEQS, SEQ_TILES * P, P), F32, kind="ExternalOutput").ap()
    tower(nc, ins, out)
    done = run_bass_kernel_spmd(nc, [{f"in_{n}": v for n, v in arrays.items()}], core_ids=[0])
    return done.results[0]["out_0"]
```

```python
from contextlib import ExitStack

import concourse.bass as bass
from concourse import mybir

F32 = mybir.dt.float32
I32 = mybir.dt.int32
U32 = mybir.dt.uint32
ALU = mybir.AluOpType
ACT = mybir.ActivationFunctionType
AX = mybir.AxisListType.X

P = 128
SEQS, SEQ_TILES = 32, 2
TILES = SEQS * SEQ_TILES
LANES = 4
HEADS, HEAD = 8, 64
WIDE = HEADS * HEAD
BLOCKS = WIDE // P
EXPERTS = 8
SORTED = TILES + EXPERTS
GATE_LANES = 4
GROUP = 8
GROUPS_OF_TILES = TILES // GROUP
EPS = 1e-5
KERNEL_EPS = 1e-4
DATA_NORM = HEAD ** -0.25
DIAG = 0.5 * HEAD ** -0.5


def both(i, s):
    return i + (s + 1)


def signals(nc, ctx):
    taken = []

    def take(name):
        taken.append(nc.alloc_semaphore(name))
        return taken[-1]

    def clear():
        nc.clear_and_free_semaphores(taken)
        nc.all_engine_barrier()

    ctx.callback(clear)
    return take


def in_turn(*parts):
    waiting = [[next(part, None), n, part] for n, part in enumerate(parts)]
    while True:
        ready = [w for w in waiting if w[0] is not None]
        if not ready:
            return
        least = min(ready, key=lambda w: (w[0], w[1]))
        least[0] = next(least[2], None)


def skewed(engine, first, second):
    in_turn(first(0, 0))
    with engine.Fori(0, SEQS - 3, 2) as i:
        in_turn(first(i, 1), second(i, 0))
        in_turn(first(i + 2, 0), second(i, 1))
    in_turn(first(SEQS - 2, 1), second(SEQS - 2, 0))
    in_turn(second(SEQS - 2, 1))


class Chip:
    pass


def broadcast_rows(vector_ap, width):
    return bass.AP(vector_ap.tensor, vector_ap.offset, [[0, P], [1, width]])


def fold_norm(nc, c, ctx, name, items, landed, landed_count, folds=()):
    take = signals(nc, ctx)
    raw_product = take(f"{name}_raw_product")
    scaled = take(f"{name}_scaled")
    row_product = take(f"{name}_row_product")
    folded = take(f"{name}_folded")
    turned = take(f"{name}_turned")
    turned_kept = take(f"{name}_turned_kept")
    joined = take(f"{name}_joined")
    joined_kept = take(f"{name}_joined_kept")
    turned_sb = ctx.enter_context(nc.sbuf_tensor(f"{name}_turned_sb", [P, WIDE if folds else 1], F32))
    BANKS = 4

    with nc.Block() as block:
        @block.tensor
        def _(pe):
            pe.wait_ge(landed, landed_count)
            for m, (w, scale, norm_bias, biases, own) in enumerate(items):
                rows = c.PS[:, m % BANKS, 0:w.shape[1]]
                if m >= BANKS:
                    pe.wait_ge(folded, m - BANKS + 1)
                if norm_bias is not None:
                    nc.tensor.matmul(rows, norm_bias, w, start=True, stop=False).then_inc(raw_product, 1)
                k = biases.shape[0]
                nc.tensor.matmul(rows, c.ident[0:k, own:own + 1].to_broadcast([k, P]), biases, start=norm_bias is None, stop=False)
                if scale is not None:
                    pe.wait_ge(scaled, m + 1)
                nc.tensor.matmul(rows, c.minus_ones[:, :], w, start=False, stop=True).then_inc(row_product, 1)
            for m, (w, matrix, _) in enumerate(folds):
                pe.wait_ge(folded, len(items))
                if m:
                    pe.wait_ge(joined_kept, m)
                for b in range(BLOCKS):
                    last = nc.tensor.transpose(c.PS[:, 4, bass.ts(b, P)], w[:, bass.ts(b, P)], c.ident[:, :])
                last.then_inc(turned, 1)
                pe.wait_ge(turned_kept, m + 1)
                for b in range(BLOCKS):
                    last = nc.tensor.matmul(c.PS[:, 5, bass.ts(b, P)], turned_sb[:, bass.ts(b, P)], matrix,
                                            start=True, stop=True)
                last.then_inc(joined, 1)

        @block.vector
        def _(dve):
            dve.wait_ge(landed, landed_count)
            for m, (w, scale, norm_bias, _, _) in enumerate(items):
                if scale is not None:
                    if norm_bias is not None:
                        dve.wait_ge(raw_product, m + 1)
                    nc.vector.tensor_scalar(w, w, scale, None, ALU.mult).then_inc(scaled, 1)
                dve.wait_ge(row_product, m + 1)
                nc.vector.scalar_tensor_tensor(w, c.PS[:, m % BANKS, 0:w.shape[1]], 1.0 / P, w, ALU.mult, ALU.add).then_inc(folded, 1)
            for m, (_, _, product) in enumerate(folds):
                dve.wait_ge(turned, m + 1)
                nc.vector.tensor_copy(turned_sb[:, :], c.PS[:, 4, :]).then_inc(turned_kept, 1)
                dve.wait_ge(joined, m + 1)
                nc.vector.tensor_copy(product, c.PS[:, 5, :]).then_inc(joined_kept, 1)


def load_constants(nc, c, ins, ctx):
    sb = lambda n, shape, dt=F32: ctx.enter_context(nc.sbuf_tensor(n, shape, dt))
    c.H = sb("H", [P, TILES, P])
    c.X = sb("X", [P, SORTED, P])
    c.ident = sb("ident", [P, P])
    c.minus_ones = sb("minus_ones", [P, P])
    c.minus_half = sb("minus_half", [P, 4])
    c.eps = sb("eps", [P, 4])
    c.ids = sb("ids", [P, TILES], I32)
    c.before = sb("before", [P, P])
    c.experts = sb("experts", [P, EXPERTS])
    c.tile_start = sb("tile_start", [1, SORTED])
    c.logits = sb("logits", [P, TILES, EXPERTS])
    c.weight = sb("weight", [P, TILES])
    c.row_of = sb("row_of", [P, TILES], I32)
    c.tile_expert = sb("tile_expert", [1, SORTED], I32)
    c.sorted_in = nc.dram_tensor("sorted_in", [(SORTED + LANES) * P, P], F32).ap()
    c.sorted_out = nc.dram_tensor("sorted_out", [SORTED * P, P], F32).ap()
    c.PS = ctx.enter_context(nc.psum_tensor("PS", [P, 8, 512], F32))
    landed = ctx.enter_context(nc.semaphore("constants_landed"))
    zeroed = ctx.enter_context(nc.semaphore("zeroed"))
    c.weights_landed = [ctx.enter_context(nc.semaphore(f"expert_weights_landed_{n}")) for n in range(2)]
    with nc.Block() as block:
        @block.sync
        def _(sp):
            sp.dma_start(c.ident[:, :], ins["ident"]).then_inc(landed, 16)
            sp.dma_start(c.ids[:, :], ins["ids"]).then_inc(landed, 16)
            sp.dma_start(c.before[:, :], ins["before"]).then_inc(landed, 16)
            sp.dma_start(c.experts[:, :], ins["experts"]).then_inc(landed, 16)
            sp.dma_start(c.tile_start[:, :], ins["tile_start"]).then_inc(landed, 16)
            sp.wait_ge(zeroed, 1)
            rows = c.sorted_in.rearrange("(p r) d -> p (r d)", p=P)
            sp.dma_start(rows[:, 0:SORTED * P], c.X[:, :, :].rearrange("p r d -> p (r d)")).then_inc(landed, 16)
            sp.dma_start(rows[:, SORTED * P:], c.X[:, 0:LANES, :].rearrange("p r d -> p (r d)")).then_inc(landed, 16)
            sp.wait_ge(landed, 7 * 16)

        @block.vector
        def _(dve):
            nc.vector.memset(c.X[:, :, :], 0.0).then_inc(zeroed, 1)
            nc.vector.memset(c.minus_ones[:, :], -1.0)
            nc.vector.memset(c.minus_half[:, :], -0.5)
            nc.vector.memset(c.eps[:, :], EPS)
            dve.drain()


def embed(nc, c, ins, layers):
    with ExitStack() as ctx:
        sb = lambda n, shape, dt=F32: ctx.enter_context(nc.sbuf_tensor(f"embed_{n}", shape, dt))
        sem = signals(nc, ctx)
        sums = [sb(f"sums_{n}", [P, GROUP, 6]) for n in range(2)]
        stat = [sb(f"stat_{n}", [P, GROUP, 2]) for n in range(2)]
        rstd = [sb(f"rstd_{n}", [P, GROUP]) for n in range(2)]
        half = sb("half", [P, GROUP])
        gathered = [sem(f"embed_gathered_{n}") for n in range(2)]
        stats = sem("embed_stats")
        rstd_ready = sem("embed_rstd")
        opened = sem("embed_proj_opened")
        block = ctx.enter_context(nc.Block())

        @block.sync
        def _(sp):
            sp.wait_ge(opened, 1)
            load_performer(nc, sp, layers[0], ins, 0)

        @block.gpsimd
        def _(pool):
            def gather(g):
                for t in range(g * GROUP, (g + 1) * GROUP):
                    pool.indirect_dma_start(out=c.H[:, t, :], out_offset=None, in_=ins["cache"],
                                            in_offset=bass.IndirectOffsetOnAxis(ap=c.ids[:, t:t + 1], axis=0)
                                            ).then_inc(gathered[g % 2], 16)

            nc.gpsimd.memset(half[:, :], -0.5)
            gather(0)
            gather(1)
            for g in range(GROUPS_OF_TILES):
                pool.wait_ge(stats, (g + 1) * GROUP)
                r = rstd[g % 2][:, :]
                nc.gpsimd.tensor_tensor(r, stat[g % 2][:, :, 1], c.eps[:, 0:1].to_broadcast([P, GROUP]), ALU.add)
                pool.drain()
                nc.gpsimd.tensor_tensor(r, r, half[:, :], ALU.pow).then_inc(rstd_ready, GROUP)
                if g + 2 < GROUPS_OF_TILES:
                    gather(g + 2)

        @block.vector
        def _(dve):
            for w in layers:
                last = nc.vector.memset(w.proj[:, :], 0.0)
            last.then_inc(opened, 1)
            with dve.Fori(0, TILES - 2 * GROUP + 1, 2 * GROUP) as t:
                tile = lambda a, n, j: a[:, bass.ds(t + (n * GROUP + j), 1), :].rearrange("p o d -> p (o d)")
                for n in range(2):
                    dve.wait_ge(gathered[n], (t + 2 * GROUP) * 8)
                    for j in range(GROUP):
                        nc.vector.bn_stats(sums[n][:, j, :], tile(c.H, n, j))
                    dve.drain()
                    for j in range(GROUP):
                        last = nc.vector.bn_aggr(stat[n][:, j, :], sums[n][:, j, :])
                    last.then_inc(stats, GROUP)
                for n in range(2):
                    dve.wait_ge(rstd_ready, t + (n + 1) * GROUP)
                    for j in range(GROUP):
                        nc.vector.tensor_scalar(tile(c.X, n, j), tile(c.H, n, j), stat[n][:, j, 0:1], rstd[n][:, j:j + 1],
                                                ALU.subtract, ALU.mult)
                dve.drain()


class NormBuffers:

    def __init__(self, nc, ctx, name):
        sb = lambda n, shape: ctx.enter_context(nc.sbuf_tensor(f"{name}_{n}", shape, F32))
        self.sums = sb("sums", [P, SEQ_TILES, 6])
        self.stat = sb("stat", [P, SEQ_TILES, 2])
        self.rstd = sb("rstd", [P, SEQ_TILES])
        self.last = None


def norm_stats(nc, dve, norm, rows):
    for t in range(SEQ_TILES):
        nc.vector.bn_stats(norm.sums[:, t, :], rows[:, t, :])
    dve.drain()
    for t in range(SEQ_TILES):
        norm.last = nc.vector.bn_aggr(norm.stat[:, t, :], norm.sums[:, t, :])


def norm_rstd(nc, pool, c, norm):
    nc.gpsimd.tensor_tensor(norm.rstd[:, :], norm.stat[:, :, 1], c.eps[:, 0:SEQ_TILES], ALU.add)
    pool.drain()
    norm.last = nc.gpsimd.tensor_tensor(norm.rstd[:, :], norm.rstd[:, :], c.minus_half[:, 0:SEQ_TILES], ALU.pow)


def norm_apply(nc, norm, rows, out):
    for t in range(SEQ_TILES):
        norm.last = nc.vector.tensor_scalar(out(t), rows[:, t, :], norm.stat[:, t, 0:1], norm.rstd[:, t:t + 1],
                                            ALU.subtract, ALU.mult)


def performer_weights(nc, c, ctx, layer):
    sb = lambda n, shape: ctx.enter_context(nc.sbuf_tensor(f"performer_{layer}_{n}", shape, F32))
    w = Chip()
    w.q, w.k, w.v, w.qd, w.kd, w.w1 = (sb(n, [P, WIDE]) for n in ("q", "k", "v", "qd", "kd", "w1"))
    w.wo, w.w2 = (sb(n, [P, BLOCKS, P]) for n in ("wo", "w2"))
    w.bo, w.b2 = (sb(n, [P, P]) for n in ("bo", "b2"))
    w.wide_biases = sb("wide_biases", [4, WIDE])
    w.columns = sb("columns", [P, 4])
    w.norm_bias = [sb("ln1_bias_wide", [P, P]), sb("ln2_bias_wide", [P, P])]
    w.proj = sb("proj", [P, P])
    w.landed = ctx.enter_context(nc.semaphore(f"performer_{layer}_landed"))
    return w


PERFORMER_LOADS = 18 * 16


def load_performer(nc, sp, w, ins, layer):
    row = lambda n: ins[f"L0_attn_{n}"][layer]
    for at, name in ((w.q, "Wq"), (w.k, "Wk"), (w.v, "Wv"), (w.w1, "W1")):
        sp.dma_start(at[:, :], row(name)).then_inc(w.landed, 16)
    for at, name in ((w.wo, "Wo"), (w.w2, "W2")):
        sp.dma_start(at[:, :, :], row(name).rearrange("(b p) d -> p b d", p=P)).then_inc(w.landed, 16)
    for at, name in ((w.bo, "bo"), (w.b2, "b2")):
        sp.dma_start(at[:, :], broadcast_rows(row(name), P)).then_inc(w.landed, 16)
    for k, name in enumerate(("bq", "bk", "bv", "b1")):
        sp.dma_start(w.wide_biases[k:k + 1, :], row(name).rearrange("(o d) -> o d", o=1)).then_inc(w.landed, 16)
    for k, name in enumerate(("ln1_s", "ln1_b", "ln2_s", "ln2_b")):
        sp.dma_start(w.columns[:, k:k + 1], row(name).rearrange("(p o) -> p o", o=1)).then_inc(w.landed, 16)
    for h in range(2):
        sp.dma_start(w.proj[bass.ts(h, HEAD), bass.ts(h, HEAD)], ins["projT"][layer]).then_inc(w.landed, 16)


def prepare_performer(nc, c, w, layer):
    with ExitStack() as ctx:
        with nc.Block() as block:
            @block.vector
            def _(dve):
                dve.wait_ge(w.landed, PERFORMER_LOADS)
                for k in range(2):
                    nc.vector.tensor_copy(w.norm_bias[k][:, :], w.columns[:, 2 * k + 1:2 * k + 2].to_broadcast([P, P]))
                nc.vector.tensor_scalar(w.proj[:, :], w.proj[:, :], DATA_NORM, None, ALU.mult)
                dve.drain()
        scale1, scale2 = w.columns[:, 0:1], w.columns[:, 2:3]
        biases = w.wide_biases[:, :]
        fold_norm(nc, c, ctx, f"performer_{layer}",
                  [(w.q[:, :], scale1, w.norm_bias[0][:, :], biases, 0),
                   (w.k[:, :], scale1, w.norm_bias[0][:, :], biases, 1),
                   (w.v[:, :], scale1, w.norm_bias[0][:, :], biases, 2),
                   (w.w1[:, :], scale2, w.norm_bias[1][:, :], biases, 3)],
                  w.landed, PERFORMER_LOADS,
                  [(w.q[:, :], w.proj[:, :], w.qd[:, :]), (w.k[:, :], w.proj[:, :], w.kd[:, :])])


def performer(nc, c, w, layer, prefetch):
    with ExitStack() as ctx:
        sb = lambda n, shape: [ctx.enter_context(nc.sbuf_tensor(f"p{layer}_{n}_{s}", shape, F32)) for s in range(2)]
        take = signals(nc, ctx)
        sem = lambda n: take(f"p{layer}_{n}")
        xn = sb("xn", [P, SEQ_TILES, P])
        xb = sb("xb", [P, SEQ_TILES, P])
        x2 = sb("x2", [P, SEQ_TILES, P])
        hT = sb("hT", [P, SEQ_TILES * P])
        square = sb("square", [P, SEQ_TILES * WIDE])
        feat = sb("feat", [P, SEQ_TILES * WIDE])
        featT = sb("featT", [P, BLOCKS, SEQ_TILES * P])
        attn = sb("attn", [P, SEQ_TILES * WIDE])
        v = sb("v", [P, SEQ_TILES, HEADS, HEAD + 1])
        ctx_sb = sb("ctx", [P, BLOCKS, 2, HEAD + 1])
        top = sb("top", [P, 2 * HEADS])
        top8 = sb("top8", [P, HEADS])
        top1 = sb("top1", [HEADS, 1])
        power = sb("power", [P, 2 * HEADS])
        shift = sb("shift", [P, 2 * HEADS])
        share = sb("share", [P, 2 * HEADS])
        norm = [NormBuffers(nc, ctx, f"p{layer}_norm_{s}") for s in range(2)]
        bank = lambda s, b: c.PS[:, 4 * s + b, :]
        banks = lambda s, b, n: c.PS[:, 4 * s + b:4 * s + b + n, :]
        m = Chip()
        m.stats, m.rstd, m.xb_ready, m.xn_ready, m.xnT, m.hT_ready, m.kd_made = map(sem, (
            "stats", "rstd", "xb_ready", "xn_ready", "xnT", "hT_ready", "kd_made"))
        m.k_made, m.k_squared, m.k_top, m.k_topT, m.k_top1, m.k_topped, m.k_arg = map(sem, (
            "k_made", "k_squared", "k_top", "k_topT", "k_top1", "k_topped", "k_arg"))
        m.k_exp, m.k_feat, m.v_made, m.v_kept, m.ctx_made, m.ctx_kept, m.q_made = map(sem, (
            "k_exp", "k_feat", "v_made", "v_kept", "ctx_made", "ctx_kept", "q_made"))
        m.q_squared, m.q_power, m.qd_made, m.q_arg, m.q_exp, m.q_featT, m.q_featT_kept = map(sem, (
            "q_squared", "q_power", "qd_made", "q_arg", "q_exp", "q_featT", "q_featT_kept"))
        m.weighed, m.attn_kept, m.attnT, m.attnT_kept, m.o_made, m.x2_stats, m.x2_rstd = map(sem, (
            "weighed", "attn_kept", "attnT", "attnT_kept", "o_made", "x2_stats", "x2_rstd"))
        m.x2b_ready, m.x2n_ready, m.x2nT, m.h2T_ready, m.f_made, m.f_kept, m.y_made = map(sem, (
            "x2b_ready", "x2n_ready", "x2nT", "h2T_ready", "f_made", "f_kept", "y_made"))
        m.done, = map(sem, (
            "done",))
        N = SEQS

        block = ctx.enter_context(nc.Block())

        @block.sync
        def _(sp):
            prefetch(sp)

        @block.tensor
        def _(pe):
            def first(i, s):
                yield 2.06
                pe.wait_ge(m.xn_ready, both(i, s))
                for t in range(2):
                    last = nc.tensor.transpose(bank(s, 0)[:, bass.ts(t, P)], xn[s][:, t, :], c.ident[:, :])
                last.then_inc(m.xnT, 1)
                yield 4.11
                pe.wait_ge(m.hT_ready, both(i, s))
                for t in range(2):
                    last = nc.tensor.matmul(bank(s, 2 + t), hT[s][:, bass.ts(t, P)], w.kd[:, :], start=True, stop=True)
                last.then_inc(m.kd_made, 1)
                for t in range(2):
                    last = nc.tensor.matmul(bank(s, t), hT[s][:, bass.ts(t, P)], w.k[:, :], start=True, stop=True)
                last.then_inc(m.k_made, 1)
                yield 9.01
                pe.wait_ge(m.k_top, both(i, s))
                pe.wait_ge(m.k_squared, both(i, s))
                nc.tensor.transpose(bank(s, 0)[0:HEADS, 0:P], top8[s][:, :], c.ident[:, :]).then_inc(m.k_topT, 1)
                yield 11.01
                pe.wait_ge(m.k_top1, both(i, s))
                nc.tensor.matmul(bank(s, 0)[:, 256:256 + HEADS], top1[s][:, 0:1].to_broadcast([HEADS, P]),
                                 c.ident[0:HEADS, 0:HEADS], start=True, stop=True).then_inc(m.k_topped, 1)
                yield 14.1
                pe.wait_ge(m.k_arg, both(i, s))
                for t in range(2):
                    last = nc.tensor.matmul(bank(s, t), hT[s][:, bass.ts(t, P)], w.v[:, :], start=True, stop=True)
                last.then_inc(m.v_made, 1)
                yield 14.94
                pe.wait_ge(m.v_kept, both(i, s))
                for t in range(2):
                    last = nc.tensor.matmul(bank(s, t), hT[s][:, bass.ts(t, P)], w.q[:, :], start=True, stop=True)
                last.then_inc(m.q_made, 1)
                yield 17.06
                pe.wait_ge(m.k_feat, both(i, s))
                for b in range(BLOCKS):
                    out = bank(s, 2 + b // 2)[:, (b % 2) * 130:(b % 2) * 130 + 130]
                    for t in range(2):
                        last = nc.tensor.matmul(out, feat[s][:, t * WIDE + b * P:t * WIDE + (b + 1) * P],
                                                v[s][:, t, 2 * b:2 * b + 2, :].rearrange("p h d -> p (h d)"),
                                                start=t == 0, stop=t == 1)
                last.then_inc(m.ctx_made, 1)
                yield 18.4
                pe.wait_ge(m.ctx_kept, both(i, s))
                for t in range(2):
                    last = nc.tensor.matmul(bank(s, 2 + t), hT[s][:, bass.ts(t, P)], w.qd[:, :], start=True, stop=True)
                last.then_inc(m.qd_made, 1)

            def second(i, s):
                yield 3.27
                pe.wait_ge(m.q_squared, both(i, s))
                pe.wait_ge(m.q_exp, both(i, s))
                for b in range(BLOCKS):
                    for t in range(2):
                        out = bank(s, b // 2)[:, (b % 2) * 256 + t * P:(b % 2) * 256 + (t + 1) * P]
                        last = nc.tensor.transpose(out, feat[s][:, t * WIDE + b * P:t * WIDE + (b + 1) * P], c.ident[:, :])
                last.then_inc(m.q_featT, 1)
                yield 7.94
                pe.wait_ge(m.q_featT_kept, both(i, s))
                for t in range(2):
                    for b in range(BLOCKS):
                        out = bank(s, 2 * t + b // 2)[:, (b % 2) * 130:(b % 2) * 130 + 130]
                        last = nc.tensor.matmul(out, featT[s][:, b, bass.ts(t, P)],
                                                ctx_sb[s][:, b, :, :].rearrange("p h d -> p (h d)"), start=True, stop=True)
                last.then_inc(m.weighed, 1)
                yield 9.52
                pe.wait_ge(m.attn_kept, both(i, s))
                for b in range(BLOCKS):
                    for t in range(2):
                        out = bank(s, b // 2)[:, (b % 2) * 256 + t * P:(b % 2) * 256 + (t + 1) * P]
                        last = nc.tensor.transpose(out, attn[s][:, t * WIDE + b * P:t * WIDE + (b + 1) * P], c.ident[:, :])
                last.then_inc(m.attnT, 1)
                yield 12.2
                pe.wait_ge(m.attnT_kept, both(i, s))
                for t in range(2):
                    for b in range(BLOCKS):
                        last = nc.tensor.matmul(bank(s, 2)[:, bass.ts(t, P)], featT[s][:, b, bass.ts(t, P)], w.wo[:, b, :],
                                                start=b == 0, stop=b == BLOCKS - 1)
                last.then_inc(m.o_made, 1)
                yield 19.47
                pe.wait_ge(m.x2n_ready, both(i, s))
                for t in range(2):
                    last = nc.tensor.transpose(bank(s, 3)[:, bass.ts(t, P)], xn[s][:, t, :], c.ident[:, :])
                last.then_inc(m.x2nT, 1)
                yield 20.39
                pe.wait_ge(m.h2T_ready, both(i, s))
                for b in range(BLOCKS):
                    last = nc.tensor.matmul(bank(s, b // 2)[:, (b % 2) * 256:(b % 2) * 256 + 256], w.w1[:, bass.ts(b, P)],
                                            hT[s][:, :], start=True, stop=True)
                last.then_inc(m.f_made, 1)
                yield 23.74
                pe.wait_ge(m.f_kept, both(i, s))
                for t in range(2):
                    for b in range(BLOCKS):
                        last = nc.tensor.matmul(bank(s, 2)[:, bass.ts(t, P)], featT[s][:, b, bass.ts(t, P)], w.w2[:, b, :],
                                                start=b == 0, stop=b == BLOCKS - 1)
                last.then_inc(m.y_made, 1)

            skewed(pe, first, second)

        @block.scalar
        def _(act):
            def first(i, s):
                yield 8.33
                act.wait_ge(m.k_made, both(i, s))
                nc.scalar.activation(square[s][:, :], banks(s, 0, 2), ACT.Square).then_inc(m.k_squared, 1)
                yield 12.74
                act.wait_ge(m.k_arg, both(i, s))
                nc.scalar.activation(feat[s][:, :], feat[s][:, :], ACT.Exp).then_inc(m.k_exp, 1)
                yield 14.72
                act.wait_ge(m.v_made, both(i, s))
                nc.scalar.activation(v[s][:, :, :, 0:HEAD].rearrange("p t h d -> p (t h) d"),
                                     banks(s, 0, 2).rearrange("p t (h d) -> p (t h) d", d=HEAD), ACT.Copy).then_inc(m.v_kept, 1)
                yield 16.49
                act.wait_ge(m.q_made, both(i, s))
                nc.scalar.activation(square[s][:, :], banks(s, 0, 2), ACT.Square).then_inc(m.q_squared, 1)

            def second(i, s):
                yield 2.53
                act.wait_ge(m.q_arg, both(i, s))
                nc.scalar.activation(feat[s][:, :], feat[s][:, :], ACT.Exp).then_inc(m.q_exp, 1)
                yield 10.19
                act.wait_ge(m.attnT, both(i, s))
                nc.scalar.activation(featT[s][:, :, :], banks(s, 0, 2).rearrange("p b (c n) -> p (b c) n", n=256), ACT.Copy).then_inc(m.attnT_kept, 1)
                yield 20.4
                act.wait_ge(m.f_made, both(i, s))
                nc.scalar.activation(featT[s][:, :, :], banks(s, 0, 2).rearrange("p b (c n) -> p (b c) n", n=256), ACT.Gelu_apprx_tanh).then_inc(m.f_kept, 1)

            skewed(act, first, second)

        @block.gpsimd
        def _(pool):
            def sums_of_squares(s):
                n = HEAD // 2
                q = square[s][:, :].rearrange("p (g d) -> p g d", d=HEAD)
                half = attn[s][:, 0:WIDE].rearrange("p (g d) -> p g d", d=n)
                nc.gpsimd.tensor_tensor(half, q[:, :, 0:n], q[:, :, n:], ALU.add)
                while n > 2:
                    n //= 2
                    pool.drain()
                    nc.gpsimd.tensor_tensor(half[:, :, 0:n], half[:, :, 0:n], half[:, :, n:2 * n], ALU.add)
                pool.drain()
                return nc.gpsimd.tensor_tensor(power[s][:, :], half[:, :, 0], half[:, :, 1], ALU.add)

            def first(i, s):
                yield 2.04
                pool.wait_ge(m.stats, both(i, s))
                norm_rstd(nc, pool, c, norm[s])
                norm[s].last.then_inc(m.rstd, 1)
                for t in range(2):
                    last = nc.gpsimd.tensor_tensor(xb[s][:, t, :], c.X[:, bass.ds((i + s) * 2 + t, 1), :].rearrange("p o d -> p (o d)"), w.bo[:, :], ALU.add)
                last.then_inc(m.xb_ready, 1)
                yield 19.02
                pool.wait_ge(m.q_squared, both(i, s))
                sums_of_squares(s).then_inc(m.q_power, 1)

            def second(i, s):
                yield 14.72
                pool.wait_ge(m.x2_stats, both(i, s))
                norm_rstd(nc, pool, c, norm[s])
                norm[s].last.then_inc(m.x2_rstd, 1)
                for t in range(2):
                    last = nc.gpsimd.tensor_tensor(xb[s][:, t, :], x2[s][:, t, :], w.b2[:, :], ALU.add)
                last.then_inc(m.x2b_ready, 1)

            skewed(pool, first, second)

        @block.vector
        def _(dve):
            for s in range(2):
                nc.vector.memset(v[s][:, :, :, HEAD:HEAD + 1], 1.0)
                nc.vector.memset(ctx_sb[s][:, :, :, :], 0.0)
            dve.drain()
            halves = lambda a: a.rearrange("p (t h) -> p t h", t=2)
            heads = lambda a: a.rearrange("p (g d) -> p g d", d=HEAD)

            def exponent(s, shift_of):
                shift_of()
                dve.drain()
                return nc.vector.tensor_tensor(heads(feat[s][:, :]), banks(s, 2, 2).rearrange("p t (h d) -> p (t h) d", d=HEAD),
                                               shift[s][:, :].unsqueeze(2).to_broadcast([P, 2 * HEADS, HEAD]), ALU.subtract)

            def first(i, s):
                yield 0.27
                rows = c.X[:, bass.ds((i + s) * 2, 2), :]
                for t in range(SEQ_TILES):
                    nc.vector.bn_stats(norm[s].sums[:, t, :], c.X[:, bass.ds((i + s) * 2 + t, 1), :].rearrange("p o d -> p (o d)"))
                dve.drain()
                for t in range(SEQ_TILES):
                    last = nc.vector.bn_aggr(norm[s].stat[:, t, :], norm[s].sums[:, t, :])
                last.then_inc(m.stats, 1)
                yield 2.05
                dve.wait_ge(m.rstd, both(i, s))
                for t in range(SEQ_TILES):
                    last = nc.vector.tensor_scalar(xn[s][:, t, :], c.X[:, bass.ds((i + s) * 2 + t, 1), :].rearrange("p o d -> p (o d)"),
                                                   norm[s].stat[:, t, 0:1], norm[s].rstd[:, t:t + 1], ALU.subtract, ALU.mult)
                last.then_inc(m.xn_ready, 1)
                yield 3.05
                dve.wait_ge(m.xnT, both(i, s))
                nc.vector.tensor_scalar(hT[s][:, :], bank(s, 0)[:, 0:256], 1.0, None, ALU.add).then_inc(m.hT_ready, 1)
                yield 7.73
                dve.wait_ge(m.kd_made, both(i, s))
                nc.vector.tensor_reduce(top[s][:, :], banks(s, 2, 2).rearrange("p t (h d) -> p (t h) d", d=HEAD), AX, ALU.max)
                dve.drain()
                nc.vector.tensor_tensor(top8[s][:, :], top[s][:, 0:HEADS], top[s][:, HEADS:], ALU.max).then_inc(m.k_top, 1)
                yield 9
                dve.wait_ge(m.k_squared, both(i, s))
                nc.vector.tensor_reduce(power[s][:, :], heads(square[s][:, :]), AX, ALU.add)
                yield 10.4
                dve.wait_ge(m.k_topT, both(i, s))
                nc.vector.tensor_reduce(top1[s][:, :], bank(s, 0)[0:HEADS, 0:P], AX, ALU.max).then_inc(m.k_top1, 1)
                yield 11.18
                dve.drain()
                dve.wait_ge(m.k_topped, both(i, s))
                exponent(s, lambda: nc.vector.scalar_tensor_tensor(
                    halves(shift[s][:, :]), halves(power[s][:, :]), DIAG,
                    bank(s, 0)[:, 256:256 + HEADS].unsqueeze(1).to_broadcast([P, 2, HEADS]), ALU.mult, ALU.add)).then_inc(m.k_arg, 1)
                yield 12.86
                dve.wait_ge(m.k_exp, both(i, s))
                nc.vector.tensor_scalar(feat[s][:, :], feat[s][:, :], KERNEL_EPS, None, ALU.add).then_inc(m.k_feat, 1)
                yield 18.26
                dve.wait_ge(m.ctx_made, both(i, s))
                for half in range(2):
                    r = bass.ts(half, HEAD)
                    made = c.PS[r, 4 * s + 2:4 * s + 4, 0:260].rearrange("p b (c h d) -> p b c h d", c=2, h=2)[:, :, :, half, :]
                    last = nc.vector.tensor_copy(ctx_sb[s][r, :, half, :].rearrange("p (b c) d -> p b c d", c=2), made)
                last.then_inc(m.ctx_kept, 1)
                yield 21
                dve.wait_ge(m.qd_made, both(i, s))
                nc.vector.tensor_reduce(top[s][:, :], banks(s, 2, 2).rearrange("p t (h d) -> p (t h) d", d=HEAD), AX, ALU.max)
                dve.drain()
                dve.wait_ge(m.q_power, both(i, s))
                exponent(s, lambda: nc.vector.scalar_tensor_tensor(
                    shift[s][:, :], power[s][:, :], DIAG, top[s][:, :], ALU.mult, ALU.add)).then_inc(m.q_arg, 1)

            def second(i, s):
                yield 7.38
                dve.wait_ge(m.q_featT, both(i, s))
                nc.vector.tensor_scalar(featT[s][:, :, :], banks(s, 0, 2).rearrange("p b (c n) -> p (b c) n", n=256),
                                        KERNEL_EPS, None, ALU.add).then_inc(m.q_featT_kept, 1)
                yield 8.12
                dve.wait_ge(m.weighed, both(i, s))
                made = banks(s, 0, 4)[:, :, 0:260].rearrange("p b (h d) -> p b h d", h=4)
                nc.vector.reciprocal(share[s][:, :].rearrange("p (b h) -> p b h", h=4), made[:, :, :, HEAD])
                dve.drain()
                nc.vector.tensor_tensor(attn[s][:, :].rearrange("p (b h d) -> p b h d", b=4, h=4), made[:, :, :, 0:HEAD],
                                        share[s][:, :].rearrange("p (b h) -> p b h", h=4).unsqueeze(3).to_broadcast([P, 4, 4, HEAD]),
                                        ALU.mult).then_inc(m.attn_kept, 1)
                yield 13.71
                dve.wait_ge(m.o_made, both(i, s))
                dve.wait_ge(m.xb_ready, both(i, s))
                nc.vector.tensor_tensor(x2[s][:, :, :], bank(s, 2)[:, 0:256].rearrange("p (t d) -> p t d", t=2), xb[s][:, :, :], ALU.add)
                dve.drain()
                norm_stats(nc, dve, norm[s], x2[s])
                norm[s].last.then_inc(m.x2_stats, 1)
                yield 19
                dve.wait_ge(m.x2_rstd, both(i, s))
                norm_apply(nc, norm[s], x2[s], lambda t: xn[s][:, t, :])
                norm[s].last.then_inc(m.x2n_ready, 1)
                yield 20.35
                dve.wait_ge(m.x2nT, both(i, s))
                nc.vector.tensor_scalar(hT[s][:, :], bank(s, 3)[:, 0:256], 1.0, None, ALU.add).then_inc(m.h2T_ready, 1)
                yield 26.67
                dve.wait_ge(m.y_made, both(i, s))
                dve.wait_ge(m.x2b_ready, both(i, s))
                nc.vector.tensor_tensor(c.X[:, bass.ds((i + s) * 2, 2), :], bank(s, 2)[:, 0:256].rearrange("p (t d) -> p t d", t=2),
                                        xb[s][:, :, :], ALU.add).then_inc(m.done, 1)

            skewed(dve, first, second)


def expert_buffers(nc, c, ctx, which):
    sb = lambda n, shape, dt=F32: ctx.enter_context(nc.sbuf_tensor(f"{n}_{which}", shape, dt))
    c.w1 = sb("expert_w1", [P, EXPERTS, WIDE])
    c.w2 = sb("expert_w2", [P, EXPERTS, BLOCKS, P])
    c.b2 = sb("expert_b2", [P, EXPERTS, P])
    c.gate = sb("gate", [P, EXPERTS])
    c.b1 = sb("expert_b1", [EXPERTS, WIDE])
    c.gate_bias = sb("gate_bias", [1, EXPERTS])
    c.gate_norm = sb("gate_norm", [P, 2])


def load_experts(nc, c, sp, ins, which, prefix, gate_w, gate_b, norm=()):
    landed = c.weights_landed[which]
    sp.dma_start(c.gate[:, :], ins[gate_w]).then_inc(landed, 16)
    sp.dma_start(c.gate_bias[:, :], ins[gate_b].rearrange("(o e) -> o e", o=1)).then_inc(landed, 16)
    for k, name in enumerate(norm):
        sp.dma_start(c.gate_norm[:, k:k + 1], ins[name].rearrange("(p o) -> p o", o=1)).then_inc(landed, 16)
    sp.dma_start(c.b1[:, :], ins[f"{prefix}_b1"]).then_inc(landed, 16)
    sp.dma_start(c.w1[:, :, :], ins[f"{prefix}_W1"].rearrange("e p f -> p e f")).then_inc(landed, 16)
    for e in range(EXPERTS):
        sp.dma_start(c.w2[:, e, :, :], ins[f"{prefix}_W2"][e].rearrange("(b p) d -> p b d", p=P)).then_inc(landed, 16)
    sp.dma_start(c.b2[:, :, :].rearrange("p e d -> p (e d)"), broadcast_rows(ins[f"{prefix}_b2"], EXPERTS * P)).then_inc(landed, 16)


EXPERT_LOADS = 16 * (EXPERTS + 5)


def prepare_experts(nc, c, which, prefix, norm=()):
    with ExitStack() as ctx:
        norm_bias = ctx.enter_context(nc.sbuf_tensor(f"prepare_{prefix}_norm_bias", [P, P], F32))
        landed, count = c.weights_landed[which], EXPERT_LOADS + 16 * len(norm)
        with nc.Block() as block:
            if norm:
                @block.vector
                def _(dve):
                    dve.wait_ge(landed, count)
                    nc.vector.tensor_copy(norm_bias[:, :], c.gate_norm[:, 1:2].to_broadcast([P, P]))
                    dve.drain()
        scale = c.gate_norm[:, 0:1] if norm else None
        bias = norm_bias[:, :] if norm else None
        fold_norm(nc, c, ctx, prefix,
                  [(c.gate[:, :], scale, bias, c.gate_bias[:, :], 0)]
                  + [(c.w1[:, e, :], scale, bias, c.b1[:, :], e) for e in range(EXPERTS)],
                  landed, count)


def gate(nc, c, name, add):
    with ExitStack() as ctx:
        sb = lambda n, shape: [ctx.enter_context(nc.sbuf_tensor(f"{name}_{n}_{s}", shape, F32)) for s in range(GATE_LANES)]
        take = signals(nc, ctx)
        sem = lambda n: take(f"{name}_{n}")
        xn = sb("xn", [P, SEQ_TILES, P])
        hT = sb("hT", [P, SEQ_TILES * P])
        norm = [NormBuffers(nc, ctx, f"{name}_norm_{s}") for s in range(GATE_LANES)]
        stats, rstd, ready, turned, turned_kept, made, kept, copied = (
            sem(n) for n in ("stats", "rstd", "ready", "turned", "turned_kept", "made", "kept", "copied"))
        block = ctx.enter_context(nc.Block())

        @block.vector
        def _(dve):
            rows = c.H if add else c.X
            row = lambda i, s, t: rows[:, bass.ds((i + s) * 2 + t, 1), :].rearrange("p o d -> p (o d)")
            with dve.Fori(0, SEQS - GATE_LANES + 1, GATE_LANES) as i:
                for s in range(GATE_LANES):
                    if add:
                        here = bass.ds((i + s) * 2, 2)
                        nc.vector.tensor_tensor(c.H[:, here, :], c.H[:, here, :], c.X[:, here, :], ALU.add)
                        dve.drain()
                    for t in range(SEQ_TILES):
                        nc.vector.bn_stats(norm[s].sums[:, t, :], row(i, s, t))
                    dve.drain()
                    for t in range(SEQ_TILES):
                        last = nc.vector.bn_aggr(norm[s].stat[:, t, :], norm[s].sums[:, t, :])
                    last.then_inc(stats, 1)
                for s in range(GATE_LANES):
                    dve.wait_ge(rstd, both(i, s))
                    for t in range(SEQ_TILES):
                        last = nc.vector.tensor_scalar(xn[s][:, t, :], row(i, s, t), norm[s].stat[:, t, 0:1], norm[s].rstd[:, t:t + 1],
                                                       ALU.subtract, ALU.mult)
                    last.then_inc(ready, 1)
                for s in range(GATE_LANES):
                    dve.wait_ge(turned, both(i, s))
                    nc.vector.tensor_scalar(hT[s][:, :], c.PS[:, s, 0:256], 1.0, None, ALU.add).then_inc(turned_kept, 1)
                for s in range(GATE_LANES):
                    dve.wait_ge(made, both(i, s))
                    nc.vector.tensor_copy(c.logits[:, bass.ds((i + s) * 2, 2), :],
                                          c.PS[:, GATE_LANES + s, 0:16].rearrange("p (t e) -> p t e", t=2)).then_inc(kept, 1)
                dve.drain()
                dve.wait_ge(copied, both(i, GATE_LANES - 1))

        @block.gpsimd
        def _(pool):
            with pool.Fori(0, SEQS - GATE_LANES + 1, GATE_LANES) as i:
                for s in range(GATE_LANES):
                    pool.wait_ge(stats, both(i, s))
                    norm_rstd(nc, pool, c, norm[s])
                    norm[s].last.then_inc(rstd, 1)

        @block.scalar
        def _(act):
            with act.Fori(0, SEQS - GATE_LANES + 1, GATE_LANES) as i:
                for s in range(GATE_LANES):
                    act.wait_ge(ready, both(i, s))
                    nc.scalar.activation(c.X[:, bass.ds((i + s) * 2, 2), :], xn[s][:, :, :], ACT.Copy).then_inc(copied, 1)

        @block.tensor
        def _(pe):
            with pe.Fori(0, SEQS - GATE_LANES + 1, GATE_LANES) as i:
                for s in range(GATE_LANES):
                    pe.wait_ge(ready, both(i, s))
                    for t in range(2):
                        last = nc.tensor.transpose(c.PS[:, s, bass.ts(t, P)], xn[s][:, t, :], c.ident[:, :])
                    last.then_inc(turned, 1)
                for s in range(GATE_LANES):
                    pe.wait_ge(turned_kept, both(i, s))
                    for t in range(2):
                        last = nc.tensor.matmul(c.PS[:, GATE_LANES + s, bass.ts(t, EXPERTS)], hT[s][:, bass.ts(t, P)], c.gate[:, :],
                                                start=True, stop=True)
                    last.then_inc(made, 1)


def route(nc, c, name):
    T = TILES
    with ExitStack() as ctx:
        sb = lambda n, shape, dt=F32: ctx.enter_context(nc.sbuf_tensor(f"{name}_{n}", shape, dt))
        take = signals(nc, ctx)
        sem = lambda n: take(f"{name}_{n}")
        largest = sb("largest", [P, T])
        first = sb("first", [P, T])
        total = sb("total", [P, T])
        chosen = sb("chosen", [P, T, EXPERTS])
        work = sb("work", [P, T, EXPERTS])
        exps = sb("exps", [P, T, EXPERTS])
        before = [sb(f"before_{n}", [P, T, EXPERTS]) for n in range(2)]
        count = sb("count", [P, EXPERTS])
        count_int = sb("count_int", [P, EXPERTS], I32)
        start = sb("start", [P, EXPERTS + 1])
        passed = sb("passed", [1, SORTED, EXPERTS])
        number = sb("number", [1, SORTED])
        shifted, expd, one_hot, counted, routed, sent = (sem(n) for n in ("shifted", "expd", "one_hot", "counted", "routed", "sent"))
        wide = lambda a: a.unsqueeze(2).to_broadcast([P, T, EXPERTS])
        block = ctx.enter_context(nc.Block())

        @block.scalar
        def _(act):
            act.wait_ge(shifted, 1)
            nc.scalar.activation(exps[:, :, :], exps[:, :, :], ACT.Exp).then_inc(expd, 1)

        @block.tensor
        def _(pe):
            pe.wait_ge(one_hot, 1)
            flat = chosen[:, :, :].rearrange("p t e -> p (t e)")
            n = T * EXPERTS
            nc.tensor.matmul(c.PS[:, 0, 0:n], c.before[:, :], flat, start=True, stop=True)
            nc.tensor.matmul(c.PS[:, 1, 0:n], c.minus_ones[:, :], flat, start=True, stop=True).then_inc(counted, 1)

        @block.vector
        def _(dve):
            v = nc.vector
            v.tensor_reduce(largest[:, :], c.logits[:, 0:T, :], AX, ALU.max)
            dve.drain()
            v.tensor_tensor(exps[:, :, :], c.logits[:, 0:T, :], wide(largest[:, :]), ALU.subtract).then_inc(shifted, 1)
            v.tensor_tensor(chosen[:, :, :], c.logits[:, 0:T, :], wide(largest[:, :]), ALU.is_equal)
            dve.drain()
            v.tensor_tensor(work[:, :, :], chosen[:, :, :], c.experts[:, :].unsqueeze(1).to_broadcast([P, T, EXPERTS]), ALU.mult)
            dve.drain()
            v.tensor_reduce(first[:, :], work[:, :, :], AX, ALU.min)
            dve.drain()
            v.tensor_tensor(chosen[:, :, :], wide(first[:, :]), c.experts[:, :].unsqueeze(1).to_broadcast([P, T, EXPERTS]),
                            ALU.is_equal).then_inc(one_hot, 1)
            dve.wait_ge(expd, 1)
            v.tensor_reduce(total[:, :], exps[:, :, :], AX, ALU.add)
            dve.drain()
            v.reciprocal(c.weight[:, 0:T], total[:, :])
            dve.wait_ge(counted, 1)
            v.tensor_scalar(before[0][:, :, :], c.PS[:, 1, 0:T * EXPERTS].rearrange("p (t e) -> p t e", e=EXPERTS), -1.0, None, ALU.mult)
            dve.drain()
            k, src = 1, 0
            while k < T:
                a, b = before[src], before[1 - src]
                v.tensor_tensor(b[:, k:, :], a[:, k:, :], a[:, 0:T - k, :], ALU.add)
                v.tensor_copy(b[:, 0:k, :], a[:, 0:k, :])
                dve.drain()
                k, src = 2 * k, 1 - src
            upto = before[src]
            v.tensor_scalar(count[:, :], upto[:, T - 1, :], float(P - 1), None, ALU.add)
            dve.drain()
            v.tensor_copy(count_int[:, :], count[:, :])
            dve.drain()
            v.tensor_scalar(count_int[:, :], count_int[:, :], 7, 7, ALU.arith_shift_right, ALU.arith_shift_left)
            dve.drain()
            v.tensor_copy(count[:, :], count_int[:, :])
            v.memset(start[:, :], 0.0)
            dve.drain()
            for e in range(EXPERTS):
                v.tensor_tensor(start[:, e + 1:e + 2], start[:, e:e + 1], count[:, e:e + 1], ALU.add)
                dve.drain()
            other = before[1 - src]
            v.tensor_tensor(other[:, :, :], upto[:, :, :], c.PS[:, 0, 0:T * EXPERTS].rearrange("p (t e) -> p t e", e=EXPERTS), ALU.add)
            dve.drain()
            v.tensor_tensor(other[:, :, :], other[:, :, :], start[:, 0:EXPERTS].unsqueeze(1).to_broadcast([P, T, EXPERTS]), ALU.add)
            v.tensor_copy(work[:, :, :], c.PS[:, 1, 0:T * EXPERTS].rearrange("p (t e) -> p t e", e=EXPERTS))
            dve.drain()
            v.tensor_tensor(other[:, :, :], other[:, :, :], work[:, :, :], ALU.add)
            dve.drain()
            v.tensor_tensor(other[:, :, :], other[:, :, :], chosen[:, :, :], ALU.mult)
            dve.drain()
            v.tensor_reduce(total[:, :], other[:, :, :], AX, ALU.add)
            dve.drain()
            v.tensor_copy(c.row_of[:, 0:T], total[:, :]).then_inc(routed, 1)
            v.tensor_tensor(passed[:, :, :], start[0:1, 1:EXPERTS + 1].unsqueeze(1).to_broadcast([1, SORTED, EXPERTS]),
                            c.tile_start[:, :].unsqueeze(2).to_broadcast([1, SORTED, EXPERTS]), ALU.is_le)
            dve.drain()
            v.tensor_reduce(number[:, :], passed[:, :, :], AX, ALU.add)
            dve.drain()
            v.tensor_scalar(number[:, :], number[:, :], float(EXPERTS - 1), None, ALU.min)
            dve.drain()
            v.tensor_copy(c.tile_expert[:, :], number[:, :])
            dve.drain()

        @block.gpsimd
        def _(pool):
            pool.wait_ge(routed, 1)
            for t in range(T):
                pool.indirect_dma_start(out=c.sorted_in, out_offset=bass.IndirectOffsetOnAxis(ap=c.row_of[:, t:t + 1], axis=0),
                                        in_=c.X[:, t, :], in_offset=None).then_inc(sent, 16)
            pool.wait_ge(sent, 16 * T)


def experts(nc, c, name, gelu):
    with ExitStack() as ctx:
        sb = lambda n, shape: [ctx.enter_context(nc.sbuf_tensor(f"{name}_{n}_{s}", shape, F32)) for s in range(LANES)]
        take = signals(nc, ctx)
        sem = lambda n: take(f"{name}_{n}")
        xs = sb("xs", [P, P])
        xsT = sb("xsT", [P, P])
        hid = sb("hid", [P, WIDE])
        hidT = sb("hidT", [P, WIDE])
        landed = [sem(f"landed_{s}") for s in range(LANES)]
        turned, turned_kept, made, kept, hidden_turned, hidden_kept, out_made, out_kept, stored = (
            sem(n) for n in ("turned", "turned_kept", "made", "kept", "hidden_turned", "hidden_kept", "out_made", "out_kept", "stored"))
        bank = lambda s, b: c.PS[:, 2 * s + b, :]
        w1 = c.w1[:, :, :].rearrange("p e f -> p (e f)")
        w2 = c.w2[:, :, :, :].rearrange("p e b d -> p (e b d)")
        b2 = c.b2[:, :, :].rearrange("p e d -> p (e d)")
        block = ctx.enter_context(nc.Block())

        @block.sync
        def _(sp):
            for s in range(LANES):
                sp.dma_start(xs[s][:, :], c.sorted_in[s * P:(s + 1) * P, :]).then_inc(landed[s], 16)
            with sp.Fori(0, SORTED - LANES + 1, LANES) as i:
                for s in range(LANES):
                    sp.wait_ge(turned, both(i, s))
                    sp.dma_start(xs[s][:, :], c.sorted_in[bass.ds((i + s + LANES) * P, P), :]).then_inc(landed[s], 16)
                for s in range(LANES):
                    sp.wait_ge(out_kept, both(i, s))
                    sp.dma_start(c.sorted_out[bass.ds((i + s) * P, P), :],
                                 c.X[:, bass.ds(i + s, 1), :].rearrange("p o d -> p (o d)")).then_inc(stored, 16)
            sp.wait_ge(stored, SORTED * 16)
            for s in range(LANES):
                sp.wait_ge(landed[s], (SORTED // LANES + 1) * 16)

        @block.tensor
        def _(pe):
            with pe.Fori(0, SORTED - LANES + 1, LANES) as i:
                for s in range(LANES):
                    pe.wait_ge(landed[s], (i + LANES) * (16 // LANES))
                    nc.tensor.transpose(bank(s, 0)[:, 0:P], xs[s][:, :], c.ident[:, :]).then_inc(turned, 1)
                which = []
                for s in range(LANES):
                    which.append(pe.value_load(c.tile_expert[0:1, bass.ds(i + s, 1)], min_val=0, max_val=EXPERTS - 1))
                    pe.wait_ge(turned_kept, both(i, s))
                    nc.tensor.matmul(bank(s, 1), xsT[s][:, :], w1[:, bass.ds(which[s] * WIDE, WIDE)], start=True, stop=True).then_inc(made, 1)
                for s in range(LANES):
                    pe.wait_ge(kept, both(i, s))
                    for b in range(BLOCKS):
                        last = nc.tensor.transpose(bank(s, 0)[:, bass.ts(b, P)], hid[s][:, bass.ts(b, P)], c.ident[:, :])
                    last.then_inc(hidden_turned, 1)
                for s in range(LANES):
                    pe.wait_ge(hidden_kept, both(i, s))
                    for b in range(BLOCKS):
                        last = nc.tensor.matmul(bank(s, 1)[:, 0:P], hidT[s][:, bass.ts(b, P)],
                                                w2[:, bass.ds(which[s] * WIDE + b * P, P)], start=b == 0, stop=b == BLOCKS - 1)
                    last.then_inc(out_made, 1)

        @block.scalar
        def _(act):
            with act.Fori(0, SORTED - LANES + 1, LANES) as i:
                for s in range(LANES):
                    act.wait_ge(made, both(i, s))
                    nc.scalar.activation(hid[s][:, :], bank(s, 1), gelu).then_inc(kept, 1)

        @block.vector
        def _(dve):
            with dve.Fori(0, SORTED - LANES + 1, LANES) as i:
                for s in range(LANES):
                    dve.wait_ge(turned, both(i, s))
                    nc.vector.tensor_scalar(xsT[s][:, :], bank(s, 0)[:, 0:P], 1.0, None, ALU.add).then_inc(turned_kept, 1)
                which = [dve.value_load(c.tile_expert[0:1, bass.ds(i + s, 1)], min_val=0, max_val=EXPERTS - 1) for s in range(LANES)]
                for s in range(LANES):
                    dve.wait_ge(hidden_turned, both(i, s))
                    nc.vector.tensor_copy(hidT[s][:, :], bank(s, 0)).then_inc(hidden_kept, 1)
                for s in range(LANES):
                    dve.wait_ge(out_made, both(i, s))
                    nc.vector.tensor_tensor(c.X[:, bass.ds(i + s, 1), :].rearrange("p o d -> p (o d)"), bank(s, 1)[:, 0:P],
                                            b2[:, bass.ds(which[s] * P, P)], ALU.add).then_inc(out_kept, 1)


def combine(nc, c, name, out=None):
    with ExitStack() as ctx:
        take = signals(nc, ctx)
        sem = lambda n: take(f"{name}_{n}")
        gathered = [sem(f"gathered_{n}") for n in range(2)]
        added, stored = sem("added"), sem("stored")
        block = ctx.enter_context(nc.Block())

        @block.gpsimd
        def _(pool):
            for g in range(GROUPS_OF_TILES):
                if g >= 2:
                    pool.wait_ge(gathered[g % 2], g // 2 * GROUP * 16)
                for t in range(g * GROUP, (g + 1) * GROUP):
                    pool.indirect_dma_start(out=c.X[:, t, :], out_offset=None, in_=c.sorted_out,
                                            in_offset=bass.IndirectOffsetOnAxis(ap=c.row_of[:, t:t + 1], axis=0)
                                            ).then_inc(gathered[g % 2], 16)

        @block.vector
        def _(dve):
            with dve.Fori(0, TILES - 2 * GROUP + 1, 2 * GROUP) as t:
                for n in range(2):
                    dve.wait_ge(gathered[n], (t + 2 * GROUP) * 8)
                    for j in range(GROUP):
                        at = t + (n * GROUP + j)
                        row = lambda a: a[:, bass.ds(at, 1), :].rearrange("p o d -> p (o d)")
                        last = nc.vector.scalar_tensor_tensor(row(c.H), row(c.X), c.weight[:, bass.ds(at, 1)], row(c.H), ALU.mult, ALU.add)
                    last.then_inc(added, GROUP)

        @block.sync
        def _(sp):
            if out is not None:
                rows = out.rearrange("b (t p) d -> p (b t) d", p=P)
                with sp.Fori(0, TILES - GROUP + 1, GROUP) as t:
                    sp.wait_ge(added, t + GROUP)
                    sp.dma_start(rows[:, bass.ds(t, GROUP), :], c.H[:, bass.ds(t, GROUP), :]).then_inc(stored, 16)
                sp.wait_ge(stored, GROUPS_OF_TILES * 16)


INNER = 256
STATE = 64
DIRS = 2
MHEADS = INNER // HEAD
CONV = 4
MIX = 6
ATANH = [1.0 / (2 * k + 1) for k in range(8, 0, -1)]


def mamba(nc, c, ins):
    with ExitStack() as ctx:
        one = lambda n, shape: ctx.enter_context(nc.sbuf_tensor(f"mamba_{n}", shape, F32))
        sb = lambda n, shape: [one(f"{n}_{s}", shape) for s in range(2)]
        take = signals(nc, ctx)
        sem = lambda n: take(f"mamba_{n}")
        m = Chip()
        m.loaded, m.negated, m.joined, m.stats, m.rstd, m.normed, m.uT = map(sem, (
            "loaded", "negated", "joined", "stats", "rstd", "normed", "uT"))
        m.uT_kept, m.bc_mixed, m.x_mixed, m.x_kept, m.started, m.convolved, m.bc_kept = map(sem, (
            "uT_kept", "bc_mixed", "x_mixed", "x_kept", "started", "convolved", "bc_kept"))
        m.gated, m.gated_kept, m.g_made, m.g_kept, m.dt_raw, m.dt_exp, m.dt_ready = map(sem, (
            "gated", "gated_kept", "g_made", "g_kept", "dt_raw", "dt_exp", "dt_ready"))
        m.steps, m.xT, m.xT_kept, m.bT_kept, m.reach, m.reach_kept, m.ends_kept = map(sem, (
            "steps", "xT", "xT_kept", "bT_kept", "reach", "reach_kept", "ends_kept"))
        m.state, m.state_kept, m.carried, m.carried_kept, m.span0, m.span0_exp, m.span1 = map(sem, (
            "state", "state_kept", "carried", "carried_kept", "span0", "span0_exp", "span1"))
        m.span1_exp, m.weights0, m.weights1, m.weights0b, m.weights1b, m.y0, m.y1 = map(sem, (
            "span1_exp", "weights0", "weights1", "weights0b", "weights1b", "y0", "y1"))
        m.yz, m.sums, m.y_rstd, m.yzT, m.yzT_kept, m.projected, m.done = map(sem, (
            "yz", "sums", "y_rstd", "yzT", "yzT_kept", "projected", "done"))
        w_in = one("w_in", [P, MIX * P + 2 * INNER + 2 * MHEADS])
        w_mix = w_in[:, 0:MIX * P]
        w_z = w_in[:, MIX * P:MIX * P + 2 * INNER]
        w_dt = w_in[:, MIX * P + 2 * INNER:]
        taps = one("taps", [P, MIX, CONV])
        tap_bias = one("tap_bias", [P, MIX])
        columns = one("columns", [P, 9])
        dt_bias = one("dt_bias", [P, 2 * MHEADS])
        decay = one("decay", [P, 2 * MHEADS])
        skip = one("skip", [P, 4, P])
        out_w = one("out_w", [P, 4 * P])
        projT = one("projT", [P, 2 * P])
        w_out = one("w_out", [P, 4, P])
        w_taps = one("w_taps", [P, CONV, 4 * P])
        inv = one("inv", [P, 2])
        two = one("two", [P, 16])
        minus_one = one("minus_one", [P, 16])
        masks = one("masks", [P, 4, P])
        before, after, upto, since = (masks[:, k, :] for k in range(4))
        x1 = sb("x1", [P, SEQ_TILES, P])
        u = sb("u", [P, SEQ_TILES, P])
        uT = sb("uT", [P, SEQ_TILES * P])
        mix = sb("mix", [P, MIX, SEQ_TILES * P])
        z = sb("z", [P, SEQ_TILES, DIRS * INNER])
        g = sb("g", [P, SEQ_TILES, DIRS, P])
        dtx = sb("dtx", [P, SEQ_TILES, DIRS * INNER])
        dtxe = sb("dtxe", [P, DIRS, INNER])
        bT = sb("bT", [P, DIRS, P])
        steps = sb("steps", [P, SEQ_TILES, DIRS, MHEADS * P])
        weights = sb("weights", [P, DIRS, MHEADS * P])
        reach = sb("reach", [P, 4, MHEADS])
        state = sb("state", [P, INNER])
        carried = sb("carried", [P, DIRS, INNER])
        yz = sb("yz", [P, SEQ_TILES, DIRS * INNER])
        yzT = sb("yzT", [P, SEQ_TILES, 4, P])
        junk = sb("junk", [P, INNER])
        sums = sb("sums", [P, SEQ_TILES * DIRS])
        rnorm = sb("rnorm", [P, SEQ_TILES])
        norm = [NormBuffers(nc, ctx, f"mamba_norm_{s}") for s in range(2)]
        n_dt = 2 * SEQ_TILES * 2 * MHEADS
        dt_raw, dt_neg, dt_exp, dt_rec, dt_z, dt_z2, dt_p, dt, step_log = (one(n, [P, n_dt]) for n in (
            "dt_raw", "dt_neg", "dt_exp", "dt_rec", "dt_z", "dt_z2", "dt_p", "dt", "step_log"))
        dt_of = lambda a, s: a[:, s * 16:(s + 1) * 16].rearrange("p (t d h) -> p t d h", t=2, d=2)
        part = lambda s: bass.ts(s, 16)
        bank = lambda s, b: c.PS[:, 4 * s + b, :]
        banks = lambda s, b, n: c.PS[:, 4 * s + b:4 * s + b + n, :]
        mixed = lambda s, b: bank(s, 1 + b // 2)[:, (b % 2) * 256:(b % 2) * 256 + 256]
        EYE = c.ident

        with nc.Block() as block:
            loads = [(w_in[:, :], "m_w_in"), (taps[:, :, :], "m_taps"), (tap_bias[:, :], "m_tap_bias"), (columns[:, :], "m_columns"),
                     (out_w[:, :], "m_out_w"), (projT[:, :], "m_projT"), (masks[:, :, :], "m_masks")]
            LOADED = (len(loads) + 3) * 16

            @block.sync
            def _(sp):
                for at, name in loads:
                    sp.dma_start(at, ins[name]).then_inc(m.loaded, 16)
                sp.dma_start(dt_bias[:, :], broadcast_rows(ins["m_dt_bias"], 8)).then_inc(m.loaded, 16)
                sp.dma_start(decay[:, :], broadcast_rows(ins["m_A_log"], 8)).then_inc(m.loaded, 16)
                sp.dma_start(w_taps[:, :, :].rearrange("p k n -> p (k n)"), broadcast_rows(ins["m_tap_rows"], CONV * 4 * P)).then_inc(m.loaded, 16)
                sp.wait_ge(m.loaded, LOADED)

            @block.scalar
            def _(act):
                act.wait_ge(m.loaded, LOADED)
                nc.scalar.activation(decay[:, :], decay[:, :], ACT.Exp).then_inc(m.negated, 1)

            @block.tensor
            def _(pe):
                pe.wait_ge(m.loaded, LOADED)
                for b in range(4):
                    last = nc.tensor.matmul(c.PS[:, 0, bass.ts(b, P)], out_w[:, bass.ts(b, P)], projT[:, bass.ts(b // 2, P)], start=True, stop=True)
                last.then_inc(m.joined, 1)

            @block.vector
            def _(dve):
                dve.wait_ge(m.loaded, LOADED)
                nc.vector.tensor_scalar(w_in[:, :], w_in[:, :], columns[:, 0:1], None, ALU.mult)
                for b in range(4):
                    nc.vector.tensor_scalar(skip[:, b, :], EYE[:, :], columns[:, 1 + b:2 + b], None, ALU.mult)
                nc.vector.memset(inv[:, :], 1.0 / INNER)
                nc.vector.memset(two[:, :], 2.0)
                nc.vector.memset(minus_one[:, :], -1.0)
                dve.drain()
                for k in range(CONV):
                    nc.vector.tensor_tensor(w_taps[:, k, :], w_taps[:, k, :], w_mix[:, 0:4 * P], ALU.mult)
                dve.wait_ge(m.negated, 1)
                nc.vector.tensor_scalar(decay[:, :], decay[:, :], -1.0, None, ALU.mult)
                dve.wait_ge(m.joined, 1)
                for b in range(4):
                    nc.vector.tensor_scalar(w_out[:, b, :], c.PS[:, 0, bass.ts(b, P)], columns[:, 5 + b:6 + b], None, ALU.mult)
                dve.drain()

        block = ctx.enter_context(nc.Block())

        @block.tensor
        def _(pe):
            mm = nc.tensor.matmul

            def spans(s, t):
                for d in range(2):
                    last = mm(bank(s, 3 * d), (after, before)[d], steps[s][:, t, d, :], start=True, stop=True)
                return last

            def outputs(s, t):
                for b in range(4):
                    out = bank(s, 1 + t)[:, bass.ts(b, P)]
                    mm(out, mix[s][:, b, bass.ts(t, P)], skip[:, b, :], start=True, stop=False)
                    for h in range(2):
                        last = mm(out[:, bass.ts(h, HEAD)], weights[s][:, b // 2, bass.ts(2 * (b % 2) + h, P)],
                                  dtx[s][:, t, b * P + h * HEAD:b * P + (h + 1) * HEAD], start=False, stop=h == 1)
                return last

            def first(i, s):
                yield 4.5
                pe.wait_ge(m.normed, both(i, s))
                for t in range(2):
                    last = nc.tensor.transpose(bank(s, 0)[:, bass.ts(t, P)], u[s][:, t, :], EYE[:, :])
                last.then_inc(m.uT, 1)
                yield 5.4
                pe.wait_ge(m.uT_kept, both(i, s))
                for t in range(2):
                    mm(bank(s, 0)[:, 256 + 8 * t:264 + 8 * t], uT[s][:, bass.ts(t, P)], w_dt, start=True, stop=True)
                for b in (4, 5):
                    last = mm(mixed(s, b), w_mix[:, bass.ts(b, P)], uT[s][:, :], start=True, stop=True)
                last.then_inc(m.bc_mixed, 1)
                n = SEQ_TILES * P
                for b in range(4):
                    for k in range(CONV):
                        to, of = (slice(k, n), slice(0, n - k)) if b < 2 else (slice(0, n - k), slice(k, n))
                        last = mm(mixed(s, b)[:, to], w_taps[:, k, bass.ts(b, P)], uT[s][:, of], start=k == 0, stop=k == CONV - 1)
                last.then_inc(m.x_mixed, 1)
                yield 17.1
                pe.wait_ge(m.x_kept, both(i, s))
                for t in range(2):
                    last = mm(bank(s, 1 + t), uT[s][:, bass.ts(t, P)], w_z, start=True, stop=True)
                last.then_inc(m.gated, 1)
                yield 20.6
                pe.wait_ge(m.bc_kept, both(i, s))
                pe.wait_ge(m.dt_raw, both(i, s))
                for t in range(2):
                    for d in range(2):
                        r = bass.ts(d, STATE)
                        last = mm(bank(s, 3 - 3 * d)[:, bass.ts(t, P)], mix[s][r, 4, bass.ts(t, P)], mix[s][r, 5, bass.ts(t, P)], start=True, stop=True)
                last.then_inc(m.g_made, 1)
                yield 22.5
                pe.wait_ge(m.gated_kept, both(i, s))
                pe.wait_ge(m.g_kept, both(i, s))
                for t in range(2):
                    nc.tensor.transpose(bank(s, 3)[:, bass.ts(t, P)], mix[s][:, 4, bass.ts(t, P)], EYE[:, :])
                for t in range(2):
                    for b in range(4):
                        last = nc.tensor.transpose(bank(s, 1 + t)[:, bass.ts(b, P)], mix[s][:, b, bass.ts(t, P)], EYE[:, :])
                last.then_inc(m.xT, 1)
                yield 23.8
                pe.wait_ge(m.dt_ready, both(i, s))
                a = dt_of(step_log, s)
                for k, (mask, t, d) in enumerate(((upto, 1, 0), (since, 0, 1), (after, 0, 0), (before, 1, 1))):
                    last = mm(bank(s, 0)[:, bass.ts(k, MHEADS)], mask, a[:, t, d, :], start=True, stop=True)
                last.then_inc(m.reach, 1)
                yield 26.9
                pe.wait_ge(m.ends_kept, both(i, s))
                pe.wait_ge(m.bT_kept, both(i, s))
                for d in range(2):
                    last = mm(c.PS[bass.ts(d, STATE), 4 * s + 3, 0:INNER], bT[s][:, d, bass.ts(d, STATE)], dtxe[s][:, d, :], start=True, stop=True)
                last.then_inc(m.state, 1)

            def second(i, s):
                yield 1
                pe.wait_ge(m.state_kept, both(i, s))
                for d in range(2):
                    r = bass.ts(d, STATE)
                    last = mm(bank(s, 3 * d)[:, 0:INNER], mix[s][r, 5, bass.ts(1 - d, P)], state[s][r, :], start=True, stop=True)
                last.then_inc(m.carried, 1)
                yield 2.5
                pe.wait_ge(m.steps, both(i, s))
                pe.wait_ge(m.carried_kept, both(i, s))
                pe.wait_ge(m.reach_kept, both(i, s))
                spans(s, 0).then_inc(m.span0, 1)
                yield 8
                pe.wait_ge(m.weights0, both(i, s))
                pe.wait_ge(m.weights0b, both(i, s))
                pe.wait_ge(m.xT_kept, both(i, s))
                outputs(s, 0).then_inc(m.y0, 1)
                yield 10.7
                pe.wait_ge(m.span0_exp, both(i, s))
                spans(s, 1).then_inc(m.span1, 1)
                yield 16.2
                pe.wait_ge(m.weights1, both(i, s))
                pe.wait_ge(m.weights1b, both(i, s))
                outputs(s, 1).then_inc(m.y1, 1)
                yield 21.6
                pe.wait_ge(m.yz, both(i, s))
                for t in range(2):
                    for b in range(4):
                        last = nc.tensor.transpose(bank(s, 1 + t)[:, bass.ts(b, P)], yz[s][:, t, bass.ts(b, P)], EYE[:, :])
                last.then_inc(m.yzT, 1)
                yield 25.2
                pe.wait_ge(m.yzT_kept, both(i, s))
                for t in range(2):
                    for d in range(2):
                        for b in range(2):
                            last = mm(bank(s, 3)[:, bass.ts(2 * t + d, P)], yzT[s][:, t, 2 * d + b, :], w_out[:, 2 * d + b, :], start=b == 0, stop=b == 1)
                last.then_inc(m.projected, 1)

            skewed(pe, first, second)

        @block.scalar
        def _(act):
            a = nc.scalar.activation
            def first(i, s):
                yield 6.5
                act.wait_ge(m.bc_mixed, both(i, s))
                for b in (4, 5):
                    last = a(mix[s][:, b, :], mixed(s, b), ACT.Identity, bias=tap_bias[:, b:b + 1], scale=taps[:, b, CONV - 1:CONV])
                last.then_inc(m.started, 1)
                yield 7.4
                act.wait_ge(m.dt_raw, both(i, s))
                a(dt_exp[:, part(s)], dt_neg[:, part(s)], ACT.Exp).then_inc(m.dt_exp, 1)
                yield 14
                act.wait_ge(m.x_mixed, both(i, s))
                for b in range(4):
                    last = a(mix[s][:, b, :], mixed(s, b), ACT.Silu, bias=tap_bias[:, b:b + 1])
                last.then_inc(m.x_kept, 1)
                yield 17.1
                act.wait_ge(m.convolved, both(i, s))
                a(mix[s][:, 4:, :], mix[s][:, 4:, :], ACT.Silu).then_inc(m.bc_kept, 1)
                yield 20.6
                act.wait_ge(m.gated, both(i, s))
                a(z[s][:, :, :], banks(s, 1, 2), ACT.Silu).then_inc(m.gated_kept, 1)
                yield 24.2
                act.wait_ge(m.reach, both(i, s))
                a(reach[s][:, :, :], bank(s, 0)[:, 0:16].rearrange("p (k h) -> p k h", h=MHEADS), ACT.Exp).then_inc(m.reach_kept, 1)

            def second(i, s):
                yield 0.5
                act.wait_ge(m.state, both(i, s))
                a(state[s][:, :], bank(s, 3)[:, 0:INNER], ACT.Copy).then_inc(m.state_kept, 1)
                yield 2.93
                act.wait_ge(m.span0, both(i, s))
                for d in range(2):
                    last = a(weights[s][:, d, :], bank(s, 3 * d), ACT.Exp)
                last.then_inc(m.span0_exp, 1)
                yield 12.5
                act.wait_ge(m.span1, both(i, s))
                act.wait_ge(m.y0, both(i, s))
                for d in range(2):
                    last = a(weights[s][:, d, :], bank(s, 3 * d), ACT.Exp)
                last.then_inc(m.span1_exp, 1)
                yield 19.27
                act.wait_ge(m.yz, both(i, s))
                for t in range(2):
                    for d in range(2):
                        k = 2 * t + d
                        a(junk[s][:, :], yz[s][:, t, bass.ts(d, INNER)], ACT.Square, accum_out=sums[s][:, k:k + 1])
                        act.drain()
                a(sums[s][:, :], sums[s][:, :], ACT.Copy).then_inc(m.sums, 1)
                yield 23.3
                act.wait_ge(m.yzT, both(i, s))
                a(yzT[s][:, :, :, :].rearrange("p t b n -> p t (b n)"), banks(s, 1, 2), ACT.Copy).then_inc(m.yzT_kept, 1)

            skewed(act, first, second)

        @block.gpsimd
        def _(pool):
            tt = nc.gpsimd.tensor_tensor
            def first(i, s):
                yield 0.8
                pool.wait_ge(m.stats, both(i, s))
                norm_rstd(nc, pool, c, norm[s])
                pool.drain()
                r, q = norm[s].rstd[:, :], rnorm[s][:, :]
                tt(q, norm[s].stat[:, :, 1], r, ALU.mult)
                pool.drain()
                tt(q, q, r, ALU.mult)
                pool.drain()
                tt(q, q, c.eps[:, 0:2], ALU.add)
                pool.drain()
                tt(q, q, c.minus_half[:, 0:2], ALU.pow)
                pool.drain()
                tt(q, q, r, ALU.mult).then_inc(m.rstd, 1)
                yield 9
                pool.wait_ge(m.dt_exp, both(i, s))
                rec, z1, z2, p, x = (one_[:, part(s)] for one_ in (dt_rec, dt_z, dt_z2, dt_p, dt_raw))
                tt(rec, dt_exp[:, part(s)], two[:, :], ALU.add)
                pool.drain()
                tt(rec, rec, minus_one[:, :], ALU.pow)
                pool.drain()
                tt(z1, dt_exp[:, part(s)], rec, ALU.mult)
                pool.drain()
                tt(z2, z1, z1, ALU.mult)
                pool.drain()
                nc.gpsimd.tensor_scalar(p, z2, ATANH[0], None, ALU.mult)
                for k in ATANH[1:] + [1.0]:
                    pool.drain()
                    nc.gpsimd.tensor_scalar(p, p, k, None, ALU.add)
                    pool.drain()
                    tt(p, p, z2 if k < 1.0 else z1, ALU.mult)
                nc.gpsimd.tensor_scalar(x, x, 0.0, None, ALU.max)
                pool.drain()
                tt(x, x, p, ALU.add)
                pool.drain()
                tt(dt[:, part(s)], x, p, ALU.add)
                pool.drain()
                tt(step_log[:, part(s)].rearrange("p (t n) -> p t n", n=8), dt[:, part(s)].rearrange("p (t n) -> p t n", n=8),
                   decay[:, :].unsqueeze(1).to_broadcast([P, 2, 8]), ALU.mult).then_inc(m.dt_ready, 1)
                pool.drain()
                yield 18.1
                for t in range(2):
                    for d in range(2):
                        last = tt(steps[s][:, t, d, :].rearrange("p (h n) -> p h n", h=MHEADS),
                                  (upto, since)[d].unsqueeze(1).to_broadcast([P, MHEADS, P]),
                                  dt_of(step_log, s)[:, t, d, :].unsqueeze(2).to_broadcast([P, MHEADS, P]), ALU.mult)
                last.then_inc(m.steps, 1)

            def second(i, s):
                yield 4.41
                pool.wait_ge(m.span0_exp, both(i, s))
                w = weights[s][:, 1, :].rearrange("p (h n) -> p h n", h=MHEADS)
                tt(w, w, g[s][:, 0, 1, :].unsqueeze(1).to_broadcast([P, MHEADS, P]), ALU.mult).then_inc(m.weights0b, 1)
                yield 14.8
                pool.wait_ge(m.span1_exp, both(i, s))
                w = weights[s][:, 1, :].rearrange("p (h n) -> p h n", h=MHEADS)
                tt(w, w, g[s][:, 1, 1, :].unsqueeze(1).to_broadcast([P, MHEADS, P]), ALU.mult).then_inc(m.weights1b, 1)
                yield 23.3
                pool.wait_ge(m.sums, both(i, s))
                q = sums[s][:, :]
                tt(q, q, inv[:, 0:1].to_broadcast([P, 4]), ALU.mult)
                pool.drain()
                tt(q, q, c.eps[:, :], ALU.add)
                pool.drain()
                tt(q, q, c.minus_half[:, :], ALU.pow).then_inc(m.y_rstd, 1)

            skewed(pool, first, second)

        @block.vector
        def _(dve):
            v = nc.vector
            row = lambda a, t: a[:, bass.ds(t, 1), :].rearrange("p o d -> p (o d)")
            def first(i, s):
                yield 0
                for t in range(2):
                    v.bn_stats(norm[s].sums[:, t, :], row(c.H, (i + s) * 2 + t))
                dve.drain()
                for t in range(2):
                    last = v.bn_aggr(norm[s].stat[:, t, :], norm[s].sums[:, t, :])
                last.then_inc(m.stats, 1)
                yield 3.4
                dve.wait_ge(m.rstd, both(i, s))
                for t in range(2):
                    mean = norm[s].stat[:, t, 0:1]
                    v.tensor_scalar(x1[s][:, t, :], row(c.H, (i + s) * 2 + t), mean, norm[s].rstd[:, t:t + 1], ALU.subtract, ALU.mult)
                    last = v.tensor_scalar(u[s][:, t, :], row(c.H, (i + s) * 2 + t), mean, rnorm[s][:, t:t + 1], ALU.subtract, ALU.mult)
                last.then_inc(m.normed, 1)
                yield 4.9
                dve.wait_ge(m.uT, both(i, s))
                v.tensor_copy(uT[s][:, :], bank(s, 0)[:, 0:256]).then_inc(m.uT_kept, 1)
                yield 6.5
                dve.wait_ge(m.bc_mixed, both(i, s))
                v.tensor_tensor(dt_raw[:, part(s)].rearrange("p (t n) -> p t n", t=2), bank(s, 0)[:, 256:272].rearrange("p (t n) -> p t n", t=2),
                                dt_bias[:, :].unsqueeze(1).to_broadcast([P, 2, 8]), ALU.add)
                dve.drain()
                v.scalar_tensor_tensor(dt_neg[:, part(s)], dt_raw[:, part(s)], -1.0, dt_raw[:, part(s)], ALU.mult, ALU.min).then_inc(m.dt_raw, 1)
                yield 7.4
                dve.wait_ge(m.started, both(i, s))
                for k in range(1, CONV):
                    for b in (4, 5):
                        src = mixed(s, b)
                        for d, r in ((0, slice(0, 64)), (1, slice(64, P))):
                            n = SEQ_TILES * P
                            to, of = (slice(k, n), slice(0, n - k)) if d == 0 else (slice(0, n - k), slice(k, n))
                            last = v.scalar_tensor_tensor(mix[s][r, b, to], src[r, of], taps[r, b, CONV - 1 - k:CONV - k], mix[s][r, b, to], ALU.mult, ALU.add)
                    if k < CONV - 1:
                        dve.drain()
                last.then_inc(m.convolved, 1)
                yield 21.2
                dve.wait_ge(m.g_made, both(i, s))
                for d in range(2):
                    last = v.tensor_tensor(g[s][:, :, d, :], bank(s, 3 - 3 * d)[:, 0:256].rearrange("p (t n) -> p t n", t=2),
                                           (upto, since)[d].unsqueeze(1).to_broadcast([P, 2, P]), ALU.mult)
                last.then_inc(m.g_kept, 1)
                yield 23.8
                dve.wait_ge(m.xT, both(i, s))
                dve.wait_ge(m.dt_ready, both(i, s))
                v.tensor_copy(bT[s][:, :, :], bank(s, 3)[:, 0:256].rearrange("p (t n) -> p t n", t=2)).then_inc(m.bT_kept, 1)
                v.tensor_tensor(dtx[s][:, :, :].rearrange("p t (h d) -> p (t h) d", d=HEAD), banks(s, 1, 2).rearrange("p t (h d) -> p (t h) d", d=HEAD),
                                dt[:, part(s)].unsqueeze(2).to_broadcast([P, 16, HEAD]), ALU.mult).then_inc(m.xT_kept, 1)
                yield 26
                dve.drain()
                dve.wait_ge(m.reach_kept, both(i, s))
                for d in range(2):
                    last = v.tensor_tensor(dtxe[s][:, d, :].rearrange("p (h d) -> p h d", d=HEAD), dtx[s][:, d, bass.ts(d, INNER)].rearrange("p (h d) -> p h d", d=HEAD),
                                           reach[s][:, 2 + d, :].unsqueeze(2).to_broadcast([P, MHEADS, HEAD]), ALU.mult)
                last.then_inc(m.ends_kept, 1)

            def second(i, s):
                yield 1.6
                dve.wait_ge(m.carried, both(i, s))
                for d in range(2):
                    last = v.tensor_tensor(carried[s][:, d, :].rearrange("p (h d) -> p h d", d=HEAD), bank(s, 3 * d)[:, 0:INNER].rearrange("p (h d) -> p h d", d=HEAD),
                                           reach[s][:, d, :].unsqueeze(2).to_broadcast([P, MHEADS, HEAD]), ALU.mult)
                last.then_inc(m.carried_kept, 1)
                yield 6.6
                dve.wait_ge(m.span0_exp, both(i, s))
                w = weights[s][:, 0, :].rearrange("p (h n) -> p h n", h=MHEADS)
                v.tensor_tensor(w, w, g[s][:, 0, 0, :].unsqueeze(1).to_broadcast([P, MHEADS, P]), ALU.mult).then_inc(m.weights0, 1)
                yield 14.8
                dve.wait_ge(m.span1_exp, both(i, s))
                w = weights[s][:, 0, :].rearrange("p (h n) -> p h n", h=MHEADS)
                v.tensor_tensor(w, w, g[s][:, 1, 0, :].unsqueeze(1).to_broadcast([P, MHEADS, P]), ALU.mult).then_inc(m.weights1, 1)
                yield 18.9
                dve.wait_ge(m.y0, both(i, s))
                dve.wait_ge(m.y1, both(i, s))
                for t in range(2):
                    at = bass.ts(1 - t, INNER)
                    v.tensor_tensor(yz[s][:, t, at], bank(s, 1 + t)[:, at], carried[s][:, 1 - t, :], ALU.add)
                    other = bass.ts(t, INNER)
                    v.tensor_tensor(yz[s][:, t, other], bank(s, 1 + t)[:, other], z[s][:, t, other], ALU.mult)
                dve.drain()
                for t in range(2):
                    at = bass.ts(1 - t, INNER)
                    last = v.tensor_tensor(yz[s][:, t, at], yz[s][:, t, at], z[s][:, t, at], ALU.mult)
                last.then_inc(m.yz, 1)
                yield 27
                dve.wait_ge(m.projected, both(i, s))
                dve.wait_ge(m.y_rstd, both(i, s))
                for d in range(2):
                    for t in range(2):
                        k = 2 * t + d
                        v.scalar_tensor_tensor(x1[s][:, t, :], bank(s, 3)[:, bass.ts(k, P)], sums[s][:, k:k + 1], x1[s][:, t, :], ALU.mult, ALU.add)
                    dve.drain()
                here = bass.ds((i + s) * 2, 2)
                v.tensor_tensor(c.H[:, here, :], c.H[:, here, :], x1[s][:, :, :], ALU.add).then_inc(m.done, 1)

            skewed(dve, first, second)


AHEADS, AHEAD = 8, 16
GROUPS = 2
LANE = 32


def attention(nc, c, ins, prefetch=lambda sp: None):
    with ExitStack() as ctx:
        one = lambda n, shape: ctx.enter_context(nc.sbuf_tensor(f"attention_{n}", shape, F32))
        sb = lambda n, shape: [one(f"{n}_{s}", shape) for s in range(2)]
        take = signals(nc, ctx)
        sem = lambda n: take(f"attention_{n}")
        m = Chip()
        m.loaded, m.cleared, m.stats, m.rstd, m.normed, m.xT, m.xT_kept = map(sem, (
            "loaded", "cleared", "stats", "rstd", "normed", "xT", "xT_kept"))
        m.qk_made, m.qk_kept, m.k_kept, m.v_made, m.v_kept, m.top_kept0, m.top_kept1 = map(sem, (
            "qk_made", "qk_kept", "k_kept", "v_made", "v_kept", "top_kept0", "top_kept1"))
        m.scored0, m.scored1, m.topT, m.q_shifted, m.summed0, m.summed1, m.raw_kept0 = map(sem, (
            "scored0", "scored1", "topT", "q_shifted", "summed0", "summed1", "raw_kept0"))
        m.raw_kept1, m.sums_spread0, m.sums_spread1, m.oT_kept, m.projected, m.xb_ready, m.done = map(sem, (
            "raw_kept1", "sums_spread0", "sums_spread1", "oT_kept", "projected", "xb_ready", "done"))
        spread = [sem(f"spread_{h}") for h in range(AHEADS)]
        exps = [sem(f"exps_{h}") for h in range(AHEADS)]
        w_q = one("w_q", [P, GROUPS * P])
        w_k = one("w_k", [P, GROUPS * P])
        w_v = one("w_v", [P, P])
        w_o = one("w_o", [P, GROUPS, P])
        lane_sums = one("lane_sums", [P, P])
        b_q = one("b_q", [1, GROUPS * P])
        b_k = one("b_k", [1, GROUPS * P])
        b_v = one("b_v", [1, P])
        b_o = one("b_o", [P, P])
        x3 = sb("x3", [P, SEQ_TILES, P])
        xb = sb("xb", [P, SEQ_TILES, P])
        xT = sb("xT", [P, SEQ_TILES * P])
        q = sb("q", [P, GROUPS, SEQ_TILES * P])
        k = sb("k", [P, GROUPS, 4, SEQ_TILES * P])
        v = sb("v", [P, SEQ_TILES, AHEADS, LANE])
        top = sb("top", [P, SEQ_TILES, GROUPS, 4, LANE])
        probs = sb("probs", [P, AHEADS, SEQ_TILES, SEQ_TILES * P])
        raw = sb("raw", [P, GROUPS * SEQ_TILES * P])
        share = sb("share", [P, GROUPS * SEQ_TILES * P])
        oT = sb("oT", [P, GROUPS, SEQ_TILES * P])
        norm = [NormBuffers(nc, ctx, f"attention_norm_{s}") for s in range(2)]
        bank = lambda s, b: c.PS[:, 4 * s + b, :]
        banks = lambda s, b, n: c.PS[:, 4 * s + b:4 * s + b + n, :]
        EYE = c.ident
        SCALE = AHEAD ** -0.5
        LAG = 2

        with nc.Block() as block:
            lanes = lambda a: a.rearrange("p (h n) -> p h n", n=LANE)[:, :, 0:AHEAD]

            @block.sync
            def _(sp):
                sp.wait_ge(m.cleared, 1)
                for at, name in ((w_q, "Wq"), (w_k, "Wk")):
                    sp.dma_start(lanes(at[:, :]), ins[f"L1_ffn_{name}"].rearrange("p (h n) -> p h n", n=AHEAD)).then_inc(m.loaded, 16)
                sp.dma_start(w_v[:, :], ins["L1_ffn_Wv"]).then_inc(m.loaded, 16)
                sp.dma_start(lane_sums[:, :], ins["lane_sums"]).then_inc(m.loaded, 16)
                for j in range(4):
                    sp.dma_start(w_o[LANE * j:LANE * j + AHEAD, :, :],
                                 ins["L1_ffn_Wo"].rearrange("(g j f) d -> j f g d", g=GROUPS, f=AHEAD)[j]).then_inc(m.loaded, 16)
                for at, name in ((b_q, "bq"), (b_k, "bk")):
                    a = ins[f"L1_ffn_{name}"]
                    sp.dma_start(lanes(at[:, :]), bass.AP(a.tensor, a.offset, [[0, 1], [AHEAD, AHEADS], [1, AHEAD]])).then_inc(m.loaded, 16)
                sp.dma_start(b_v[:, :], ins["L1_ffn_bv"].rearrange("(o d) -> o d", o=1)).then_inc(m.loaded, 16)
                sp.dma_start(b_o[:, :], broadcast_rows(ins["L1_ffn_bo"], P)).then_inc(m.loaded, 16)
                sp.wait_ge(m.loaded, 12 * 16)

            @block.vector
            def _(dve):
                for a in (w_q, w_k, b_q, b_k):
                    nc.vector.memset(a[:, :], 0.0)
                nc.vector.memset(w_o[:, :, :], 0.0)
                dve.drain()
                nc.vector.memset(b_k[:, :].rearrange("p (h n) -> p h n", n=LANE)[:, :, AHEAD:AHEAD + 1], 1.0).then_inc(m.cleared, 1)
        with ExitStack() as inner:
            fold_norm(nc, c, inner, "attention",
                      [(w_q[:, :], None, None, b_q[:, :], 0), (w_k[:, :], None, None, b_k[:, :], 0), (w_v[:, :], None, None, b_v[:, :], 0)],
                      m.loaded, 12 * 16)

        block = ctx.enter_context(nc.Block())

        @block.sync
        def _(sp):
            prefetch(sp)

        lane = lambda j: slice(LANE * j, LANE * (j + 1))

        @block.tensor
        def _(pe):
            mm = nc.tensor.matmul

            def scores(i, s, g):
                for t in range(2):
                    for pair in range(2):
                        last = mm(bank(s, 2 * t + pair), q[s][:, g, bass.ts(t, P)], k[s][:, g, 2 * pair:2 * pair + 2, :].rearrange("p j n -> p (j n)"),
                                  start=True, stop=True)
                return last

            def first(i, s):
                yield 3
                pe.wait_ge(m.normed, both(i, s))
                for t in range(2):
                    last = nc.tensor.transpose(bank(s, 0)[:, bass.ts(t, P)], x3[s][:, t, :], EYE[:, :])
                last.then_inc(m.xT, 1)
                yield 4
                pe.wait_ge(m.xT_kept, both(i, s))
                for g in range(GROUPS):
                    mm(bank(s, 1)[:, g * 256:(g + 1) * 256], w_q[:, bass.ts(g, P)], xT[s][:, :], start=True, stop=True)
                    last = mm(bank(s, 2)[:, g * 256:(g + 1) * 256], w_k[:, bass.ts(g, P)], xT[s][:, :], start=True, stop=True)
                last.then_inc(m.qk_made, 1)
                for t in range(2):
                    last = mm(bank(s, 3)[:, bass.ts(t, P)], xT[s][:, bass.ts(t, P)], w_v[:, :], start=True, stop=True)
                last.then_inc(m.v_made, 1)
                yield 7
                pe.wait_ge(m.qk_kept, both(i, s))
                pe.wait_ge(m.k_kept, both(i, s))
                pe.wait_ge(m.v_kept, both(i, s))
                scores(i, s, 0).then_inc(m.scored0, 1)
                yield 13
                pe.wait_ge(m.top_kept0, both(i, s))
                scores(i, s, 1).then_inc(m.scored1, 1)
                yield 18.7
                pe.wait_ge(m.top_kept1, both(i, s))
                for g in range(GROUPS):
                    for t in range(2):
                        last = nc.tensor.transpose(bank(s, 0)[:, (2 * g + t) * P:(2 * g + t + 1) * P],
                                                   top[s][:, t, g, :, :].rearrange("p j n -> p (j n)"), EYE[:, :])
                last.then_inc(m.topT, 1)

            def second(i, s):
                def spread_sums(g):
                    return mm(bank(s, 3 - g)[:, 256:], lane_sums[:, :], raw[s][:, g * 256:(g + 1) * 256], start=True, stop=True)

                for h in range(AHEADS + LAG):
                    yield 0.2 + 1.8 * h
                    if h < AHEADS:
                        g, j = divmod(h, 4)
                        if h == 0:
                            pe.wait_ge(m.q_shifted, both(i, s))
                        if h >= 2:
                            pe.wait_ge(exps[h - 2], both(i, s))
                        for t in range(2):
                            last = mm(bank(s, h % 2)[:, t * 256:(t + 1) * 256], k[s][:, g, j, bass.ts(t, P)], q[s][:, g, :], start=True, stop=True)
                        last.then_inc(spread[h], 1)
                    if h >= LAG:
                        g, j = divmod(h - LAG, 4)
                        pe.wait_ge(exps[h - LAG], both(i, s))
                        for n in range(2):
                            last = mm(c.PS[lane(j), 4 * s + 3 - g, 0:256], v[s][:, n, h - LAG, :],
                                      probs[s][:, h - LAG, n, :], start=n == 0, stop=n == 1)
                        if h - LAG in (3, 7):
                            last.then_inc((m.summed0, m.summed1)[g], 1)
                    if h == 4 + LAG:
                        pe.wait_ge(m.raw_kept0, both(i, s))
                        spread_sums(0).then_inc(m.sums_spread0, 1)
                yield 19
                pe.wait_ge(m.raw_kept1, both(i, s))
                spread_sums(1).then_inc(m.sums_spread1, 1)
                yield 22
                pe.wait_ge(m.oT_kept, both(i, s))
                for t in range(2):
                    for g in range(GROUPS):
                        last = mm(bank(s, 1)[:, bass.ts(t, P)], oT[s][:, g, bass.ts(t, P)], w_o[:, g, :], start=g == 0, stop=g == GROUPS - 1)
                last.then_inc(m.projected, 1)

            skewed(pe, first, second)

        @block.scalar
        def _(act):
            a = nc.scalar.activation

            def first(i, s):
                yield 6.2
                act.wait_ge(m.normed, both(i, s))
                act.wait_ge(m.qk_made, both(i, s))
                for j in range(3):
                    last = a(k[s][lane(j), :, j, :], c.PS[lane(j), 4 * s + 2, :].rearrange("p (g n) -> p g n", g=2), ACT.Copy)
                last.then_inc(m.k_kept, 1)

            def second(i, s):
                for h in range(AHEADS):
                    yield 1.2 + 1.8 * h
                    act.wait_ge(spread[h], both(i, s))
                    a(probs[s][:, h, :, :], bank(s, h % 2).rearrange("p (t n) -> p t n", t=2), ACT.Exp, scale=SCALE).then_inc(exps[h], 1)
                    if h == 3 + LAG:
                        act.wait_ge(m.summed0, both(i, s))
                        a(raw[s][:, 0:256], bank(s, 3)[:, 0:256], ACT.Copy).then_inc(m.raw_kept0, 1)
                yield 18
                act.wait_ge(m.summed1, both(i, s))
                a(raw[s][:, 256:], bank(s, 2)[:, 0:256], ACT.Copy).then_inc(m.raw_kept1, 1)

            skewed(act, first, second)

        @block.gpsimd
        def _(pool):
            def first(i, s):
                yield 1
                pool.wait_ge(m.stats, both(i, s))
                norm_rstd(nc, pool, c, norm[s])
                norm[s].last.then_inc(m.rstd, 1)

            def second(i, s):
                yield 1
                pool.wait_ge(m.normed, both(i, s))
                nc.gpsimd.tensor_tensor(xb[s][:, :, :], x3[s][:, :, :], b_o[:, :].unsqueeze(1).to_broadcast([P, 2, P]), ALU.add).then_inc(m.xb_ready, 1)

            skewed(pool, first, second)

        @block.vector
        def _(dve):
            vv = nc.vector
            for s in range(2):
                vv.memset(v[s][:, :, :, AHEAD:], 1.0)
                vv.memset(top[s][:, :, :, :, :], 0.0)
                vv.memset(k[s][:, :, :, :], 0.0)
            dve.drain()
            row = lambda a, t: a[:, bass.ds(t, 1), :].rearrange("p o d -> p (o d)")

            def maxima(s, g):
                return vv.tensor_reduce(top[s][:, :, g, :, AHEAD], banks(s, 0, 4).rearrange("p (t c) (j n) -> p t (c j) n", t=2, j=2),
                                        AX, ALU.max, negate=True)

            def first(i, s):
                yield 0
                for t in range(2):
                    vv.bn_stats(norm[s].sums[:, t, :], row(c.H, (i + s) * 2 + t))
                dve.drain()
                for t in range(2):
                    last = vv.bn_aggr(norm[s].stat[:, t, :], norm[s].sums[:, t, :])
                last.then_inc(m.stats, 1)
                yield 2.4
                dve.wait_ge(m.rstd, both(i, s))
                for t in range(2):
                    last = vv.tensor_scalar(x3[s][:, t, :], row(c.H, (i + s) * 2 + t), norm[s].stat[:, t, 0:1], norm[s].rstd[:, t:t + 1],
                                            ALU.subtract, ALU.mult)
                last.then_inc(m.normed, 1)
                yield 3.5
                dve.wait_ge(m.xT, both(i, s))
                vv.tensor_scalar(xT[s][:, :], bank(s, 0)[:, 0:256], 1.0, None, ALU.add).then_inc(m.xT_kept, 1)
                yield 6
                dve.wait_ge(m.qk_made, both(i, s))
                vv.tensor_copy(k[s][lane(3), :, 3, :], c.PS[lane(3), 4 * s + 2, :].rearrange("p (g n) -> p g n", g=2))
                vv.tensor_copy(q[s][:, :, :], bank(s, 1).rearrange("p (g n) -> p g n", g=2)).then_inc(m.qk_kept, 1)
                dve.wait_ge(m.v_made, both(i, s))
                vv.tensor_copy(v[s][:, :, :, 0:AHEAD].rearrange("p t h d -> p (t h) d"),
                               bank(s, 3)[:, 0:256].rearrange("p (g d) -> p g d", d=AHEAD)).then_inc(m.v_kept, 1)
                yield 10.5
                dve.wait_ge(m.scored0, both(i, s))
                maxima(s, 0).then_inc(m.top_kept0, 1)
                yield 16.4
                dve.wait_ge(m.scored1, both(i, s))
                maxima(s, 1).then_inc(m.top_kept1, 1)
                yield 19.2
                dve.wait_ge(m.topT, both(i, s))
                vv.tensor_tensor(q[s][:, :, :], bank(s, 0).rearrange("p (g n) -> p g n", g=2), q[s][:, :, :], ALU.add).then_inc(m.q_shifted, 1)

            def second(i, s):
                yield 12
                dve.wait_ge(m.sums_spread0, both(i, s))
                vv.reciprocal(share[s][:, 0:256], bank(s, 3)[:, 256:])
                dve.drain()
                vv.tensor_tensor(oT[s][:, 0, :], raw[s][:, 0:256], share[s][:, 0:256], ALU.mult)
                yield 20
                dve.wait_ge(m.sums_spread1, both(i, s))
                vv.reciprocal(share[s][:, 256:], bank(s, 2)[:, 256:])
                dve.drain()
                vv.tensor_tensor(oT[s][:, 1, :], raw[s][:, 256:], share[s][:, 256:], ALU.mult).then_inc(m.oT_kept, 1)
                yield 23
                dve.wait_ge(m.projected, both(i, s))
                dve.wait_ge(m.xb_ready, both(i, s))
                vv.tensor_tensor(c.X[:, bass.ds((i + s) * 2, 2), :], bank(s, 1)[:, 0:256].rearrange("p (t d) -> p t d", t=2), xb[s][:, :, :],
                                 ALU.add).then_inc(m.done, 1)

            skewed(dve, first, second)


def tower(nc, ins, out):
    c = Chip()
    gate0 = ("L0_ffn", "L0_ffn_Ws", "L0_ffn_bs")
    gate1 = ("L1_ffn", "L1_ffn_gate_W", "L1_ffn_gate_b")
    norm1 = ("L1_ffn_ln1_g", "L1_ffn_ln1_b")
    with ExitStack() as ctx:
        load_constants(nc, c, ins, ctx)
        with ExitStack() as mixture:
            expert_buffers(nc, c, mixture, 0)
            with ExitStack() as layers:
                w = [performer_weights(nc, c, layers, layer) for layer in range(2)]
                embed(nc, c, ins, w)
                prepare_performer(nc, c, w[0], 0)
                performer(nc, c, w[0], 0, lambda sp: load_performer(nc, sp, w[1], ins, 1))
                prepare_performer(nc, c, w[1], 1)
                performer(nc, c, w[1], 1, lambda sp: load_experts(nc, c, sp, ins, 0, *gate0))
            prepare_experts(nc, c, 0, "L0_ffn")
            gate(nc, c, "gate0", add=True)
            route(nc, c, "route0")
            experts(nc, c, "experts0", ACT.Gelu)
            combine(nc, c, "combine0")
        mamba(nc, c, ins)
        with ExitStack() as mixture:
            expert_buffers(nc, c, mixture, 1)
            attention(nc, c, ins, lambda sp: load_experts(nc, c, sp, ins, 1, *gate1, norm=norm1))
            prepare_experts(nc, c, 1, "L1_ffn", norm1)
            gate(nc, c, "gate1", add=False)
            route(nc, c, "route1")
            experts(nc, c, "experts1", ACT.Gelu_apprx_tanh)
            combine(nc, c, "combine1", out)


def laid_out(inputs):
    import numpy as np

    z = {name: np.asarray(a) for name, a in inputs.items()}
    keep = [n for n in z if n.startswith(("L0_attn_", "L0_ffn_", "L1_ffn_")) and n != "L0_attn_proj"]
    a = {n: z[n] for n in keep}
    a["ids"] = z["x"].reshape(TILES, P).T
    a["cache"] = z["L0_tok_sin_cos_cache"][..., ::-1].reshape(-1, P)
    a["projT"] = z["L0_attn_proj"].transpose(0, 2, 1)
    f, b = ({n: z[f"L1_attn_{d}_{n}"] for n in ("in_w", "conv_w", "conv_b", "dt_bias", "A_log", "D", "gnorm_w", "out_w")} for d in "fb")
    fw, bw = f["in_w"], b["in_w"]
    x, bs, cs, dts = (slice(lo, hi) for lo, hi in ((256, 512), (512, 576), (576, 640), (640, 644)))
    a["m_w_in"] = np.concatenate([fw[x], bw[x], fw[bs], bw[bs], fw[cs], bw[cs], fw[0:256], bw[0:256], fw[dts], bw[dts]]).T

    def channels(n):
        g, h = f[n], b[n]
        joined = np.concatenate([g[0:256], h[0:256], g[256:320], h[256:320], g[320:384], h[320:384]])
        return np.moveaxis(joined.reshape((MIX, P) + joined.shape[1:]), 0, 1)

    a["m_taps"] = channels("conv_w")
    a["m_tap_rows"] = np.concatenate([f["conv_w"][0:256], b["conv_w"][0:256]]).T[::-1].reshape(-1)
    a["m_tap_bias"] = channels("conv_b")
    join = lambda n: np.concatenate([f[n], b[n]])
    a["m_columns"] = np.concatenate([z["L1_attn_norm_w"][None], np.repeat(join("D"), HEAD).reshape(4, P), join("gnorm_w").reshape(4, P)]).T
    a["m_dt_bias"] = join("dt_bias")
    a["m_A_log"] = join("A_log")
    a["m_out_w"] = np.concatenate([f["out_w"], b["out_w"]], 1)
    a["m_projT"] = np.concatenate([z["L1_attn_proj_w"][:, :P].T, z["L1_attn_proj_w"][:, P:].T], 1)
    r, t = np.arange(P)[:, None], np.arange(P)[None]
    a["lane_sums"] = ((r % LANE == AHEAD) & (r // LANE == t // LANE)).astype(np.float32)
    a["m_masks"] = np.stack([r < t, r > t, r <= t, r >= t], 1).astype(np.float32)
    a["before"] = (r < t).astype(np.float32)
    a["ident"] = (r == t).astype(np.float32)
    a["experts"] = np.broadcast_to(np.arange(EXPERTS, dtype=np.float32) - EXPERTS, (P, EXPERTS))
    a["tile_start"] = (np.arange(SORTED, dtype=np.float32) * P)[None]
    return {n: np.ascontiguousarray(v) for n, v in a.items()}


def kernel(**inputs):
    import concourse.bacc as bacc
    from concourse.bass_utils import run_bass_kernel_spmd

    nc = bacc.Bacc("TRN2", target_bir_lowering=False, num_devices=1)
    arrays = laid_out(inputs)
    ins = {n: nc.dram_tensor(f"in_{n}", v.shape, mybir.dt.from_np(v.dtype), kind="ExternalInput").ap() for n, v in arrays.items()}
    out = nc.dram_tensor("out_0", (SEQS, SEQ_TILES * P, P), F32, kind="ExternalOutput").ap()
    tower(nc, ins, out)
    done = run_bass_kernel_spmd(nc, [{f"in_{n}": v for n, v in arrays.items()}], core_ids=[0])
    return done.results[0]["out_0"]
```

```python
from contextlib import ExitStack

import concourse.bass as bass
from concourse import mybir

F32 = mybir.dt.float32
I32 = mybir.dt.int32
U32 = mybir.dt.uint32
ALU = mybir.AluOpType
ACT = mybir.ActivationFunctionType
AX = mybir.AxisListType.X

P = 128
SEQS, SEQ_TILES = 32, 2
TILES = SEQS * SEQ_TILES
LANES = 4
HEADS, HEAD = 8, 64
WIDE = HEADS * HEAD
BLOCKS = WIDE // P
EXPERTS = 8
SORTED = TILES + EXPERTS
GATE_LANES = 4
GROUP = 8
GROUPS_OF_TILES = TILES // GROUP
EPS = 1e-5
KERNEL_EPS = 1e-4
DATA_NORM = HEAD ** -0.25
DIAG = 0.5 * HEAD ** -0.5


def both(i, s):
    return i + (s + 1)


def signals(nc, ctx):
    taken = []

    def take(name):
        taken.append(nc.alloc_semaphore(name))
        return taken[-1]

    def clear():
        nc.clear_and_free_semaphores(taken)
        nc.all_engine_barrier()

    ctx.callback(clear)
    return take


def in_turn(*parts):
    waiting = [[next(part, None), n, part] for n, part in enumerate(parts)]
    while True:
        ready = [w for w in waiting if w[0] is not None]
        if not ready:
            return
        least = min(ready, key=lambda w: (w[0], w[1]))
        least[0] = next(least[2], None)


def skewed(engine, first, second):
    in_turn(first(0, 0))
    with engine.Fori(0, SEQS - 3, 2) as i:
        in_turn(first(i, 1), second(i, 0))
        in_turn(first(i + 2, 0), second(i, 1))
    in_turn(first(SEQS - 2, 1), second(SEQS - 2, 0))
    in_turn(second(SEQS - 2, 1))


class Chip:
    pass


def broadcast_rows(vector_ap, width):
    return bass.AP(vector_ap.tensor, vector_ap.offset, [[0, P], [1, width]])


def fold_norm(nc, c, ctx, name, items, landed, landed_count, folds=()):
    take = signals(nc, ctx)
    raw_product = take(f"{name}_raw_product")
    scaled = take(f"{name}_scaled")
    row_product = take(f"{name}_row_product")
    folded = take(f"{name}_folded")
    turned = take(f"{name}_turned")
    turned_kept = take(f"{name}_turned_kept")
    joined = take(f"{name}_joined")
    joined_kept = take(f"{name}_joined_kept")
    turned_sb = ctx.enter_context(nc.sbuf_tensor(f"{name}_turned_sb", [P, WIDE if folds else 1], F32))
    BANKS = 4

    with nc.Block() as block:
        @block.tensor
        def _(pe):
            pe.wait_ge(landed, landed_count)
            for m, (w, scale, norm_bias, biases, own) in enumerate(items):
                rows = c.PS[:, m % BANKS, 0:w.shape[1]]
                if m >= BANKS:
                    pe.wait_ge(folded, m - BANKS + 1)
                if norm_bias is not None:
                    nc.tensor.matmul(rows, norm_bias, w, start=True, stop=False).then_inc(raw_product, 1)
                k = biases.shape[0]
                nc.tensor.matmul(rows, c.ident[0:k, own:own + 1].to_broadcast([k, P]), biases, start=norm_bias is None, stop=False)
                if scale is not None:
                    pe.wait_ge(scaled, m + 1)
                nc.tensor.matmul(rows, c.minus_ones[:, :], w, start=False, stop=True).then_inc(row_product, 1)
            for m, (w, matrix, _) in enumerate(folds):
                pe.wait_ge(folded, len(items))
                if m:
                    pe.wait_ge(joined_kept, m)
                for b in range(BLOCKS):
                    last = nc.tensor.transpose(c.PS[:, 4, bass.ts(b, P)], w[:, bass.ts(b, P)], c.ident[:, :])
                last.then_inc(turned, 1)
                pe.wait_ge(turned_kept, m + 1)
                for b in range(BLOCKS):
                    last = nc.tensor.matmul(c.PS[:, 5, bass.ts(b, P)], turned_sb[:, bass.ts(b, P)], matrix,
                                            start=True, stop=True)
                last.then_inc(joined, 1)

        @block.vector
        def _(dve):
            dve.wait_ge(landed, landed_count)
            for m, (w, scale, norm_bias, _, _) in enumerate(items):
                if scale is not None:
                    if norm_bias is not None:
                        dve.wait_ge(raw_product, m + 1)
                    nc.vector.tensor_scalar(w, w, scale, None, ALU.mult).then_inc(scaled, 1)
                dve.wait_ge(row_product, m + 1)
                nc.vector.scalar_tensor_tensor(w, c.PS[:, m % BANKS, 0:w.shape[1]], 1.0 / P, w, ALU.mult, ALU.add).then_inc(folded, 1)
            for m, (_, _, product) in enumerate(folds):
                dve.wait_ge(turned, m + 1)
                nc.vector.tensor_copy(turned_sb[:, :], c.PS[:, 4, :]).then_inc(turned_kept, 1)
                dve.wait_ge(joined, m + 1)
                nc.vector.tensor_copy(product, c.PS[:, 5, :]).then_inc(joined_kept, 1)


def load_constants(nc, c, ins, ctx):
    sb = lambda n, shape, dt=F32: ctx.enter_context(nc.sbuf_tensor(n, shape, dt))
    c.H = sb("H", [P, TILES + 2 * SEQ_TILES, P])
    c.X = sb("X", [P, SORTED, P])
    c.ident = sb("ident", [P, P])
    c.minus_ones = sb("minus_ones", [P, P])
    c.minus_half = sb("minus_half", [P, 4])
    c.eps = sb("eps", [P, 4])
    c.ids = sb("ids", [P, TILES], I32)
    c.before = sb("before", [P, P])
    c.experts = sb("experts", [P, EXPERTS])
    c.tile_start = sb("tile_start", [1, SORTED])
    c.logits = sb("logits", [P, TILES, EXPERTS])
    c.weight = sb("weight", [P, TILES + 2 * SEQ_TILES])
    c.row_of = sb("row_of", [P, TILES + 4 * SEQ_TILES], I32)
    c.tile_expert = sb("tile_expert", [1, SORTED], I32)
    c.sorted_in = nc.dram_tensor("sorted_in", [(SORTED + LANES) * P, P], F32).ap()
    c.sorted_out = nc.dram_tensor("sorted_out", [SORTED * P, P], F32).ap()
    c.PS = ctx.enter_context(nc.psum_tensor("PS", [P, 8, 512], F32))
    landed = ctx.enter_context(nc.semaphore("constants_landed"))
    c.weights_landed = [ctx.enter_context(nc.semaphore(f"expert_weights_landed_{n}")) for n in range(2)]
    with nc.Block() as block:
        @block.sync
        def _(sp):
            sp.dma_start(c.ident[:, :], ins["ident"]).then_inc(landed, 16)
            sp.dma_start(c.ids[:, :], ins["ids"]).then_inc(landed, 16)
            sp.dma_start(c.before[:, :], ins["before"]).then_inc(landed, 16)
            sp.dma_start(c.experts[:, :], ins["experts"]).then_inc(landed, 16)
            sp.dma_start(c.tile_start[:, :], ins["tile_start"]).then_inc(landed, 16)
            sp.wait_ge(landed, 5 * 16)

        @block.vector
        def _(dve):
            nc.vector.memset(c.minus_ones[:, :], -1.0)
            nc.vector.memset(c.minus_half[:, :], -0.5)
            nc.vector.memset(c.eps[:, :], EPS)
            nc.vector.memset(c.H[:, TILES:, :], 0.0)
            nc.vector.memset(c.weight[:, TILES:], 0.0)
            nc.vector.memset(c.X[:, TILES:TILES + 2 * SEQ_TILES, :], 0.0)
            nc.vector.memset(c.row_of[:, TILES:], 0)
            dve.drain()


def embed(nc, c, ins, layers):
    with ExitStack() as ctx:
        sb = lambda n, shape, dt=F32: ctx.enter_context(nc.sbuf_tensor(f"embed_{n}", shape, dt))
        sem = signals(nc, ctx)
        sums = [sb(f"sums_{n}", [P, GROUP, 6]) for n in range(2)]
        stat = [sb(f"stat_{n}", [P, GROUP, 2]) for n in range(2)]
        rstd = [sb(f"rstd_{n}", [P, GROUP]) for n in range(2)]
        half = sb("half", [P, GROUP])
        gathered = [sem(f"embed_gathered_{n}") for n in range(2)]
        stats = sem("embed_stats")
        rstd_ready = sem("embed_rstd")
        opened = sem("embed_proj_opened")
        zeroed, filled = sem("embed_zeroed"), sem("embed_filled")
        zeros = c.w1[:, :, :].rearrange("p e f -> p (e f)")
        block = ctx.enter_context(nc.Block())

        @block.sync
        def _(sp):
            sp.wait_ge(opened, 1)
            load_performer(nc, sp, layers[0], ins, 0)
            sp.wait_ge(zeroed, 1)
            buffer = c.sorted_in.rearrange("(p r) d -> p (r d)", p=P)
            starts = range(0, buffer.shape[1], zeros.shape[1])
            for at in starts:
                n = min(zeros.shape[1], buffer.shape[1] - at)
                sp.dma_start(buffer[:, at:at + n], zeros[:, 0:n]).then_inc(filled, 16)
            sp.wait_ge(filled, 16 * len(starts))

        @block.gpsimd
        def _(pool):
            def gather(g):
                for t in range(g * GROUP, (g + 1) * GROUP):
                    pool.indirect_dma_start(out=c.H[:, t, :], out_offset=None, in_=ins["cache"],
                                            in_offset=bass.IndirectOffsetOnAxis(ap=c.ids[:, t:t + 1], axis=0)
                                            ).then_inc(gathered[g % 2], 16)

            nc.gpsimd.memset(half[:, :], -0.5)
            gather(0)
            gather(1)
            for g in range(GROUPS_OF_TILES):
                pool.wait_ge(stats, (g + 1) * GROUP)
                r = rstd[g % 2][:, :]
                nc.gpsimd.tensor_tensor(r, stat[g % 2][:, :, 1], c.eps[:, 0:1].to_broadcast([P, GROUP]), ALU.add)
                pool.drain()
                nc.gpsimd.tensor_tensor(r, r, half[:, :], ALU.pow).then_inc(rstd_ready, GROUP)
                if g + 2 < GROUPS_OF_TILES:
                    gather(g + 2)

        @block.vector
        def _(dve):
            for w in layers:
                last = nc.vector.memset(w.proj[:, :], 0.0)
            last.then_inc(opened, 1)
            nc.vector.memset(zeros, 0.0).then_inc(zeroed, 1)
            with dve.Fori(0, TILES - 2 * GROUP + 1, 2 * GROUP) as t:
                tile = lambda a, n, j: a[:, bass.ds(t + (n * GROUP + j), 1), :].rearrange("p o d -> p (o d)")
                for n in range(2):
                    dve.wait_ge(gathered[n], (t + 2 * GROUP) * 8)
                    for j in range(GROUP):
                        nc.vector.bn_stats(sums[n][:, j, :], tile(c.H, n, j))
                    dve.drain()
                    for j in range(GROUP):
                        last = nc.vector.bn_aggr(stat[n][:, j, :], sums[n][:, j, :])
                    last.then_inc(stats, GROUP)
                for n in range(2):
                    dve.wait_ge(rstd_ready, t + (n + 1) * GROUP)
                    for j in range(GROUP):
                        nc.vector.tensor_scalar(tile(c.X, n, j), tile(c.H, n, j), stat[n][:, j, 0:1], rstd[n][:, j:j + 1],
                                                ALU.subtract, ALU.mult)
                dve.drain()


class NormBuffers:

    def __init__(self, nc, ctx, name):
        sb = lambda n, shape: ctx.enter_context(nc.sbuf_tensor(f"{name}_{n}", shape, F32))
        self.sums = sb("sums", [P, SEQ_TILES, 6])
        self.stat = sb("stat", [P, SEQ_TILES, 2])
        self.rstd = sb("rstd", [P, SEQ_TILES])
        self.last = None


def norm_stats(nc, dve, norm, rows):
    for t in range(SEQ_TILES):
        nc.vector.bn_stats(norm.sums[:, t, :], rows[:, t, :])
    dve.drain()
    for t in range(SEQ_TILES):
        norm.last = nc.vector.bn_aggr(norm.stat[:, t, :], norm.sums[:, t, :])


def norm_rstd(nc, pool, c, norm):
    nc.gpsimd.tensor_tensor(norm.rstd[:, :], norm.stat[:, :, 1], c.eps[:, 0:SEQ_TILES], ALU.add)
    pool.drain()
    norm.last = nc.gpsimd.tensor_tensor(norm.rstd[:, :], norm.rstd[:, :], c.minus_half[:, 0:SEQ_TILES], ALU.pow)


def norm_apply(nc, norm, rows, out):
    for t in range(SEQ_TILES):
        norm.last = nc.vector.tensor_scalar(out(t), rows[:, t, :], norm.stat[:, t, 0:1], norm.rstd[:, t:t + 1],
                                            ALU.subtract, ALU.mult)


def performer_weights(nc, c, ctx, layer):
    sb = lambda n, shape: ctx.enter_context(nc.sbuf_tensor(f"performer_{layer}_{n}", shape, F32))
    w = Chip()
    w.q, w.k, w.v, w.qd, w.kd, w.w1 = (sb(n, [P, WIDE]) for n in ("q", "k", "v", "qd", "kd", "w1"))
    w.wo, w.w2 = (sb(n, [P, BLOCKS, P]) for n in ("wo", "w2"))
    w.bo, w.b2 = (sb(n, [P, P]) for n in ("bo", "b2"))
    w.wide_biases = sb("wide_biases", [4, WIDE])
    w.columns = sb("columns", [P, 4])
    w.norm_bias = [sb("ln1_bias_wide", [P, P]), sb("ln2_bias_wide", [P, P])]
    w.proj = sb("proj", [P, P])
    w.landed = ctx.enter_context(nc.semaphore(f"performer_{layer}_landed"))
    return w


PERFORMER_LOADS = 18 * 16


def load_performer(nc, sp, w, ins, layer):
    row = lambda n: ins[f"L0_attn_{n}"][layer]
    for at, name in ((w.q, "Wq"), (w.k, "Wk"), (w.v, "Wv"), (w.w1, "W1")):
        sp.dma_start(at[:, :], row(name)).then_inc(w.landed, 16)
    for at, name in ((w.wo, "Wo"), (w.w2, "W2")):
        sp.dma_start(at[:, :, :], row(name).rearrange("(b p) d -> p b d", p=P)).then_inc(w.landed, 16)
    for at, name in ((w.bo, "bo"), (w.b2, "b2")):
        sp.dma_start(at[:, :], broadcast_rows(row(name), P)).then_inc(w.landed, 16)
    for k, name in enumerate(("bq", "bk", "bv", "b1")):
        sp.dma_start(w.wide_biases[k:k + 1, :], row(name).rearrange("(o d) -> o d", o=1)).then_inc(w.landed, 16)
    for k, name in enumerate(("ln1_s", "ln1_b", "ln2_s", "ln2_b")):
        sp.dma_start(w.columns[:, k:k + 1], row(name).rearrange("(p o) -> p o", o=1)).then_inc(w.landed, 16)
    for h in range(2):
        sp.dma_start(w.proj[bass.ts(h, HEAD), bass.ts(h, HEAD)], ins["projT"][layer]).then_inc(w.landed, 16)


def prepare_performer(nc, c, w, layer):
    with ExitStack() as ctx:
        with nc.Block() as block:
            @block.vector
            def _(dve):
                dve.wait_ge(w.landed, PERFORMER_LOADS)
                for k in range(2):
                    nc.vector.tensor_copy(w.norm_bias[k][:, :], w.columns[:, 2 * k + 1:2 * k + 2].to_broadcast([P, P]))
                nc.vector.tensor_scalar(w.proj[:, :], w.proj[:, :], DATA_NORM, None, ALU.mult)
                dve.drain()
        scale1, scale2 = w.columns[:, 0:1], w.columns[:, 2:3]
        biases = w.wide_biases[:, :]
        fold_norm(nc, c, ctx, f"performer_{layer}",
                  [(w.q[:, :], scale1, w.norm_bias[0][:, :], biases, 0),
                   (w.k[:, :], scale1, w.norm_bias[0][:, :], biases, 1),
                   (w.v[:, :], scale1, w.norm_bias[0][:, :], biases, 2),
                   (w.w1[:, :], scale2, w.norm_bias[1][:, :], biases, 3)],
                  w.landed, PERFORMER_LOADS,
                  [(w.q[:, :], w.proj[:, :], w.qd[:, :]), (w.k[:, :], w.proj[:, :], w.kd[:, :])])


def performer(nc, c, w, layer, prefetch):
    with ExitStack() as ctx:
        sb = lambda n, shape: [ctx.enter_context(nc.sbuf_tensor(f"p{layer}_{n}_{s}", shape, F32)) for s in range(2)]
        take = signals(nc, ctx)
        sem = lambda n: take(f"p{layer}_{n}")
        xn = sb("xn", [P, SEQ_TILES, P])
        xb = sb("xb", [P, SEQ_TILES, P])
        x2 = sb("x2", [P, SEQ_TILES, P])
        hT = sb("hT", [P, SEQ_TILES * P])
        square = sb("square", [P, SEQ_TILES * WIDE])
        feat = sb("feat", [P, SEQ_TILES * WIDE])
        featT = sb("featT", [P, BLOCKS, SEQ_TILES * P])
        attn = sb("attn", [P, SEQ_TILES * WIDE])
        v = sb("v", [P, SEQ_TILES, HEADS, HEAD + 1])
        ctx_sb = sb("ctx", [P, BLOCKS, 2, HEAD + 1])
        top = sb("top", [P, 2 * HEADS])
        top8 = sb("top8", [P, HEADS])
        top1 = sb("top1", [HEADS, 1])
        power = sb("power", [P, 2 * HEADS])
        shift = sb("shift", [P, 2 * HEADS])
        share = sb("share", [P, 2 * HEADS])
        norm = [NormBuffers(nc, ctx, f"p{layer}_norm_{s}") for s in range(2)]
        norm2 = [NormBuffers(nc, ctx, f"p{layer}_norm2_{s}") for s in range(2)]
        tiles = lambda a: a.rearrange("p (t d) -> p t d", t=SEQ_TILES)
        x2b = [tiles(square[s][:, 0:SEQ_TILES * P]) for s in range(2)]
        x2n = [tiles(square[s][:, SEQ_TILES * P:2 * SEQ_TILES * P]) for s in range(2)]
        bank = lambda s, b: c.PS[:, 4 * s + b, :]
        banks = lambda s, b, n: c.PS[:, 4 * s + b:4 * s + b + n, :]
        m = Chip()
        m.stats, m.rstd, m.xb_ready, m.xn_ready, m.xnT, m.hT_ready, m.kd_made = map(sem, (
            "stats", "rstd", "xb_ready", "xn_ready", "xnT", "hT_ready", "kd_made"))
        m.k_made, m.k_squared, m.k_top, m.k_topT, m.k_top1, m.k_topped, m.k_arg0 = map(sem, (
            "k_made", "k_squared", "k_top", "k_topT", "k_top1", "k_topped", "k_arg0"))
        m.k_arg1, m.k_exp0, m.k_exp1, m.k_feat, m.v_made, m.v_kept, m.ctx_made = map(sem, (
            "k_arg1", "k_exp0", "k_exp1", "k_feat", "v_made", "v_kept", "ctx_made"))
        m.ctx_kept, m.q_made, m.q_squared, m.q_power, m.qd_made, m.q_arg0, m.q_arg1 = map(sem, (
            "ctx_kept", "q_made", "q_squared", "q_power", "qd_made", "q_arg0", "q_arg1"))
        m.q_exp0, m.q_exp1, m.q_featT0, m.q_featT1, m.q_featT_kept0, m.q_featT_kept1, m.weighed0 = map(sem, (
            "q_exp0", "q_exp1", "q_featT0", "q_featT1", "q_featT_kept0", "q_featT_kept1", "weighed0"))
        m.weighed1, m.attn_kept0, m.attn_kept1, m.attnT0, m.attnT1, m.attnT_kept0, m.attnT_kept1 = map(sem, (
            "weighed1", "attn_kept0", "attn_kept1", "attnT0", "attnT1", "attnT_kept0", "attnT_kept1"))
        m.o_made, m.x2_stats, m.x2_rstd, m.x2b_ready, m.x2n_ready, m.x2nT, m.h2T_ready = map(sem, (
            "o_made", "x2_stats", "x2_rstd", "x2b_ready", "x2n_ready", "x2nT", "h2T_ready"))
        m.f_made0, m.f_made1, m.f_kept0, m.f_kept1, m.y_made, m.done = map(sem, (
            "f_made0", "f_made1", "f_kept0", "f_kept1", "y_made", "done"))
        N = SEQS

        block = ctx.enter_context(nc.Block())

        @block.sync
        def _(sp):
            prefetch(sp)

        @block.tensor
        def _(pe):
            def turn(rows, s, t, into):
                for b in range(BLOCKS):
                    last = nc.tensor.transpose(bank(s, into)[:, bass.ts(b, P)], rows[:, t * WIDE + b * P:t * WIDE + (b + 1) * P], c.ident[:, :])
                return last

            def weigh(s, t):
                for b in range(BLOCKS):
                    out = bank(s, 2 - 2 * t + b // 2)[:, (b % 2) * 130:(b % 2) * 130 + 130]
                    last = nc.tensor.matmul(out, featT[s][:, b, bass.ts(t, P)],
                                            ctx_sb[s][:, b, :, :].rearrange("p h d -> p (h d)"), start=True, stop=True)
                return last

            def first(i, s):
                yield 3.6
                pe.wait_ge(m.xn_ready, both(i, s))
                for t in range(2):
                    last = nc.tensor.transpose(bank(s, 0)[:, bass.ts(t, P)], xn[s][:, t, :], c.ident[:, :])
                last.then_inc(m.xnT, 1)
                yield 4.5
                pe.wait_ge(m.hT_ready, both(i, s))
                for t in range(2):
                    last = nc.tensor.matmul(bank(s, 2 + t), hT[s][:, bass.ts(t, P)], w.kd[:, :], start=True, stop=True)
                last.then_inc(m.kd_made, 1)
                for t in range(2):
                    last = nc.tensor.matmul(bank(s, t), hT[s][:, bass.ts(t, P)], w.k[:, :], start=True, stop=True)
                last.then_inc(m.k_made, 1)
                yield 9.4
                pe.wait_ge(m.k_top, both(i, s))
                pe.wait_ge(m.k_squared, both(i, s))
                nc.tensor.transpose(bank(s, 0)[0:HEADS, 0:P], top8[s][:, :], c.ident[:, :]).then_inc(m.k_topT, 1)
                yield 10.71
                pe.wait_ge(m.k_top1, both(i, s))
                nc.tensor.matmul(bank(s, 0)[:, 256:256 + HEADS], top1[s][:, 0:1].to_broadcast([HEADS, P]),
                                 c.ident[0:HEADS, 0:HEADS], start=True, stop=True).then_inc(m.k_topped, 1)
                yield 12.9
                pe.wait_ge(m.k_arg0, both(i, s))
                for t in range(2):
                    last = nc.tensor.matmul(bank(s, t), hT[s][:, bass.ts(t, P)], w.v[:, :], start=True, stop=True)
                last.then_inc(m.v_made, 1)
                yield 15.9
                pe.wait_ge(m.v_kept, both(i, s))
                for t in range(2):
                    last = nc.tensor.matmul(bank(s, t), hT[s][:, bass.ts(t, P)], w.q[:, :], start=True, stop=True)
                last.then_inc(m.q_made, 1)
                yield 17.7
                pe.wait_ge(m.k_feat, both(i, s))
                for b in range(BLOCKS):
                    out = bank(s, 2 + b // 2)[:, (b % 2) * 130:(b % 2) * 130 + 130]
                    for t in range(2):
                        last = nc.tensor.matmul(out, feat[s][:, t * WIDE + b * P:t * WIDE + (b + 1) * P],
                                                v[s][:, t, 2 * b:2 * b + 2, :].rearrange("p h d -> p (h d)"),
                                                start=t == 0, stop=t == 1)
                last.then_inc(m.ctx_made, 1)

            def second(i, s):
                yield 3.96
                pe.wait_ge(m.ctx_kept, both(i, s))
                for t in range(2):
                    last = nc.tensor.matmul(bank(s, 2 + t), hT[s][:, bass.ts(t, P)], w.qd[:, :], start=True, stop=True)
                last.then_inc(m.qd_made, 1)
                yield 8.83
                pe.wait_ge(m.q_squared, both(i, s))
                pe.wait_ge(m.q_exp0, both(i, s))
                turn(feat[s], s, 0, 0).then_inc(m.q_featT0, 1)
                yield 9.33
                pe.wait_ge(m.q_exp1, both(i, s))
                turn(feat[s], s, 1, 1).then_inc(m.q_featT1, 1)
                yield 10.13
                pe.wait_ge(m.q_featT_kept0, both(i, s))
                weigh(s, 0).then_inc(m.weighed0, 1)
                yield 10.26
                pe.wait_ge(m.q_featT_kept1, both(i, s))
                weigh(s, 1).then_inc(m.weighed1, 1)
                yield 11.26
                pe.wait_ge(m.attn_kept0, both(i, s))
                turn(attn[s], s, 0, 2).then_inc(m.attnT0, 1)
                yield 12.26
                pe.wait_ge(m.attn_kept1, both(i, s))
                turn(attn[s], s, 1, 0).then_inc(m.attnT1, 1)
                yield 13.46
                for t in range(2):
                    pe.wait_ge((m.attnT_kept0, m.attnT_kept1)[t], both(i, s))
                    for b in range(BLOCKS):
                        last = nc.tensor.matmul(bank(s, 3)[:, bass.ts(t, P)], featT[s][:, b, bass.ts(t, P)], w.wo[:, b, :],
                                                start=b == 0, stop=b == BLOCKS - 1)
                last.then_inc(m.o_made, 1)
                yield 19
                pe.wait_ge(m.x2n_ready, both(i, s))
                for t in range(2):
                    last = nc.tensor.transpose(bank(s, 2)[:, bass.ts(t, P)], x2n[s][:, t, :], c.ident[:, :])
                last.then_inc(m.x2nT, 1)
                yield 20.26
                pe.wait_ge(m.h2T_ready, both(i, s))
                for b in range(BLOCKS):
                    last = nc.tensor.matmul(bank(s, b // 2)[:, (b % 2) * 256:(b % 2) * 256 + 256], w.w1[:, bass.ts(b, P)],
                                            hT[s][:, :], start=True, stop=True)
                    if b % 2:
                        last.then_inc((m.f_made0, m.f_made1)[b // 2], 1)
                yield 24.16
                for b in range(BLOCKS):
                    if b % 2 == 0:
                        pe.wait_ge((m.f_kept0, m.f_kept1)[b // 2], both(i, s))
                    for t in range(2):
                        last = nc.tensor.matmul(bank(s, 2 + t)[:, 0:P], featT[s][:, b, bass.ts(t, P)], w.w2[:, b, :],
                                                start=b == 0, stop=b == BLOCKS - 1)
                last.then_inc(m.y_made, 1)

            skewed(pe, first, second)

        @block.scalar
        def _(act):
            exp = lambda a: nc.scalar.activation(a, a, ACT.Exp)

            def first(i, s):
                yield 8
                act.wait_ge(m.k_made, both(i, s))
                nc.scalar.activation(square[s][:, :], banks(s, 0, 2), ACT.Square).then_inc(m.k_squared, 1)
                yield 12.9
                for t in range(2):
                    act.wait_ge((m.k_arg0, m.k_arg1)[t], both(i, s))
                    exp(feat[s][:, bass.ts(t, WIDE)]).then_inc((m.k_exp0, m.k_exp1)[t], 1)
                yield 14.8
                act.wait_ge(m.v_made, both(i, s))
                nc.scalar.activation(v[s][:, :, :, 0:HEAD].rearrange("p t h d -> p (t h) d"),
                                     banks(s, 0, 2).rearrange("p t (h d) -> p (t h) d", d=HEAD), ACT.Copy).then_inc(m.v_kept, 1)
                yield 17.7
                act.wait_ge(m.q_made, both(i, s))
                nc.scalar.activation(square[s][:, :], banks(s, 0, 2), ACT.Square).then_inc(m.q_squared, 1)

            def second(i, s):
                yield 7.53
                for t in range(2):
                    act.wait_ge((m.q_arg0, m.q_arg1)[t], both(i, s))
                    exp(feat[s][:, bass.ts(t, WIDE)]).then_inc((m.q_exp0, m.q_exp1)[t], 1)
                yield 11.76
                act.wait_ge(m.attnT0, both(i, s))
                nc.scalar.activation(featT[s][:, :, bass.ts(0, P)], bank(s, 2).rearrange("p (b n) -> p b n", n=P), ACT.Copy).then_inc(m.attnT_kept0, 1)
                yield 12.76
                act.wait_ge(m.attnT1, both(i, s))
                nc.scalar.activation(featT[s][:, :, bass.ts(1, P)], bank(s, 0).rearrange("p (b n) -> p b n", n=P), ACT.Copy).then_inc(m.attnT_kept1, 1)
                yield 22.06
                for n in range(2):
                    act.wait_ge((m.f_made0, m.f_made1)[n], both(i, s))
                    nc.scalar.activation(featT[s][:, 2 * n:2 * n + 2, :], bank(s, n).rearrange("p (c n) -> p c n", n=256), ACT.Gelu_apprx_tanh).then_inc((m.f_kept0, m.f_kept1)[n], 1)

            skewed(act, first, second)

        @block.gpsimd
        def _(pool):
            def sums_of_squares(s):
                n = HEAD // 2
                q = square[s][:, :].rearrange("p (g d) -> p g d", d=HEAD)
                half = attn[s][:, 0:WIDE].rearrange("p (g d) -> p g d", d=n)
                nc.gpsimd.tensor_tensor(half, q[:, :, 0:n], q[:, :, n:], ALU.add)
                while n > 2:
                    n //= 2
                    pool.drain()
                    nc.gpsimd.tensor_tensor(half[:, :, 0:n], half[:, :, 0:n], half[:, :, n:2 * n], ALU.add)
                pool.drain()
                return nc.gpsimd.tensor_tensor(power[s][:, :], half[:, :, 0], half[:, :, 1], ALU.add)

            def rows_rstd(i, s):
                norm_rstd(nc, pool, c, norm[s])
                norm[s].last.then_inc(m.rstd, 1)
                for t in range(2):
                    last = nc.gpsimd.tensor_tensor(xb[s][:, t, :], c.X[:, bass.ds((i + s) * 2 + t, 1), :].rearrange("p o d -> p (o d)"), w.bo[:, :], ALU.add)
                last.then_inc(m.xb_ready, 1)

            for s in range(2):
                pool.wait_ge(m.stats, s + 1)
                rows_rstd(0, s)
            def first(i, s):
                yield from ()

            def second(i, s):
                yield 0.93
                pool.wait_ge(m.q_squared, both(i, s))
                sums_of_squares(s).then_inc(m.q_power, 1)
                yield 16.56
                pool.wait_ge(m.x2_stats, both(i, s))
                norm_rstd(nc, pool, c, norm2[s])
                norm2[s].last.then_inc(m.x2_rstd, 1)
                for t in range(2):
                    last = nc.gpsimd.tensor_tensor(x2b[s][:, t, :], x2[s][:, t, :], w.b2[:, :], ALU.add)
                last.then_inc(m.x2b_ready, 1)
                yield 18.56
                pool.wait_ge(m.stats, both(i + 2, s))
                rows_rstd(i + 2, s)

            skewed(pool, first, second)

        @block.vector
        def _(dve):
            for s in range(2):
                nc.vector.memset(v[s][:, :, :, HEAD:HEAD + 1], 1.0)
                nc.vector.memset(ctx_sb[s][:, :, :, :], 0.0)
            dve.drain()
            halves = lambda a: a.rearrange("p (t h) -> p t h", t=2)
            heads = lambda a: a.rearrange("p (g d) -> p g d", d=HEAD)

            def normalise(s, t):
                made = banks(s, 2 - 2 * t, 2)[:, :, 0:260].rearrange("p b (h d) -> p b h d", h=4)
                part = share[s][:, bass.ts(t, HEADS)].rearrange("p (b h) -> p b h", h=4)
                nc.vector.reciprocal(part, made[:, :, :, HEAD])
                dve.drain()
                return nc.vector.tensor_tensor(attn[s][:, bass.ts(t, WIDE)].rearrange("p (b h d) -> p b h d", b=2, h=4), made[:, :, :, 0:HEAD],
                                               part.unsqueeze(3).to_broadcast([P, 2, 4, HEAD]), ALU.mult)

            def exponent(s, shift_of, done):
                shift_of()
                dve.drain()
                for t in range(2):
                    nc.vector.tensor_tensor(heads(feat[s][:, bass.ts(t, WIDE)]), bank(s, 2 + t).rearrange("p (h d) -> p h d", d=HEAD),
                                            shift[s][:, bass.ts(t, HEADS)].unsqueeze(2).to_broadcast([P, HEADS, HEAD]), ALU.subtract).then_inc(done[t], 1)

            x_tile = lambda i, s, t: c.X[:, bass.ds((i + s) * 2 + t, 1), :].rearrange("p o d -> p (o d)")

            def rows_stats(i, s):
                for t in range(SEQ_TILES):
                    nc.vector.bn_stats(norm[s].sums[:, t, :], x_tile(i, s, t))
                dve.drain()
                for t in range(SEQ_TILES):
                    last = nc.vector.bn_aggr(norm[s].stat[:, t, :], norm[s].sums[:, t, :])
                return last

            def rows_normed(i, s):
                for t in range(SEQ_TILES):
                    last = nc.vector.tensor_scalar(xn[s][:, t, :], x_tile(i, s, t), norm[s].stat[:, t, 0:1], norm[s].rstd[:, t:t + 1],
                                                   ALU.subtract, ALU.mult)
                return last

            for s in range(2):
                rows_stats(0, s).then_inc(m.stats, 1)
            for s in range(2):
                dve.wait_ge(m.rstd, s + 1)
                rows_normed(0, s).then_inc(m.xn_ready, 1)
            def first(i, s):
                yield 4
                dve.wait_ge(m.xnT, both(i, s))
                nc.vector.tensor_scalar(hT[s][:, :], bank(s, 0)[:, 0:256], 1.0, None, ALU.add).then_inc(m.hT_ready, 1)
                yield 8
                dve.wait_ge(m.kd_made, both(i, s))
                nc.vector.tensor_reduce(top[s][:, :], banks(s, 2, 2).rearrange("p t (h d) -> p (t h) d", d=HEAD), AX, ALU.max)
                dve.drain()
                nc.vector.tensor_tensor(top8[s][:, :], top[s][:, 0:HEADS], top[s][:, HEADS:], ALU.max).then_inc(m.k_top, 1)
                yield 10.02
                dve.wait_ge(m.k_squared, both(i, s))
                nc.vector.tensor_reduce(power[s][:, :], heads(square[s][:, :]), AX, ALU.add)
                yield 10.7
                dve.wait_ge(m.k_topT, both(i, s))
                nc.vector.tensor_reduce(top1[s][:, :], bank(s, 0)[0:HEADS, 0:P], AX, ALU.max).then_inc(m.k_top1, 1)
                yield 11.3
                dve.drain()
                dve.wait_ge(m.k_topped, both(i, s))
                exponent(s, lambda: nc.vector.scalar_tensor_tensor(
                    halves(shift[s][:, :]), halves(power[s][:, :]), DIAG,
                    bank(s, 0)[:, 256:256 + HEADS].unsqueeze(1).to_broadcast([P, 2, HEADS]), ALU.mult, ALU.add),
                    (m.k_arg0, m.k_arg1))
                yield 14.8
                for t in range(2):
                    dve.wait_ge((m.k_exp0, m.k_exp1)[t], both(i, s))
                    f = feat[s][:, bass.ts(t, WIDE)]
                    last = nc.vector.tensor_scalar(f, f, KERNEL_EPS, None, ALU.add)
                last.then_inc(m.k_feat, 1)

            def second(i, s):
                yield 1.63
                dve.wait_ge(m.ctx_made, both(i, s))
                for half in range(2):
                    r = bass.ts(half, HEAD)
                    made = c.PS[r, 4 * s + 2:4 * s + 4, 0:260].rearrange("p b (c h d) -> p b c h d", c=2, h=2)[:, :, :, half, :]
                    last = nc.vector.tensor_copy(ctx_sb[s][r, :, half, :].rearrange("p (b c) d -> p b c d", c=2), made)
                last.then_inc(m.ctx_kept, 1)
                yield 4.73
                dve.wait_ge(m.qd_made, both(i, s))
                nc.vector.tensor_reduce(top[s][:, :], banks(s, 2, 2).rearrange("p t (h d) -> p (t h) d", d=HEAD), AX, ALU.max)
                dve.drain()
                dve.wait_ge(m.q_power, both(i, s))
                exponent(s, lambda: nc.vector.scalar_tensor_tensor(
                    shift[s][:, :], power[s][:, :], DIAG, top[s][:, :], ALU.mult, ALU.add),
                    (m.q_arg0, m.q_arg1))
                yield 9.33
                dve.wait_ge(m.q_featT0, both(i, s))
                nc.vector.tensor_scalar(featT[s][:, :, bass.ts(0, P)], bank(s, 0).rearrange("p (b n) -> p b n", n=P),
                                        KERNEL_EPS, None, ALU.add).then_inc(m.q_featT_kept0, 1)
                yield 9.34
                dve.wait_ge(m.q_featT1, both(i, s))
                nc.vector.tensor_scalar(featT[s][:, :, bass.ts(1, P)], bank(s, 1).rearrange("p (b n) -> p b n", n=P),
                                        KERNEL_EPS, None, ALU.add).then_inc(m.q_featT_kept1, 1)
                yield 10.26
                dve.wait_ge(m.weighed0, both(i, s))
                normalise(s, 0).then_inc(m.attn_kept0, 1)
                yield 11.26
                dve.wait_ge(m.weighed1, both(i, s))
                normalise(s, 1).then_inc(m.attn_kept1, 1)
                yield 15.07
                dve.wait_ge(m.o_made, both(i, s))
                dve.wait_ge(m.xb_ready, both(i, s))
                nc.vector.tensor_tensor(x2[s][:, :, :], bank(s, 3)[:, 0:256].rearrange("p (t d) -> p t d", t=2), xb[s][:, :, :], ALU.add)
                dve.drain()
                norm_stats(nc, dve, norm2[s], x2[s])
                norm2[s].last.then_inc(m.x2_stats, 1)
                yield 16.26
                rows_stats(i + 2, s).then_inc(m.stats, 1)
                yield 18.66
                dve.wait_ge(m.x2_rstd, both(i, s))
                norm_apply(nc, norm2[s], x2[s], lambda t: x2n[s][:, t, :])
                norm2[s].last.then_inc(m.x2n_ready, 1)
                yield 19.76
                dve.wait_ge(m.x2nT, both(i, s))
                nc.vector.tensor_scalar(hT[s][:, :], bank(s, 2)[:, 0:256], 1.0, None, ALU.add).then_inc(m.h2T_ready, 1)
                yield 20.76
                dve.wait_ge(m.rstd, both(i + 2, s))
                rows_normed(i + 2, s).then_inc(m.xn_ready, 1)
                yield 25.96
                dve.wait_ge(m.y_made, both(i, s))
                dve.wait_ge(m.x2b_ready, both(i, s))
                nc.vector.tensor_tensor(c.X[:, bass.ds((i + s) * 2, 2), :], banks(s, 2, 2)[:, :, 0:P],
                                        x2b[s], ALU.add).then_inc(m.done, 1)

            skewed(dve, first, second)


def expert_buffers(nc, c, ctx, which):
    sb = lambda n, shape, dt=F32: ctx.enter_context(nc.sbuf_tensor(f"{n}_{which}", shape, dt))
    c.w1 = sb("expert_w1", [P, EXPERTS, WIDE])
    c.w2 = sb("expert_w2", [P, EXPERTS, BLOCKS, P])
    c.b2 = sb("expert_b2", [P, EXPERTS, P])
    c.gate = sb("gate", [P, EXPERTS])
    c.b1 = sb("expert_b1", [EXPERTS, WIDE])
    c.gate_bias = sb("gate_bias", [1, EXPERTS])
    c.gate_norm = sb("gate_norm", [P, 2])


def load_experts(nc, c, sp, ins, which, prefix, gate_w, gate_b, norm=()):
    landed = c.weights_landed[which]
    sp.dma_start(c.gate[:, :], ins[gate_w]).then_inc(landed, 16)
    sp.dma_start(c.gate_bias[:, :], ins[gate_b].rearrange("(o e) -> o e", o=1)).then_inc(landed, 16)
    for k, name in enumerate(norm):
        sp.dma_start(c.gate_norm[:, k:k + 1], ins[name].rearrange("(p o) -> p o", o=1)).then_inc(landed, 16)
    sp.dma_start(c.b1[:, :], ins[f"{prefix}_b1"]).then_inc(landed, 16)
    sp.dma_start(c.w1[:, :, :], ins[f"{prefix}_W1"].rearrange("e p f -> p e f")).then_inc(landed, 16)
    for e in range(EXPERTS):
        sp.dma_start(c.w2[:, e, :, :], ins[f"{prefix}_W2"][e].rearrange("(b p) d -> p b d", p=P)).then_inc(landed, 16)
    sp.dma_start(c.b2[:, :, :].rearrange("p e d -> p (e d)"), broadcast_rows(ins[f"{prefix}_b2"], EXPERTS * P)).then_inc(landed, 16)


EXPERT_LOADS = 16 * (EXPERTS + 5)


def prepare_experts(nc, c, which, prefix, norm=()):
    with ExitStack() as ctx:
        norm_bias = ctx.enter_context(nc.sbuf_tensor(f"prepare_{prefix}_norm_bias", [P, P], F32))
        landed, count = c.weights_landed[which], EXPERT_LOADS + 16 * len(norm)
        with nc.Block() as block:
            if norm:
                @block.vector
                def _(dve):
                    dve.wait_ge(landed, count)
                    nc.vector.tensor_copy(norm_bias[:, :], c.gate_norm[:, 1:2].to_broadcast([P, P]))
                    dve.drain()
        scale = c.gate_norm[:, 0:1] if norm else None
        bias = norm_bias[:, :] if norm else None
        fold_norm(nc, c, ctx, prefix,
                  [(c.gate[:, :], scale, bias, c.gate_bias[:, :], 0)]
                  + [(c.w1[:, e, :], scale, bias, c.b1[:, :], e) for e in range(EXPERTS)],
                  landed, count)


def gate(nc, c, name, add):
    with ExitStack() as ctx:
        sb = lambda n, shape: [ctx.enter_context(nc.sbuf_tensor(f"{name}_{n}_{s}", shape, F32)) for s in range(GATE_LANES)]
        take = signals(nc, ctx)
        sem = lambda n: take(f"{name}_{n}")
        xn = sb("xn", [P, SEQ_TILES, P])
        hT = sb("hT", [P, SEQ_TILES * P])
        norm = [NormBuffers(nc, ctx, f"{name}_norm_{s}") for s in range(GATE_LANES)]
        stats, rstd, ready, turned, turned_kept, made, kept, copied = (
            sem(n) for n in ("stats", "rstd", "ready", "turned", "turned_kept", "made", "kept", "copied"))
        block = ctx.enter_context(nc.Block())

        @block.vector
        def _(dve):
            rows = c.H if add else c.X
            row = lambda i, s, t: rows[:, bass.ds((i + s) * 2 + t, 1), :].rearrange("p o d -> p (o d)")
            with dve.Fori(0, SEQS - GATE_LANES + 1, GATE_LANES) as i:
                for s in range(GATE_LANES):
                    if add:
                        here = bass.ds((i + s) * 2, 2)
                        nc.vector.tensor_tensor(c.H[:, here, :], c.H[:, here, :], c.X[:, here, :], ALU.add)
                        dve.drain()
                    for t in range(SEQ_TILES):
                        nc.vector.bn_stats(norm[s].sums[:, t, :], row(i, s, t))
                    dve.drain()
                    for t in range(SEQ_TILES):
                        last = nc.vector.bn_aggr(norm[s].stat[:, t, :], norm[s].sums[:, t, :])
                    last.then_inc(stats, 1)
                for s in range(GATE_LANES):
                    dve.wait_ge(rstd, both(i, s))
                    for t in range(SEQ_TILES):
                        last = nc.vector.tensor_scalar(xn[s][:, t, :], row(i, s, t), norm[s].stat[:, t, 0:1], norm[s].rstd[:, t:t + 1],
                                                       ALU.subtract, ALU.mult)
                    last.then_inc(ready, 1)
                for s in range(GATE_LANES):
                    dve.wait_ge(turned, both(i, s))
                    nc.vector.tensor_scalar(hT[s][:, :], c.PS[:, s, 0:256], 1.0, None, ALU.add).then_inc(turned_kept, 1)
                for s in range(GATE_LANES):
                    dve.wait_ge(made, both(i, s))
                    nc.vector.tensor_copy(c.logits[:, bass.ds((i + s) * 2, 2), :],
                                          c.PS[:, GATE_LANES + s, 0:16].rearrange("p (t e) -> p t e", t=2)).then_inc(kept, 1)
                dve.drain()
                dve.wait_ge(copied, both(i, GATE_LANES - 1))

        @block.gpsimd
        def _(pool):
            with pool.Fori(0, SEQS - GATE_LANES + 1, GATE_LANES) as i:
                for s in range(GATE_LANES):
                    pool.wait_ge(stats, both(i, s))
                    norm_rstd(nc, pool, c, norm[s])
                    norm[s].last.then_inc(rstd, 1)

        @block.scalar
        def _(act):
            with act.Fori(0, SEQS - GATE_LANES + 1, GATE_LANES) as i:
                for s in range(GATE_LANES):
                    act.wait_ge(ready, both(i, s))
                    nc.scalar.activation(c.X[:, bass.ds((i + s) * 2, 2), :], xn[s][:, :, :], ACT.Copy).then_inc(copied, 1)

        @block.tensor
        def _(pe):
            with pe.Fori(0, SEQS - GATE_LANES + 1, GATE_LANES) as i:
                for s in range(GATE_LANES):
                    pe.wait_ge(ready, both(i, s))
                    for t in range(2):
                        last = nc.tensor.transpose(c.PS[:, s, bass.ts(t, P)], xn[s][:, t, :], c.ident[:, :])
                    last.then_inc(turned, 1)
                for s in range(GATE_LANES):
                    pe.wait_ge(turned_kept, both(i, s))
                    for t in range(2):
                        last = nc.tensor.matmul(c.PS[:, GATE_LANES + s, bass.ts(t, EXPERTS)], hT[s][:, bass.ts(t, P)], c.gate[:, :],
                                                start=True, stop=True)
                    last.then_inc(made, 1)


def route(nc, c, name):
    T = TILES
    with ExitStack() as ctx:
        sb = lambda n, shape, dt=F32: ctx.enter_context(nc.sbuf_tensor(f"{name}_{n}", shape, dt))
        take = signals(nc, ctx)
        sem = lambda n: take(f"{name}_{n}")
        largest = sb("largest", [P, T])
        first = sb("first", [P, T])
        total = sb("total", [P, T])
        chosen = sb("chosen", [P, T, EXPERTS])
        work = sb("work", [P, T, EXPERTS])
        exps = sb("exps", [P, T, EXPERTS])
        before = [sb(f"before_{n}", [P, T, EXPERTS]) for n in range(2)]
        count = sb("count", [P, EXPERTS])
        count_int = sb("count_int", [P, EXPERTS], I32)
        start = sb("start", [P, EXPERTS + 1])
        passed = sb("passed", [1, SORTED, EXPERTS])
        number = sb("number", [1, SORTED])
        shifted, expd, one_hot, counted, routed, sent = (sem(n) for n in ("shifted", "expd", "one_hot", "counted", "routed", "sent"))
        wide = lambda a: a.unsqueeze(2).to_broadcast([P, T, EXPERTS])
        block = ctx.enter_context(nc.Block())

        @block.scalar
        def _(act):
            act.wait_ge(shifted, 1)
            nc.scalar.activation(exps[:, :, :], exps[:, :, :], ACT.Exp).then_inc(expd, 1)

        @block.tensor
        def _(pe):
            pe.wait_ge(one_hot, 1)
            flat = chosen[:, :, :].rearrange("p t e -> p (t e)")
            n = T * EXPERTS
            nc.tensor.matmul(c.PS[:, 0, 0:n], c.before[:, :], flat, start=True, stop=True)
            nc.tensor.matmul(c.PS[:, 1, 0:n], c.minus_ones[:, :], flat, start=True, stop=True).then_inc(counted, 1)

        @block.vector
        def _(dve):
            v = nc.vector
            v.tensor_reduce(largest[:, :], c.logits[:, 0:T, :], AX, ALU.max)
            dve.drain()
            v.tensor_tensor(exps[:, :, :], c.logits[:, 0:T, :], wide(largest[:, :]), ALU.subtract).then_inc(shifted, 1)
            v.tensor_tensor(chosen[:, :, :], c.logits[:, 0:T, :], wide(largest[:, :]), ALU.is_equal)
            dve.drain()
            v.tensor_tensor(work[:, :, :], chosen[:, :, :], c.experts[:, :].unsqueeze(1).to_broadcast([P, T, EXPERTS]), ALU.mult)
            dve.drain()
            v.tensor_reduce(first[:, :], work[:, :, :], AX, ALU.min)
            dve.drain()
            v.tensor_tensor(chosen[:, :, :], wide(first[:, :]), c.experts[:, :].unsqueeze(1).to_broadcast([P, T, EXPERTS]),
                            ALU.is_equal).then_inc(one_hot, 1)
            dve.wait_ge(expd, 1)
            v.tensor_reduce(total[:, :], exps[:, :, :], AX, ALU.add)
            dve.drain()
            v.reciprocal(c.weight[:, 0:T], total[:, :])
            dve.wait_ge(counted, 1)
            v.tensor_scalar(before[0][:, :, :], c.PS[:, 1, 0:T * EXPERTS].rearrange("p (t e) -> p t e", e=EXPERTS), -1.0, None, ALU.mult)
            dve.drain()
            k, src = 1, 0
            while k < T:
                a, b = before[src], before[1 - src]
                v.tensor_tensor(b[:, k:, :], a[:, k:, :], a[:, 0:T - k, :], ALU.add)
                v.tensor_copy(b[:, 0:k, :], a[:, 0:k, :])
                dve.drain()
                k, src = 2 * k, 1 - src
            upto = before[src]
            v.tensor_scalar(count[:, :], upto[:, T - 1, :], float(P - 1), None, ALU.add)
            dve.drain()
            v.tensor_copy(count_int[:, :], count[:, :])
            dve.drain()
            v.tensor_scalar(count_int[:, :], count_int[:, :], 7, 7, ALU.arith_shift_right, ALU.arith_shift_left)
            dve.drain()
            v.tensor_copy(count[:, :], count_int[:, :])
            v.memset(start[:, :], 0.0)
            dve.drain()
            for e in range(EXPERTS):
                v.tensor_tensor(start[:, e + 1:e + 2], start[:, e:e + 1], count[:, e:e + 1], ALU.add)
                dve.drain()
            other = before[1 - src]
            v.tensor_tensor(other[:, :, :], upto[:, :, :], c.PS[:, 0, 0:T * EXPERTS].rearrange("p (t e) -> p t e", e=EXPERTS), ALU.add)
            dve.drain()
            v.tensor_tensor(other[:, :, :], other[:, :, :], start[:, 0:EXPERTS].unsqueeze(1).to_broadcast([P, T, EXPERTS]), ALU.add)
            v.tensor_copy(work[:, :, :], c.PS[:, 1, 0:T * EXPERTS].rearrange("p (t e) -> p t e", e=EXPERTS))
            dve.drain()
            v.tensor_tensor(other[:, :, :], other[:, :, :], work[:, :, :], ALU.add)
            dve.drain()
            v.tensor_tensor(other[:, :, :], other[:, :, :], chosen[:, :, :], ALU.mult)
            dve.drain()
            v.tensor_reduce(total[:, :], other[:, :, :], AX, ALU.add)
            dve.drain()
            v.tensor_copy(c.row_of[:, 0:T], total[:, :]).then_inc(routed, 1)
            v.tensor_tensor(passed[:, :, :], start[0:1, 1:EXPERTS + 1].unsqueeze(1).to_broadcast([1, SORTED, EXPERTS]),
                            c.tile_start[:, :].unsqueeze(2).to_broadcast([1, SORTED, EXPERTS]), ALU.is_le)
            dve.drain()
            v.tensor_reduce(number[:, :], passed[:, :, :], AX, ALU.add)
            dve.drain()
            v.tensor_scalar(number[:, :], number[:, :], float(EXPERTS - 1), None, ALU.min)
            dve.drain()
            v.tensor_copy(c.tile_expert[:, :], number[:, :])
            dve.drain()

        @block.gpsimd
        def _(pool):
            pool.wait_ge(routed, 1)
            for t in range(T):
                pool.indirect_dma_start(out=c.sorted_in, out_offset=bass.IndirectOffsetOnAxis(ap=c.row_of[:, t:t + 1], axis=0),
                                        in_=c.X[:, t, :], in_offset=None).then_inc(sent, 16)
            pool.wait_ge(sent, 16 * T)


def experts(nc, c, name, gelu):
    with ExitStack() as ctx:
        sb = lambda n, shape: [ctx.enter_context(nc.sbuf_tensor(f"{name}_{n}_{s}", shape, F32)) for s in range(LANES)]
        take = signals(nc, ctx)
        sem = lambda n: take(f"{name}_{n}")
        xs = sb("xs", [P, P])
        xsT = sb("xsT", [P, P])
        hid = sb("hid", [P, WIDE])
        hidT = sb("hidT", [P, WIDE])
        landed = [sem(f"landed_{s}") for s in range(LANES)]
        turned, turned_kept, made, kept, hidden_turned, hidden_kept, out_made, out_kept, stored = (
            sem(n) for n in ("turned", "turned_kept", "made", "kept", "hidden_turned", "hidden_kept", "out_made", "out_kept", "stored"))
        bank = lambda s, b: c.PS[:, 2 * s + b, :]
        w1 = c.w1[:, :, :].rearrange("p e f -> p (e f)")
        w2 = c.w2[:, :, :, :].rearrange("p e b d -> p (e b d)")
        b2 = c.b2[:, :, :].rearrange("p e d -> p (e d)")
        block = ctx.enter_context(nc.Block())

        @block.sync
        def _(sp):
            for s in range(LANES):
                sp.dma_start(xs[s][:, :], c.sorted_in[s * P:(s + 1) * P, :]).then_inc(landed[s], 16)
            with sp.Fori(0, SORTED - LANES + 1, LANES) as i:
                for s in range(LANES):
                    sp.wait_ge(turned, both(i, s))
                    sp.dma_start(xs[s][:, :], c.sorted_in[bass.ds((i + s + LANES) * P, P), :]).then_inc(landed[s], 16)
                for s in range(LANES):
                    sp.wait_ge(out_kept, both(i, s))
                    sp.dma_start(c.sorted_out[bass.ds((i + s) * P, P), :],
                                 c.X[:, bass.ds(i + s, 1), :].rearrange("p o d -> p (o d)")).then_inc(stored, 16)
            sp.wait_ge(stored, SORTED * 16)
            for s in range(LANES):
                sp.wait_ge(landed[s], (SORTED // LANES + 1) * 16)

        @block.tensor
        def _(pe):
            turn = lambda s: nc.tensor.transpose(bank(s, 0)[:, 0:P], xs[s][:, :], c.ident[:, :]).then_inc(turned, 1)
            for s in range(LANES):
                pe.wait_ge(landed[s], 16)
                turn(s)
            with pe.Fori(0, SORTED - LANES + 1, LANES) as i:
                which = []
                for s in range(LANES):
                    which.append(pe.value_load(c.tile_expert[0:1, bass.ds(i + s, 1)], min_val=0, max_val=EXPERTS - 1))
                    pe.wait_ge(turned_kept, both(i, s))
                    nc.tensor.matmul(bank(s, 1), xsT[s][:, :], w1[:, bass.ds(which[s] * WIDE, WIDE)], start=True, stop=True).then_inc(made, 1)
                for s in range(LANES):
                    pe.wait_ge(kept, both(i, s))
                    for b in range(BLOCKS):
                        last = nc.tensor.transpose(bank(s, 0)[:, bass.ts(b, P)], hid[s][:, bass.ts(b, P)], c.ident[:, :])
                    last.then_inc(hidden_turned, 1)
                for s in range(LANES):
                    pe.wait_ge(hidden_kept, both(i, s))
                    for b in range(BLOCKS):
                        last = nc.tensor.matmul(bank(s, 1)[:, 0:P], hidT[s][:, bass.ts(b, P)],
                                                w2[:, bass.ds(which[s] * WIDE + b * P, P)], start=b == 0, stop=b == BLOCKS - 1)
                    last.then_inc(out_made, 1)
                    pe.wait_ge(landed[s], (i + 2 * LANES) * (16 // LANES))
                    turn(s)

        @block.scalar
        def _(act):
            with act.Fori(0, SORTED - LANES + 1, LANES) as i:
                for s in range(LANES):
                    act.wait_ge(made, both(i, s))
                    nc.scalar.activation(hid[s][:, :], bank(s, 1), gelu).then_inc(kept, 1)

        @block.vector
        def _(dve):
            keep = lambda s: nc.vector.tensor_scalar(xsT[s][:, :], bank(s, 0)[:, 0:P], 1.0, None, ALU.add).then_inc(turned_kept, 1)
            for s in range(LANES):
                dve.wait_ge(turned, s + 1)
                keep(s)
            with dve.Fori(0, SORTED - LANES + 1, LANES) as i:
                which = [dve.value_load(c.tile_expert[0:1, bass.ds(i + s, 1)], min_val=0, max_val=EXPERTS - 1) for s in range(LANES)]
                for s in range(LANES):
                    dve.wait_ge(hidden_turned, both(i, s))
                    nc.vector.tensor_copy(hidT[s][:, :], bank(s, 0)).then_inc(hidden_kept, 1)
                for s in range(LANES):
                    dve.wait_ge(out_made, both(i, s))
                    nc.vector.tensor_tensor(c.X[:, bass.ds(i + s, 1), :].rearrange("p o d -> p (o d)"), bank(s, 1)[:, 0:P],
                                            b2[:, bass.ds(which[s] * P, P)], ALU.add).then_inc(out_kept, 1)
                    dve.wait_ge(turned, both(i + LANES, s))
                    keep(s)


def combine(nc, c, name, out):
    with ExitStack() as ctx:
        take = signals(nc, ctx)
        sem = lambda n: take(f"{name}_{n}")
        gathered = [sem(f"gathered_{n}") for n in range(2)]
        added, stored = sem("added"), sem("stored")
        block = ctx.enter_context(nc.Block())

        @block.gpsimd
        def _(pool):
            for g in range(GROUPS_OF_TILES):
                if g >= 2:
                    pool.wait_ge(gathered[g % 2], g // 2 * GROUP * 16)
                for t in range(g * GROUP, (g + 1) * GROUP):
                    pool.indirect_dma_start(out=c.X[:, t, :], out_offset=None, in_=c.sorted_out,
                                            in_offset=bass.IndirectOffsetOnAxis(ap=c.row_of[:, t:t + 1], axis=0)
                                            ).then_inc(gathered[g % 2], 16)

        @block.vector
        def _(dve):
            with dve.Fori(0, TILES - 2 * GROUP + 1, 2 * GROUP) as t:
                for n in range(2):
                    dve.wait_ge(gathered[n], (t + 2 * GROUP) * 8)
                    for j in range(GROUP):
                        at = t + (n * GROUP + j)
                        row = lambda a: a[:, bass.ds(at, 1), :].rearrange("p o d -> p (o d)")
                        last = nc.vector.scalar_tensor_tensor(row(c.H), row(c.X), c.weight[:, bass.ds(at, 1)], row(c.H), ALU.mult, ALU.add)
                    last.then_inc(added, GROUP)

        @block.sync
        def _(sp):
            rows = out.rearrange("b (t p) d -> p (b t) d", p=P)
            with sp.Fori(0, TILES - GROUP + 1, GROUP) as t:
                sp.wait_ge(added, t + GROUP)
                sp.dma_start(rows[:, bass.ds(t, GROUP), :], c.H[:, bass.ds(t, GROUP), :]).then_inc(stored, 16)
            sp.wait_ge(stored, GROUPS_OF_TILES * 16)


INNER = 256
STATE = 64
DIRS = 2
MHEADS = INNER // HEAD
CONV = 4
MIX = 6
ATANH = [1.0 / (2 * k + 1) for k in range(8, 0, -1)]


def mamba(nc, c, ins):
    with ExitStack() as ctx:
        one = lambda n, shape: ctx.enter_context(nc.sbuf_tensor(f"mamba_{n}", shape, F32))
        sb = lambda n, shape: [one(f"{n}_{s}", shape) for s in range(2)]
        take = signals(nc, ctx)
        sem = lambda n: take(f"mamba_{n}")
        m = Chip()
        m.loaded, m.negated, m.joined, m.stats, m.rstd, m.normed, m.uT = map(sem, (
            "loaded", "negated", "joined", "stats", "rstd", "normed", "uT"))
        m.uT_kept, m.bc_mixed, m.x_mixed0, m.x_mixed1, m.x_kept0, m.x_kept1, m.started = map(sem, (
            "uT_kept", "bc_mixed", "x_mixed0", "x_mixed1", "x_kept0", "x_kept1", "started"))
        m.convolved, m.bc_kept, m.gated0, m.gated1, m.gated_kept, m.g_made, m.g_kept = map(sem, (
            "convolved", "bc_kept", "gated0", "gated1", "gated_kept", "g_made", "g_kept"))
        m.dt_raw, m.dt_exp, m.dt_ready, m.steps, m.xT, m.xT_kept, m.bT_kept = map(sem, (
            "dt_raw", "dt_exp", "dt_ready", "steps", "xT", "xT_kept", "bT_kept"))
        m.reach, m.reach_kept, m.ends_kept, m.state, m.state_kept, m.carried, m.carried_kept = map(sem, (
            "reach", "reach_kept", "ends_kept", "state", "state_kept", "carried", "carried_kept"))
        m.span0, m.span0_exp, m.span1, m.span1_exp, m.weights0, m.weights1, m.weights0b = map(sem, (
            "span0", "span0_exp", "span1", "span1_exp", "weights0", "weights1", "weights0b"))
        m.weights1b, m.y0, m.y1, m.yz0, m.yz1, m.sums, m.y_rstd = map(sem, (
            "weights1b", "y0", "y1", "yz0", "yz1", "sums", "y_rstd"))
        m.yzT0, m.yzT1, m.yzT_kept0, m.yzT_kept1, m.projected, m.done = map(sem, (
            "yzT0", "yzT1", "yzT_kept0", "yzT_kept1", "projected", "done"))
        w_in = one("w_in", [P, MIX * P + 2 * INNER + 2 * MHEADS])
        w_mix = w_in[:, 0:MIX * P]
        w_z = w_in[:, MIX * P:MIX * P + 2 * INNER]
        w_dt = w_in[:, MIX * P + 2 * INNER:]
        taps = one("taps", [P, MIX, CONV])
        tap_bias = one("tap_bias", [P, MIX])
        columns = one("columns", [P, 9])
        dt_bias = one("dt_bias", [P, 2 * MHEADS])
        decay = one("decay", [P, 2 * MHEADS])
        skip = one("skip", [P, 4, P])
        out_w = one("out_w", [P, 4 * P])
        projT = one("projT", [P, 2 * P])
        w_out = one("w_out", [P, 4, P])
        w_taps = one("w_taps", [P, CONV, 4 * P])
        inv = one("inv", [P, 2])
        two = one("two", [P, 16])
        minus_one = one("minus_one", [P, 16])
        masks = one("masks", [P, 4, P])
        before, after, upto, since = (masks[:, k, :] for k in range(4))
        x1 = sb("x1", [P, SEQ_TILES, P])
        u = sb("u", [P, SEQ_TILES, P])
        uT = sb("uT", [P, SEQ_TILES * P])
        mix = sb("mix", [P, MIX, SEQ_TILES * P])
        z = sb("z", [P, SEQ_TILES, DIRS * INNER])
        g = sb("g", [P, SEQ_TILES, DIRS, P])
        dtx = sb("dtx", [P, SEQ_TILES, DIRS * INNER])
        dtxe = sb("dtxe", [P, DIRS, INNER])
        bT = sb("bT", [P, DIRS, P])
        steps = sb("steps", [P, SEQ_TILES, DIRS, MHEADS * P])
        weights = sb("weights", [P, DIRS, MHEADS * P])
        reach = sb("reach", [P, 4, MHEADS])
        state = sb("state", [P, INNER])
        carried = sb("carried", [P, DIRS, INNER])
        yz = sb("yz", [P, SEQ_TILES, DIRS * INNER])
        yzT = sb("yzT", [P, SEQ_TILES, 4, P])
        junk = sb("junk", [P, INNER])
        sums = sb("sums", [P, SEQ_TILES * DIRS])
        rnorm = sb("rnorm", [P, SEQ_TILES])
        norm = [NormBuffers(nc, ctx, f"mamba_norm_{s}") for s in range(2)]
        n_dt = 2 * SEQ_TILES * 2 * MHEADS
        dt_raw, dt_neg, dt_exp, dt_rec, dt_z, dt_z2, dt_p, dt, step_log = (one(n, [P, n_dt]) for n in (
            "dt_raw", "dt_neg", "dt_exp", "dt_rec", "dt_z", "dt_z2", "dt_p", "dt", "step_log"))
        dt_of = lambda a, s: a[:, s * 16:(s + 1) * 16].rearrange("p (t d h) -> p t d h", t=2, d=2)
        rows = sb("rows", [P, SEQ_TILES, P])
        row_ids = [[ctx.enter_context(nc.sbuf_tensor(f"mamba_row_id_{s}_{t}", [P, 1], I32)) for t in range(SEQ_TILES)] for s in range(2)]
        gathered = [sem(f"gathered_{s}") for s in range(2)]
        part = lambda s: bass.ts(s, 16)
        bank = lambda s, b: c.PS[:, 4 * s + b, :]
        banks = lambda s, b, n: c.PS[:, 4 * s + b:4 * s + b + n, :]
        mixed = lambda s, b: bank(s, 1 + b // 2)[:, (b % 2) * 256:(b % 2) * 256 + 256]
        EYE = c.ident

        with nc.Block() as block:
            loads = [(w_in[:, :], "m_w_in"), (taps[:, :, :], "m_taps"), (tap_bias[:, :], "m_tap_bias"), (columns[:, :], "m_columns"),
                     (out_w[:, :], "m_out_w"), (projT[:, :], "m_projT"), (masks[:, :, :], "m_masks")]
            LOADED = (len(loads) + 3) * 16

            @block.sync
            def _(sp):
                for at, name in loads:
                    sp.dma_start(at, ins[name]).then_inc(m.loaded, 16)
                sp.dma_start(dt_bias[:, :], broadcast_rows(ins["m_dt_bias"], 8)).then_inc(m.loaded, 16)
                sp.dma_start(decay[:, :], broadcast_rows(ins["m_A_log"], 8)).then_inc(m.loaded, 16)
                sp.dma_start(w_taps[:, :, :].rearrange("p k n -> p (k n)"), broadcast_rows(ins["m_tap_rows"], CONV * 4 * P)).then_inc(m.loaded, 16)
                sp.wait_ge(m.loaded, LOADED)

            @block.scalar
            def _(act):
                act.wait_ge(m.loaded, LOADED)
                nc.scalar.activation(decay[:, :], decay[:, :], ACT.Exp).then_inc(m.negated, 1)

            @block.tensor
            def _(pe):
                pe.wait_ge(m.loaded, LOADED)
                for b in range(4):
                    last = nc.tensor.matmul(c.PS[:, 0, bass.ts(b, P)], out_w[:, bass.ts(b, P)], projT[:, bass.ts(b // 2, P)], start=True, stop=True)
                last.then_inc(m.joined, 1)

            @block.vector
            def _(dve):
                dve.wait_ge(m.loaded, LOADED)
                nc.vector.tensor_scalar(w_in[:, :], w_in[:, :], columns[:, 0:1], None, ALU.mult)
                for b in range(4):
                    nc.vector.tensor_scalar(skip[:, b, :], EYE[:, :], columns[:, 1 + b:2 + b], None, ALU.mult)
                nc.vector.memset(inv[:, :], 1.0 / INNER)
                nc.vector.memset(two[:, :], 2.0)
                nc.vector.memset(minus_one[:, :], -1.0)
                dve.drain()
                for k in range(CONV):
                    nc.vector.tensor_tensor(w_taps[:, k, :], w_taps[:, k, :], w_mix[:, 0:4 * P], ALU.mult)
                dve.wait_ge(m.negated, 1)
                nc.vector.tensor_scalar(decay[:, :], decay[:, :], -1.0, None, ALU.mult)
                dve.wait_ge(m.joined, 1)
                for b in range(4):
                    nc.vector.tensor_scalar(w_out[:, b, :], c.PS[:, 0, bass.ts(b, P)], columns[:, 5 + b:6 + b], None, ALU.mult)
                dve.drain()

        block = ctx.enter_context(nc.Block())

        @block.tensor
        def _(pe):
            mm = nc.tensor.matmul

            def spans(s, t):
                for d in range(2):
                    last = mm(bank(s, 3 * d), (after, before)[d], steps[s][:, t, d, :], start=True, stop=True)
                return last

            def outputs(s, t):
                for b in range(4):
                    out = bank(s, 1 + t)[:, bass.ts(b, P)]
                    mm(out, mix[s][:, b, bass.ts(t, P)], skip[:, b, :], start=True, stop=False)
                    for h in range(2):
                        last = mm(out[:, bass.ts(h, HEAD)], weights[s][:, b // 2, bass.ts(2 * (b % 2) + h, P)],
                                  dtx[s][:, t, b * P + h * HEAD:b * P + (h + 1) * HEAD], start=False, stop=h == 1)
                return last

            def first(i, s):
                yield 2.41
                pe.wait_ge(m.normed, both(i, s))
                for t in range(2):
                    last = nc.tensor.transpose(bank(s, 0)[:, bass.ts(t, P)], u[s][:, t, :], EYE[:, :])
                last.then_inc(m.uT, 1)
                yield 6.63
                pe.wait_ge(m.uT_kept, both(i, s))
                for t in range(2):
                    mm(bank(s, 0)[:, 256 + 8 * t:264 + 8 * t], uT[s][:, bass.ts(t, P)], w_dt, start=True, stop=True)
                for b in (4, 5):
                    last = mm(mixed(s, b), w_mix[:, bass.ts(b, P)], uT[s][:, :], start=True, stop=True)
                last.then_inc(m.bc_mixed, 1)
                n = SEQ_TILES * P
                for b in range(4):
                    for k in range(CONV):
                        to, of = (slice(k, n), slice(0, n - k)) if b < 2 else (slice(0, n - k), slice(k, n))
                        last = mm(mixed(s, b)[:, to], w_taps[:, k, bass.ts(b, P)], uT[s][:, of], start=k == 0, stop=k == CONV - 1)
                    if b % 2:
                        last.then_inc((m.x_mixed0, m.x_mixed1)[b // 2], 1)
                yield 9.79
                for t in range(2):
                    pe.wait_ge((m.x_kept0, m.x_kept1)[t], both(i, s))
                    mm(bank(s, 1 + t), uT[s][:, bass.ts(t, P)], w_z, start=True, stop=True).then_inc((m.gated0, m.gated1)[t], 1)
                yield 12.31
                pe.wait_ge(m.bc_kept, both(i, s))
                pe.wait_ge(m.dt_raw, both(i, s))
                for t in range(2):
                    for d in range(2):
                        r = bass.ts(d, STATE)
                        last = mm(bank(s, 3 - 3 * d)[:, bass.ts(t, P)], mix[s][r, 4, bass.ts(t, P)], mix[s][r, 5, bass.ts(t, P)], start=True, stop=True)
                last.then_inc(m.g_made, 1)
                yield 16.83
                pe.wait_ge(m.gated_kept, both(i, s))
                pe.wait_ge(m.g_kept, both(i, s))
                for t in range(2):
                    nc.tensor.transpose(bank(s, 3)[:, bass.ts(t, P)], mix[s][:, 4, bass.ts(t, P)], EYE[:, :])
                for t in range(2):
                    for b in range(4):
                        last = nc.tensor.transpose(bank(s, 1 + t)[:, bass.ts(b, P)], mix[s][:, b, bass.ts(t, P)], EYE[:, :])
                last.then_inc(m.xT, 1)
                yield 16.84
                pe.wait_ge(m.dt_ready, both(i, s))
                a = dt_of(step_log, s)
                for k, (mask, t, d) in enumerate(((upto, 1, 0), (since, 0, 1), (after, 0, 0), (before, 1, 1))):
                    last = mm(bank(s, 0)[:, bass.ts(k, MHEADS)], mask, a[:, t, d, :], start=True, stop=True)
                last.then_inc(m.reach, 1)
                yield 18.25
                pe.wait_ge(m.ends_kept, both(i, s))
                pe.wait_ge(m.bT_kept, both(i, s))
                for d in range(2):
                    last = mm(c.PS[bass.ts(d, STATE), 4 * s + 3, 0:INNER], bT[s][:, d, bass.ts(d, STATE)], dtxe[s][:, d, :], start=True, stop=True)
                last.then_inc(m.state, 1)
                yield 19.57
                pe.wait_ge(m.state_kept, both(i, s))
                for d in range(2):
                    r = bass.ts(d, STATE)
                    last = mm(bank(s, 3 * d)[:, 0:INNER], mix[s][r, 5, bass.ts(1 - d, P)], state[s][r, :], start=True, stop=True)
                last.then_inc(m.carried, 1)
                yield 21.56
                pe.wait_ge(m.steps, both(i, s))
                pe.wait_ge(m.carried_kept, both(i, s))
                pe.wait_ge(m.reach_kept, both(i, s))
                spans(s, 0).then_inc(m.span0, 1)

            def second(i, s):
                yield 0.82
                pe.wait_ge(m.weights0, both(i, s))
                pe.wait_ge(m.weights0b, both(i, s))
                pe.wait_ge(m.xT_kept, both(i, s))
                outputs(s, 0).then_inc(m.y0, 1)
                yield 3.9
                pe.wait_ge(m.span0_exp, both(i, s))
                spans(s, 1).then_inc(m.span1, 1)
                yield 8.67
                pe.wait_ge(m.weights1, both(i, s))
                pe.wait_ge(m.weights1b, both(i, s))
                outputs(s, 1).then_inc(m.y1, 1)
                yield 17.18
                for t in range(2):
                    pe.wait_ge((m.yz0, m.yz1)[t], both(i, s))
                    for b in range(4):
                        last = nc.tensor.transpose(bank(s, 1 + t)[:, bass.ts(b, P)], yz[s][:, t, bass.ts(b, P)], EYE[:, :])
                    last.then_inc((m.yzT0, m.yzT1)[t], 1)
                yield 20.63
                for t in range(2):
                    pe.wait_ge((m.yzT_kept0, m.yzT_kept1)[t], both(i, s))
                    for d in range(2):
                        for b in range(2):
                            last = mm(bank(s, 3)[:, bass.ts(2 * t + d, P)], yzT[s][:, t, 2 * d + b, :], w_out[:, 2 * d + b, :], start=b == 0, stop=b == 1)
                last.then_inc(m.projected, 1)

            skewed(pe, first, second)

        @block.scalar
        def _(act):
            a = nc.scalar.activation
            def first(i, s):
                yield 7.28
                act.wait_ge(m.bc_mixed, both(i, s))
                for b in (4, 5):
                    last = a(mix[s][:, b, :], mixed(s, b), ACT.Identity, bias=tap_bias[:, b:b + 1], scale=taps[:, b, CONV - 1:CONV])
                last.then_inc(m.started, 1)
                yield 8.15
                act.wait_ge(m.dt_raw, both(i, s))
                a(dt_exp[:, part(s)], dt_neg[:, part(s)], ACT.Exp).then_inc(m.dt_exp, 1)
                yield 8.16
                for b in range(4):
                    if b % 2 == 0:
                        act.wait_ge((m.x_mixed0, m.x_mixed1)[b // 2], both(i, s))
                    last = a(mix[s][:, b, :], mixed(s, b), ACT.Silu, bias=tap_bias[:, b:b + 1])
                    if b % 2:
                        last.then_inc((m.x_kept0, m.x_kept1)[b // 2], 1)
                yield 11.22
                act.wait_ge(m.convolved, both(i, s))
                a(mix[s][:, 4:, :], mix[s][:, 4:, :], ACT.Silu).then_inc(m.bc_kept, 1)
                yield 13.17
                for t in range(2):
                    act.wait_ge((m.gated0, m.gated1)[t], both(i, s))
                    last = a(z[s][:, t, :], bank(s, 1 + t), ACT.Silu)
                last.then_inc(m.gated_kept, 1)
                yield 16.85
                act.wait_ge(m.reach, both(i, s))
                a(reach[s][:, :, :], bank(s, 0)[:, 0:16].rearrange("p (k h) -> p k h", h=MHEADS), ACT.Exp).then_inc(m.reach_kept, 1)
                yield 19.56
                act.wait_ge(m.state, both(i, s))
                a(state[s][:, :], bank(s, 3)[:, 0:INNER], ACT.Copy).then_inc(m.state_kept, 1)
                yield 21.57
                act.wait_ge(m.span0, both(i, s))
                for d in range(2):
                    last = a(weights[s][:, d, :], bank(s, 3 * d), ACT.Exp)
                last.then_inc(m.span0_exp, 1)

            def second(i, s):
                yield 5.95
                act.wait_ge(m.span1, both(i, s))
                act.wait_ge(m.y0, both(i, s))
                for d in range(2):
                    last = a(weights[s][:, d, :], bank(s, 3 * d), ACT.Exp)
                last.then_inc(m.span1_exp, 1)
                yield 18.79
                for t in range(2):
                    act.wait_ge((m.yzT0, m.yzT1)[t], both(i, s))
                    a(yzT[s][:, t, :, :].rearrange("p b n -> p (b n)"), bank(s, 1 + t), ACT.Copy).then_inc((m.yzT_kept0, m.yzT_kept1)[t], 1)
                yield 20.37
                for t in range(2):
                    act.wait_ge((m.yz0, m.yz1)[t], both(i, s))
                    for d in range(2):
                        k = 2 * t + d
                        a(junk[s][:, :], yz[s][:, t, bass.ts(d, INNER)], ACT.Square, accum_out=sums[s][:, k:k + 1])
                        act.drain()
                a(sums[s][:, :], sums[s][:, :], ACT.Copy).then_inc(m.sums, 1)

            skewed(act, first, second)

        @block.gpsimd
        def _(pool):
            tt = nc.gpsimd.tensor_tensor

            def gather(i, s):
                for t in range(SEQ_TILES):
                    nc.gpsimd.tensor_copy(row_ids[s][t][:, :], c.row_of[:, bass.ds((i + s) * 2 + t, 1)])
                pool.drain()
                for t in range(SEQ_TILES):
                    pool.indirect_dma_start(out=rows[s][:, t, :], out_offset=None, in_=c.sorted_out,
                                            in_offset=bass.IndirectOffsetOnAxis(ap=row_ids[s][t][:, :], axis=0)).then_inc(gathered[s], 16)

            def rows_rstd(s):
                norm_rstd(nc, pool, c, norm[s])
                pool.drain()
                r, q = norm[s].rstd[:, :], rnorm[s][:, :]
                tt(q, norm[s].stat[:, :, 1], r, ALU.mult)
                pool.drain()
                tt(q, q, r, ALU.mult)
                pool.drain()
                tt(q, q, c.eps[:, 0:2], ALU.add)
                pool.drain()
                tt(q, q, c.minus_half[:, 0:2], ALU.pow)
                pool.drain()
                tt(q, q, r, ALU.mult).then_inc(m.rstd, 1)

            for s in range(2):
                gather(0, s)
            for s in range(2):
                pool.wait_ge(m.stats, s + 1)
                rows_rstd(s)
                gather(2, s)
            def first(i, s):
                yield 8.36
                pool.wait_ge(m.dt_exp, both(i, s))
                rec, z1, z2, p, x = (one_[:, part(s)] for one_ in (dt_rec, dt_z, dt_z2, dt_p, dt_raw))
                tt(rec, dt_exp[:, part(s)], two[:, :], ALU.add)
                pool.drain()
                tt(rec, rec, minus_one[:, :], ALU.pow)
                pool.drain()
                tt(z1, dt_exp[:, part(s)], rec, ALU.mult)
                pool.drain()
                tt(z2, z1, z1, ALU.mult)
                pool.drain()
                nc.gpsimd.tensor_scalar(p, z2, ATANH[0], None, ALU.mult)
                for k in ATANH[1:] + [1.0]:
                    pool.drain()
                    nc.gpsimd.tensor_scalar(p, p, k, None, ALU.add)
                    pool.drain()
                    tt(p, p, z2 if k < 1.0 else z1, ALU.mult)
                nc.gpsimd.tensor_scalar(x, x, 0.0, None, ALU.max)
                pool.drain()
                tt(x, x, p, ALU.add)
                pool.drain()
                tt(dt[:, part(s)], x, p, ALU.add)
                pool.drain()
                tt(step_log[:, part(s)].rearrange("p (t n) -> p t n", n=8), dt[:, part(s)].rearrange("p (t n) -> p t n", n=8),
                   decay[:, :].unsqueeze(1).to_broadcast([P, 2, 8]), ALU.mult).then_inc(m.dt_ready, 1)
                pool.drain()
                yield 9.97
                for t in range(2):
                    for d in range(2):
                        last = tt(steps[s][:, t, d, :].rearrange("p (h n) -> p h n", h=MHEADS),
                                  (upto, since)[d].unsqueeze(1).to_broadcast([P, MHEADS, P]),
                                  dt_of(step_log, s)[:, t, d, :].unsqueeze(2).to_broadcast([P, MHEADS, P]), ALU.mult)
                last.then_inc(m.steps, 1)
                yield 24.17
                pool.wait_ge(m.span0_exp, both(i, s))
                w = weights[s][:, 1, :].rearrange("p (h n) -> p h n", h=MHEADS)
                tt(w, w, g[s][:, 0, 1, :].unsqueeze(1).to_broadcast([P, MHEADS, P]), ALU.mult).then_inc(m.weights0b, 1)

            def second(i, s):
                yield 6.45
                pool.wait_ge(m.span1_exp, both(i, s))
                w = weights[s][:, 1, :].rearrange("p (h n) -> p h n", h=MHEADS)
                tt(w, w, g[s][:, 1, 1, :].unsqueeze(1).to_broadcast([P, MHEADS, P]), ALU.mult).then_inc(m.weights1b, 1)
                yield 9.94
                pool.wait_ge(m.stats, both(i + 2, s))
                rows_rstd(s)
                gather(i + 4, s)
                yield 20.38
                pool.wait_ge(m.sums, both(i, s))
                q = sums[s][:, :]
                tt(q, q, inv[:, 0:1].to_broadcast([P, 4]), ALU.mult)
                pool.drain()
                tt(q, q, c.eps[:, :], ALU.add)
                pool.drain()
                tt(q, q, c.minus_half[:, :], ALU.pow).then_inc(m.y_rstd, 1)

            skewed(pool, first, second)
            for s in range(2):
                pool.wait_ge(gathered[s], (SEQS // 2 + 2) * 2 * 16)

        @block.vector
        def _(dve):
            v = nc.vector
            row = lambda a, t: a[:, bass.ds(t, 1), :].rearrange("p o d -> p (o d)")

            def gate_outputs(s, t):
                at, other = bass.ts(1 - t, INNER), bass.ts(t, INNER)
                v.tensor_tensor(yz[s][:, t, at], bank(s, 1 + t)[:, at], carried[s][:, 1 - t, :], ALU.add)
                v.tensor_tensor(yz[s][:, t, other], bank(s, 1 + t)[:, other], z[s][:, t, other], ALU.mult)
                dve.drain()
                return v.tensor_tensor(yz[s][:, t, at], yz[s][:, t, at], z[s][:, t, at], ALU.mult)

            def rows_stats(i, s):
                dve.wait_ge(gathered[s], (i + 2) * 16)
                for t in range(2):
                    at = (i + s) * 2 + t
                    v.scalar_tensor_tensor(row(c.H, at), rows[s][:, t, :], c.weight[:, bass.ds(at, 1)], row(c.H, at), ALU.mult, ALU.add)
                dve.drain()
                for t in range(2):
                    v.bn_stats(norm[s].sums[:, t, :], row(c.H, (i + s) * 2 + t))
                dve.drain()
                for t in range(2):
                    last = v.bn_aggr(norm[s].stat[:, t, :], norm[s].sums[:, t, :])
                return last

            for s in range(2):
                rows_stats(0, s).then_inc(m.stats, 1)
            def first(i, s):
                yield 2.4
                dve.drain()
                dve.wait_ge(m.rstd, both(i, s))
                for t in range(2):
                    mean = norm[s].stat[:, t, 0:1]
                    v.tensor_scalar(x1[s][:, t, :], row(c.H, (i + s) * 2 + t), mean, norm[s].rstd[:, t:t + 1], ALU.subtract, ALU.mult)
                    last = v.tensor_scalar(u[s][:, t, :], row(c.H, (i + s) * 2 + t), mean, rnorm[s][:, t:t + 1], ALU.subtract, ALU.mult)
                last.then_inc(m.normed, 1)
                yield 4.27
                dve.wait_ge(m.uT, both(i, s))
                v.tensor_copy(uT[s][:, :], bank(s, 0)[:, 0:256]).then_inc(m.uT_kept, 1)
                yield 6.64
                dve.wait_ge(m.bc_mixed, both(i, s))
                v.tensor_tensor(dt_raw[:, part(s)].rearrange("p (t n) -> p t n", t=2), bank(s, 0)[:, 256:272].rearrange("p (t n) -> p t n", t=2),
                                dt_bias[:, :].unsqueeze(1).to_broadcast([P, 2, 8]), ALU.add)
                dve.drain()
                v.scalar_tensor_tensor(dt_neg[:, part(s)], dt_raw[:, part(s)], -1.0, dt_raw[:, part(s)], ALU.mult, ALU.min).then_inc(m.dt_raw, 1)
                yield 7.29
                dve.wait_ge(m.started, both(i, s))
                for k in range(1, CONV):
                    for b in (4, 5):
                        src = mixed(s, b)
                        for d, r in ((0, slice(0, 64)), (1, slice(64, P))):
                            n = SEQ_TILES * P
                            to, of = (slice(k, n), slice(0, n - k)) if d == 0 else (slice(0, n - k), slice(k, n))
                            last = v.scalar_tensor_tensor(mix[s][r, b, to], src[r, of], taps[r, b, CONV - 1 - k:CONV - k], mix[s][r, b, to], ALU.mult, ALU.add)
                    if k < CONV - 1:
                        dve.drain()
                last.then_inc(m.convolved, 1)
                yield 16.82
                dve.wait_ge(m.g_made, both(i, s))
                for d in range(2):
                    last = v.tensor_tensor(g[s][:, :, d, :], bank(s, 3 - 3 * d)[:, 0:256].rearrange("p (t n) -> p t n", t=2),
                                           (upto, since)[d].unsqueeze(1).to_broadcast([P, 2, P]), ALU.mult)
                last.then_inc(m.g_kept, 1)
                yield 16.94
                dve.wait_ge(m.xT, both(i, s))
                dve.wait_ge(m.dt_ready, both(i, s))
                v.tensor_copy(bT[s][:, :, :], bank(s, 3)[:, 0:256].rearrange("p (t n) -> p t n", t=2)).then_inc(m.bT_kept, 1)
                v.tensor_tensor(dtx[s][:, :, :].rearrange("p t (h d) -> p (t h) d", d=HEAD), banks(s, 1, 2).rearrange("p t (h d) -> p (t h) d", d=HEAD),
                                dt[:, part(s)].unsqueeze(2).to_broadcast([P, 16, HEAD]), ALU.mult).then_inc(m.xT_kept, 1)
                yield 18.15
                dve.drain()
                dve.wait_ge(m.reach_kept, both(i, s))
                for d in range(2):
                    last = v.tensor_tensor(dtxe[s][:, d, :].rearrange("p (h d) -> p h d", d=HEAD), dtx[s][:, d, bass.ts(d, INNER)].rearrange("p (h d) -> p h d", d=HEAD),
                                           reach[s][:, 2 + d, :].unsqueeze(2).to_broadcast([P, MHEADS, HEAD]), ALU.mult)
                last.then_inc(m.ends_kept, 1)
                yield 19.95
                dve.wait_ge(m.carried, both(i, s))
                for d in range(2):
                    last = v.tensor_tensor(carried[s][:, d, :].rearrange("p (h d) -> p h d", d=HEAD), bank(s, 3 * d)[:, 0:INNER].rearrange("p (h d) -> p h d", d=HEAD),
                                           reach[s][:, d, :].unsqueeze(2).to_broadcast([P, MHEADS, HEAD]), ALU.mult)
                last.then_inc(m.carried_kept, 1)

            def second(i, s):
                yield 0.81
                dve.wait_ge(m.span0_exp, both(i, s))
                w = weights[s][:, 0, :].rearrange("p (h n) -> p h n", h=MHEADS)
                v.tensor_tensor(w, w, g[s][:, 0, 0, :].unsqueeze(1).to_broadcast([P, MHEADS, P]), ALU.mult).then_inc(m.weights0, 1)
                yield 8.66
                dve.wait_ge(m.span1_exp, both(i, s))
                w = weights[s][:, 0, :].rearrange("p (h n) -> p h n", h=MHEADS)
                v.tensor_tensor(w, w, g[s][:, 1, 0, :].unsqueeze(1).to_broadcast([P, MHEADS, P]), ALU.mult).then_inc(m.weights1, 1)
                yield 8.67
                rows_stats(i + 2, s).then_inc(m.stats, 1)
                yield 13.55
                dve.wait_ge(m.y0, both(i, s))
                gate_outputs(s, 0).then_inc(m.yz0, 1)
                yield 13.92
                dve.wait_ge(m.y1, both(i, s))
                gate_outputs(s, 1).then_inc(m.yz1, 1)
                yield 25.46
                dve.wait_ge(m.projected, both(i, s))
                dve.wait_ge(m.y_rstd, both(i, s))
                for d in range(2):
                    for t in range(2):
                        k = 2 * t + d
                        v.scalar_tensor_tensor(x1[s][:, t, :], bank(s, 3)[:, bass.ts(k, P)], sums[s][:, k:k + 1], x1[s][:, t, :], ALU.mult, ALU.add)
                    dve.drain()
                here = bass.ds((i + s) * 2, 2)
                v.tensor_tensor(c.H[:, here, :], c.H[:, here, :], x1[s][:, :, :], ALU.add).then_inc(m.done, 1)

            skewed(dve, first, second)


AHEADS, AHEAD = 8, 16
GROUPS = 2
LANE = 32


def attention(nc, c, ins, prefetch=lambda sp: None):
    with ExitStack() as ctx:
        one = lambda n, shape: ctx.enter_context(nc.sbuf_tensor(f"attention_{n}", shape, F32))
        sb = lambda n, shape: [one(f"{n}_{s}", shape) for s in range(2)]
        take = signals(nc, ctx)
        sem = lambda n: take(f"attention_{n}")
        m = Chip()
        m.loaded, m.cleared, m.stats, m.rstd, m.normed, m.xT, m.xT_kept = map(sem, (
            "loaded", "cleared", "stats", "rstd", "normed", "xT", "xT_kept"))
        m.qk_made, m.qk_kept, m.k_kept, m.v_made, m.v_kept, m.top_kept0, m.top_kept1 = map(sem, (
            "qk_made", "qk_kept", "k_kept", "v_made", "v_kept", "top_kept0", "top_kept1"))
        m.scored0, m.scored1, m.topT, m.q_shifted, m.summed0, m.summed1, m.raw_kept0 = map(sem, (
            "scored0", "scored1", "topT", "q_shifted", "summed0", "summed1", "raw_kept0"))
        m.raw_kept1, m.sums_spread0, m.sums_spread1, m.oT_kept, m.projected, m.xb_ready, m.done = map(sem, (
            "raw_kept1", "sums_spread0", "sums_spread1", "oT_kept", "projected", "xb_ready", "done"))
        spread = [sem(f"spread_{h}") for h in range(AHEADS)]
        exps = [sem(f"exps_{h}") for h in range(AHEADS)]
        w_q = one("w_q", [P, GROUPS * P])
        w_k = one("w_k", [P, GROUPS * P])
        w_v = one("w_v", [P, P])
        w_o = one("w_o", [P, GROUPS, P])
        lane_sums = one("lane_sums", [P, P])
        b_q = one("b_q", [1, GROUPS * P])
        b_k = one("b_k", [1, GROUPS * P])
        b_v = one("b_v", [1, P])
        b_o = one("b_o", [P, P])
        x3 = sb("x3", [P, SEQ_TILES, P])
        xb = sb("xb", [P, SEQ_TILES, P])
        xT = sb("xT", [P, SEQ_TILES * P])
        q = sb("q", [P, GROUPS, SEQ_TILES * P])
        k = sb("k", [P, GROUPS, 4, SEQ_TILES * P])
        v = sb("v", [P, SEQ_TILES, AHEADS, LANE])
        top = sb("top", [P, SEQ_TILES, GROUPS, 4, LANE])
        probs = sb("probs", [P, AHEADS, SEQ_TILES, SEQ_TILES * P])
        raw = sb("raw", [P, GROUPS * SEQ_TILES * P])
        share = sb("share", [P, GROUPS * SEQ_TILES * P])
        oT = sb("oT", [P, GROUPS, SEQ_TILES * P])
        norm = [NormBuffers(nc, ctx, f"attention_norm_{s}") for s in range(2)]
        bank = lambda s, b: c.PS[:, 4 * s + b, :]
        banks = lambda s, b, n: c.PS[:, 4 * s + b:4 * s + b + n, :]
        EYE = c.ident
        SCALE = AHEAD ** -0.5
        LAG = 2

        with nc.Block() as block:
            lanes = lambda a: a.rearrange("p (h n) -> p h n", n=LANE)[:, :, 0:AHEAD]

            @block.sync
            def _(sp):
                sp.wait_ge(m.cleared, 1)
                for at, name in ((w_q, "Wq"), (w_k, "Wk")):
                    sp.dma_start(lanes(at[:, :]), ins[f"L1_ffn_{name}"].rearrange("p (h n) -> p h n", n=AHEAD)).then_inc(m.loaded, 16)
                sp.dma_start(w_v[:, :], ins["L1_ffn_Wv"]).then_inc(m.loaded, 16)
                sp.dma_start(lane_sums[:, :], ins["lane_sums"]).then_inc(m.loaded, 16)
                for j in range(4):
                    sp.dma_start(w_o[LANE * j:LANE * j + AHEAD, :, :],
                                 ins["L1_ffn_Wo"].rearrange("(g j f) d -> j f g d", g=GROUPS, f=AHEAD)[j]).then_inc(m.loaded, 16)
                for at, name in ((b_q, "bq"), (b_k, "bk")):
                    a = ins[f"L1_ffn_{name}"]
                    sp.dma_start(lanes(at[:, :]), bass.AP(a.tensor, a.offset, [[0, 1], [AHEAD, AHEADS], [1, AHEAD]])).then_inc(m.loaded, 16)
                sp.dma_start(b_v[:, :], ins["L1_ffn_bv"].rearrange("(o d) -> o d", o=1)).then_inc(m.loaded, 16)
                sp.dma_start(b_o[:, :], broadcast_rows(ins["L1_ffn_bo"], P)).then_inc(m.loaded, 16)
                sp.wait_ge(m.loaded, 12 * 16)

            @block.vector
            def _(dve):
                for a in (w_q, w_k, b_q, b_k):
                    nc.vector.memset(a[:, :], 0.0)
                nc.vector.memset(w_o[:, :, :], 0.0)
                dve.drain()
                nc.vector.memset(b_k[:, :].rearrange("p (h n) -> p h n", n=LANE)[:, :, AHEAD:AHEAD + 1], 1.0).then_inc(m.cleared, 1)
        with ExitStack() as inner:
            fold_norm(nc, c, inner, "attention",
                      [(w_q[:, :], None, None, b_q[:, :], 0), (w_k[:, :], None, None, b_k[:, :], 0), (w_v[:, :], None, None, b_v[:, :], 0)],
                      m.loaded, 12 * 16)

        block = ctx.enter_context(nc.Block())

        @block.sync
        def _(sp):
            prefetch(sp)

        lane = lambda j: slice(LANE * j, LANE * (j + 1))

        @block.tensor
        def _(pe):
            mm = nc.tensor.matmul

            def scores(i, s, g):
                for t in range(2):
                    for pair in range(2):
                        last = mm(bank(s, 2 * t + pair), q[s][:, g, bass.ts(t, P)], k[s][:, g, 2 * pair:2 * pair + 2, :].rearrange("p j n -> p (j n)"),
                                  start=True, stop=True)
                return last

            def first(i, s):
                yield 3
                pe.wait_ge(m.normed, both(i, s))
                for t in range(2):
                    last = nc.tensor.transpose(bank(s, 0)[:, bass.ts(t, P)], x3[s][:, t, :], EYE[:, :])
                last.then_inc(m.xT, 1)
                yield 4
                pe.wait_ge(m.xT_kept, both(i, s))
                for g in range(GROUPS):
                    mm(bank(s, 1)[:, g * 256:(g + 1) * 256], w_q[:, bass.ts(g, P)], xT[s][:, :], start=True, stop=True)
                    last = mm(bank(s, 2)[:, g * 256:(g + 1) * 256], w_k[:, bass.ts(g, P)], xT[s][:, :], start=True, stop=True)
                last.then_inc(m.qk_made, 1)
                for t in range(2):
                    last = mm(bank(s, 3)[:, bass.ts(t, P)], xT[s][:, bass.ts(t, P)], w_v[:, :], start=True, stop=True)
                last.then_inc(m.v_made, 1)
                yield 7
                pe.wait_ge(m.qk_kept, both(i, s))
                pe.wait_ge(m.k_kept, both(i, s))
                pe.wait_ge(m.v_kept, both(i, s))
                scores(i, s, 0).then_inc(m.scored0, 1)
                yield 13
                pe.wait_ge(m.top_kept0, both(i, s))
                scores(i, s, 1).then_inc(m.scored1, 1)
                yield 18.7
                pe.wait_ge(m.top_kept1, both(i, s))
                for g in range(GROUPS):
                    for t in range(2):
                        last = nc.tensor.transpose(bank(s, 0)[:, (2 * g + t) * P:(2 * g + t + 1) * P],
                                                   top[s][:, t, g, :, :].rearrange("p j n -> p (j n)"), EYE[:, :])
                last.then_inc(m.topT, 1)

            def second(i, s):
                def spread_sums(g):
                    return mm(bank(s, 3 - g)[:, 256:], lane_sums[:, :], raw[s][:, g * 256:(g + 1) * 256], start=True, stop=True)

                for h in range(AHEADS + LAG):
                    yield 0 + 1.92 * h
                    if h < AHEADS:
                        g, j = divmod(h, 4)
                        if h == 0:
                            pe.wait_ge(m.q_shifted, both(i, s))
                        if h >= 2:
                            pe.wait_ge(exps[h - 2], both(i, s))
                        for t in range(2):
                            last = mm(bank(s, h % 2)[:, t * 256:(t + 1) * 256], k[s][:, g, j, bass.ts(t, P)], q[s][:, g, :], start=True, stop=True)
                        last.then_inc(spread[h], 1)
                    if h >= LAG:
                        g, j = divmod(h - LAG, 4)
                        pe.wait_ge(exps[h - LAG], both(i, s))
                        for n in range(2):
                            last = mm(c.PS[lane(j), 4 * s + 3 - g, 0:256], v[s][:, n, h - LAG, :],
                                      probs[s][:, h - LAG, n, :], start=n == 0, stop=n == 1)
                        if h - LAG in (3, 7):
                            last.then_inc((m.summed0, m.summed1)[g], 1)
                    if h == 4 + LAG:
                        pe.wait_ge(m.raw_kept0, both(i, s))
                        spread_sums(0).then_inc(m.sums_spread0, 1)
                yield 19
                pe.wait_ge(m.raw_kept1, both(i, s))
                spread_sums(1).then_inc(m.sums_spread1, 1)
                yield 22
                pe.wait_ge(m.oT_kept, both(i, s))
                for t in range(2):
                    for g in range(GROUPS):
                        last = mm(bank(s, 1)[:, bass.ts(t, P)], oT[s][:, g, bass.ts(t, P)], w_o[:, g, :], start=g == 0, stop=g == GROUPS - 1)
                last.then_inc(m.projected, 1)

            skewed(pe, first, second)

        @block.scalar
        def _(act):
            a = nc.scalar.activation

            def first(i, s):
                yield 6.2
                act.wait_ge(m.normed, both(i, s))
                act.wait_ge(m.qk_made, both(i, s))
                for j in range(3):
                    last = a(k[s][lane(j), :, j, :], c.PS[lane(j), 4 * s + 2, :].rearrange("p (g n) -> p g n", g=2), ACT.Copy)
                last.then_inc(m.k_kept, 1)

            def second(i, s):
                for h in range(AHEADS):
                    yield 1.2 + 1.8 * h
                    act.wait_ge(spread[h], both(i, s))
                    a(probs[s][:, h, :, :], bank(s, h % 2).rearrange("p (t n) -> p t n", t=2), ACT.Exp, scale=SCALE).then_inc(exps[h], 1)
                    if h == 3 + LAG:
                        act.wait_ge(m.summed0, both(i, s))
                        a(raw[s][:, 0:256], bank(s, 3)[:, 0:256], ACT.Copy).then_inc(m.raw_kept0, 1)
                yield 18
                act.wait_ge(m.summed1, both(i, s))
                a(raw[s][:, 256:], bank(s, 2)[:, 0:256], ACT.Copy).then_inc(m.raw_kept1, 1)

            skewed(act, first, second)

        @block.gpsimd
        def _(pool):
            def rows_rstd(s):
                norm_rstd(nc, pool, c, norm[s])
                norm[s].last.then_inc(m.rstd, 1)

            def first(i, s):
                yield from ()

            def second(i, s):
                yield 1
                pool.wait_ge(m.normed, both(i, s))
                nc.gpsimd.tensor_tensor(xb[s][:, :, :], x3[s][:, :, :], b_o[:, :].unsqueeze(1).to_broadcast([P, 2, P]), ALU.add).then_inc(m.xb_ready, 1)
                yield 4
                pool.wait_ge(m.stats, both(i + 2, s))
                rows_rstd(s)

            for s in range(2):
                pool.wait_ge(m.stats, s + 1)
                rows_rstd(s)
            skewed(pool, first, second)

        @block.vector
        def _(dve):
            vv = nc.vector
            for s in range(2):
                vv.memset(v[s][:, :, :, AHEAD:], 1.0)
                vv.memset(top[s][:, :, :, :, :], 0.0)
                vv.memset(k[s][:, :, :, :], 0.0)
            dve.drain()
            row = lambda a, t: a[:, bass.ds(t, 1), :].rearrange("p o d -> p (o d)")

            def maxima(s, g):
                return vv.tensor_reduce(top[s][:, :, g, :, AHEAD], banks(s, 0, 4).rearrange("p (t c) (j n) -> p t (c j) n", t=2, j=2),
                                        AX, ALU.max, negate=True)

            def rows_stats(i, s):
                for t in range(2):
                    vv.bn_stats(norm[s].sums[:, t, :], row(c.H, (i + s) * 2 + t))
                dve.drain()
                for t in range(2):
                    last = vv.bn_aggr(norm[s].stat[:, t, :], norm[s].sums[:, t, :])
                return last

            def rows_normed(i, s):
                for t in range(2):
                    last = vv.tensor_scalar(x3[s][:, t, :], row(c.H, (i + s) * 2 + t), norm[s].stat[:, t, 0:1], norm[s].rstd[:, t:t + 1],
                                            ALU.subtract, ALU.mult)
                return last

            def first(i, s):
                yield 3.5
                dve.wait_ge(m.xT, both(i, s))
                vv.tensor_scalar(xT[s][:, :], bank(s, 0)[:, 0:256], 1.0, None, ALU.add).then_inc(m.xT_kept, 1)
                yield 6
                dve.wait_ge(m.qk_made, both(i, s))
                vv.tensor_copy(k[s][lane(3), :, 3, :], c.PS[lane(3), 4 * s + 2, :].rearrange("p (g n) -> p g n", g=2))
                vv.tensor_copy(q[s][:, :, :], bank(s, 1).rearrange("p (g n) -> p g n", g=2)).then_inc(m.qk_kept, 1)
                dve.wait_ge(m.v_made, both(i, s))
                vv.tensor_copy(v[s][:, :, :, 0:AHEAD].rearrange("p t h d -> p (t h) d"),
                               bank(s, 3)[:, 0:256].rearrange("p (g d) -> p g d", d=AHEAD)).then_inc(m.v_kept, 1)
                yield 10.5
                dve.wait_ge(m.scored0, both(i, s))
                maxima(s, 0).then_inc(m.top_kept0, 1)
                yield 17.17
                dve.wait_ge(m.scored1, both(i, s))
                maxima(s, 1).then_inc(m.top_kept1, 1)
                yield 19.2
                dve.wait_ge(m.topT, both(i, s))
                vv.tensor_tensor(q[s][:, :, :], bank(s, 0).rearrange("p (g n) -> p g n", g=2), q[s][:, :, :], ALU.add).then_inc(m.q_shifted, 1)

            def second(i, s):
                yield 3
                rows_stats(i + 2, s).then_inc(m.stats, 1)
                yield 8
                dve.wait_ge(m.rstd, both(i + 2, s))
                dve.wait_ge(m.xb_ready, both(i, s))
                rows_normed(i + 2, s).then_inc(m.normed, 1)
                yield 12.1
                dve.wait_ge(m.sums_spread0, both(i, s))
                vv.reciprocal(share[s][:, 0:256], bank(s, 3)[:, 256:])
                dve.drain()
                vv.tensor_tensor(oT[s][:, 0, :], raw[s][:, 0:256], share[s][:, 0:256], ALU.mult)
                yield 20
                dve.wait_ge(m.sums_spread1, both(i, s))
                vv.reciprocal(share[s][:, 256:], bank(s, 2)[:, 256:])
                dve.drain()
                vv.tensor_tensor(oT[s][:, 1, :], raw[s][:, 256:], share[s][:, 256:], ALU.mult).then_inc(m.oT_kept, 1)
                yield 23
                dve.wait_ge(m.projected, both(i, s))
                vv.tensor_tensor(c.X[:, bass.ds((i + s) * 2, 2), :], bank(s, 1)[:, 0:256].rearrange("p (t d) -> p t d", t=2), xb[s][:, :, :],
                                 ALU.add).then_inc(m.done, 1)

            for s in range(2):
                rows_stats(0, s).then_inc(m.stats, 1)
            for s in range(2):
                dve.wait_ge(m.rstd, s + 1)
                rows_normed(0, s).then_inc(m.normed, 1)
            skewed(dve, first, second)


def tower(nc, ins, out):
    c = Chip()
    gate0 = ("L0_ffn", "L0_ffn_Ws", "L0_ffn_bs")
    gate1 = ("L1_ffn", "L1_ffn_gate_W", "L1_ffn_gate_b")
    norm1 = ("L1_ffn_ln1_g", "L1_ffn_ln1_b")
    with ExitStack() as ctx:
        load_constants(nc, c, ins, ctx)
        with ExitStack() as mixture:
            expert_buffers(nc, c, mixture, 0)
            with ExitStack() as layers:
                w = [performer_weights(nc, c, layers, layer) for layer in range(2)]
                embed(nc, c, ins, w)
                prepare_performer(nc, c, w[0], 0)
                performer(nc, c, w[0], 0, lambda sp: load_performer(nc, sp, w[1], ins, 1))
                prepare_performer(nc, c, w[1], 1)
                performer(nc, c, w[1], 1, lambda sp: load_experts(nc, c, sp, ins, 0, *gate0))
            prepare_experts(nc, c, 0, "L0_ffn")
            gate(nc, c, "gate0", add=True)
            route(nc, c, "route0")
            experts(nc, c, "experts0", ACT.Gelu)
        mamba(nc, c, ins)
        with ExitStack() as mixture:
            expert_buffers(nc, c, mixture, 1)
            attention(nc, c, ins, lambda sp: load_experts(nc, c, sp, ins, 1, *gate1, norm=norm1))
            prepare_experts(nc, c, 1, "L1_ffn", norm1)
            gate(nc, c, "gate1", add=False)
            route(nc, c, "route1")
            experts(nc, c, "experts1", ACT.Gelu_apprx_tanh)
            combine(nc, c, "combine1", out)


def laid_out(inputs):
    import numpy as np

    z = {name: np.asarray(a) for name, a in inputs.items()}
    keep = [n for n in z if n.startswith(("L0_attn_", "L0_ffn_", "L1_ffn_")) and n != "L0_attn_proj"]
    a = {n: z[n] for n in keep}
    a["ids"] = z["x"].reshape(TILES, P).T
    a["cache"] = z["L0_tok_sin_cos_cache"][..., ::-1].reshape(-1, P)
    a["projT"] = z["L0_attn_proj"].transpose(0, 2, 1)
    f, b = ({n: z[f"L1_attn_{d}_{n}"] for n in ("in_w", "conv_w", "conv_b", "dt_bias", "A_log", "D", "gnorm_w", "out_w")} for d in "fb")
    fw, bw = f["in_w"], b["in_w"]
    x, bs, cs, dts = (slice(lo, hi) for lo, hi in ((256, 512), (512, 576), (576, 640), (640, 644)))
    a["m_w_in"] = np.concatenate([fw[x], bw[x], fw[bs], bw[bs], fw[cs], bw[cs], fw[0:256], bw[0:256], fw[dts], bw[dts]]).T

    def channels(n):
        g, h = f[n], b[n]
        joined = np.concatenate([g[0:256], h[0:256], g[256:320], h[256:320], g[320:384], h[320:384]])
        return np.moveaxis(joined.reshape((MIX, P) + joined.shape[1:]), 0, 1)

    a["m_taps"] = channels("conv_w")
    a["m_tap_rows"] = np.concatenate([f["conv_w"][0:256], b["conv_w"][0:256]]).T[::-1].reshape(-1)
    a["m_tap_bias"] = channels("conv_b")
    join = lambda n: np.concatenate([f[n], b[n]])
    a["m_columns"] = np.concatenate([z["L1_attn_norm_w"][None], np.repeat(join("D"), HEAD).reshape(4, P), join("gnorm_w").reshape(4, P)]).T
    a["m_dt_bias"] = join("dt_bias")
    a["m_A_log"] = join("A_log")
    a["m_out_w"] = np.concatenate([f["out_w"], b["out_w"]], 1)
    a["m_projT"] = np.concatenate([z["L1_attn_proj_w"][:, :P].T, z["L1_attn_proj_w"][:, P:].T], 1)
    r, t = np.arange(P)[:, None], np.arange(P)[None]
    a["lane_sums"] = ((r % LANE == AHEAD) & (r // LANE == t // LANE)).astype(np.float32)
    a["m_masks"] = np.stack([r < t, r > t, r <= t, r >= t], 1).astype(np.float32)
    a["before"] = (r < t).astype(np.float32)
    a["ident"] = (r == t).astype(np.float32)
    a["experts"] = np.broadcast_to(np.arange(EXPERTS, dtype=np.float32) - EXPERTS, (P, EXPERTS))
    a["tile_start"] = (np.arange(SORTED, dtype=np.float32) * P)[None]
    return {n: np.ascontiguousarray(v) for n, v in a.items()}


def kernel(**inputs):
    import concourse.bacc as bacc
    from concourse.bass_utils import run_bass_kernel_spmd

    nc = bacc.Bacc("TRN2", target_bir_lowering=False, num_devices=1)
    arrays = laid_out(inputs)
    ins = {n: nc.dram_tensor(f"in_{n}", v.shape, mybir.dt.from_np(v.dtype), kind="ExternalInput").ap() for n, v in arrays.items()}
    out = nc.dram_tensor("out_0", (SEQS, SEQ_TILES * P, P), F32, kind="ExternalOutput").ap()
    tower(nc, ins, out)
    done = run_bass_kernel_spmd(nc, [{f"in_{n}": v for n, v in arrays.items()}], core_ids=[0])
    return done.results[0]["out_0"]
```
